# Optimizing a Trainium2 kernel written in Bass

```python
import numpy as np
import jax
import jax.numpy as jnp

def _softmax(x, axis=-1):
    return jax.nn.softmax(x, axis=axis)

def _gelu(x):
    return jax.nn.gelu(x, approximate=True)

def _silu(x):
    return jax.nn.silu(x)

def _sigmoid(x):
    return jax.nn.sigmoid(x)

def _layernorm(x, axis=-1, eps=1e-05):
    m = jnp.mean(x, axis=axis, keepdims=True)
    v = jnp.var(x, axis=axis, keepdims=True)
    return (x - m) / jnp.sqrt(v + eps)

def _scatter_add(tgt, idx, src, axis=0):
    return tgt.at[idx].add(src)

def _segment_sum(src, seg, n):
    return jax.ops.segment_sum(src, seg, n)
kernel_name = 'mk_prb_d1_jaxref_r4_92fa31'

def setup_inputs(seed: int=0):
    np.random.seed(seed)
    _w = jnp.asarray

    def _L0_attn_setup():
        import jax, jax.numpy as jnp
        import numpy as np
        B, T, D, H = (2, 512, 512, 16)
        DK = D // H
        NEG = -1e+30
        key = jax.random.key(seed)
        kx, kq, kk, kv, ko = jax.random.split(key, 5)
        s = 0.02
        return {'x': jax.random.normal(kx, (B, T, D), jnp.float32), 'Wq': jax.random.normal(kq, (D, D), jnp.float32) * s, 'Wk': jax.random.normal(kk, (D, D), jnp.float32) * s, 'Wv': jax.random.normal(kv, (D, D), jnp.float32) * s, 'Wo': jax.random.normal(ko, (D, D), jnp.float32) * s}
    _L0_attn_in = _L0_attn_setup()

    def _L0_ffn_setup():
        import jax, jax.numpy as jnp
        import numpy as np
        H = 512
        I_MOE = 352
        E = 8
        TOP_K = 2
        NG = 4
        TOPK_G = 2
        SCALE = 2.5
        N_SHARED = 2
        I_SHARED = I_MOE * N_SHARED
        B, S = (1, 512)

        def _mlp(x, gw, uw, dw):
            return jax.nn.silu(x @ gw.T) * (x @ uw.T) @ dw.T

        def _route(x2d, rw, bias):
            T = x2d.shape[0]
            logits = x2d.astype(jnp.float32) @ rw.astype(jnp.float32).T
            scores = jax.nn.sigmoid(logits)
            sfc = scores + bias[None, :]
            grp = sfc.reshape(T, NG, E // NG)
            group_scores = jnp.sum(jax.lax.top_k(grp, 2)[0], axis=-1)
            grp_idx = jax.lax.top_k(group_scores, TOPK_G)[1]
            group_mask = jnp.zeros((T, NG), jnp.float32).at[jnp.arange(T)[:, None], grp_idx].set(1.0)
            score_mask = jnp.repeat(group_mask, E // NG, axis=1)
            masked = jnp.where(score_mask > 0, sfc, 0.0)
            topk_idx = jax.lax.top_k(masked, TOP_K)[1]
            topk_w = jnp.take_along_axis(scores, topk_idx, axis=1)
            topk_w = topk_w / (jnp.sum(topk_w, axis=-1, keepdims=True) + 1e-20)
            return (topk_idx, topk_w * SCALE)
        key = jax.random.key(seed)
        ks = jax.random.split(key, 9)
        sc = 0.02
        return {'x': jax.random.normal(ks[0], (B, S, H), dtype=jnp.float32), 'router_weight': jax.random.normal(ks[1], (E, H), dtype=jnp.float32) * sc, 'e_score_correction_bias': jnp.zeros((E,), dtype=jnp.float32), 'gate_w': jax.random.normal(ks[2], (E, I_MOE, H), dtype=jnp.float32) * sc, 'up_w': jax.random.normal(ks[3], (E, I_MOE, H), dtype=jnp.float32) * sc, 'down_w': jax.random.normal(ks[4], (E, H, I_MOE), dtype=jnp.float32) * sc, 'shared_gate_w': jax.random.normal(ks[5], (I_SHARED, H), dtype=jnp.float32) * sc, 'shared_up_w': jax.random.normal(ks[6], (I_SHARED, H), dtype=jnp.float32) * sc, 'shared_down_w': jax.random.normal(ks[7], (H, I_SHARED), dtype=jnp.float32) * sc}
    _L0_ffn_in = _L0_ffn_setup()
    _d = {'L0_attn_x': _L0_attn_in['x'], 'L0_attn_Wq': _L0_attn_in['Wq'], 'L0_attn_Wk': _L0_attn_in['Wk'], 'L0_attn_Wv': _L0_attn_in['Wv'], 'L0_attn_Wo': _L0_attn_in['Wo'], 'L0_ffn_router_weight': _L0_ffn_in['router_weight'], 'L0_ffn_e_score_correction_bias': _L0_ffn_in['e_score_correction_bias'], 'L0_ffn_gate_w': _L0_ffn_in['gate_w'], 'L0_ffn_up_w': _L0_ffn_in['up_w'], 'L0_ffn_down_w': _L0_ffn_in['down_w'], 'L0_ffn_shared_gate_w': _L0_ffn_in['shared_gate_w'], 'L0_ffn_shared_up_w': _L0_ffn_in['shared_up_w'], 'L0_ffn_shared_down_w': _L0_ffn_in['shared_down_w']}
    _x0 = _d['L0_attn_x']
    _d['L0_attn_x'] = jax.random.normal(jax.random.fold_in(jax.random.key(seed), 1), (2, 1024, 512), dtype=_x0.dtype)
    del _x0
    return _d

def reference(L0_attn_x, L0_attn_Wq, L0_attn_Wk, L0_attn_Wv, L0_attn_Wo, L0_ffn_router_weight, L0_ffn_e_score_correction_bias, L0_ffn_gate_w, L0_ffn_up_w, L0_ffn_down_w, L0_ffn_shared_gate_w, L0_ffn_shared_up_w, L0_ffn_shared_down_w):

    def _L0_attn_ref(x, Wq, Wk, Wv, Wo):
        import jax, jax.numpy as jnp
        import numpy as np
        B, T, D, H = (2, 512, 512, 16)
        DK = D // H
        NEG = -1e+30
        b, t, _ = x.shape
        scale = 1.0 / np.sqrt(DK).astype(np.float32)

        def split_heads(y):
            return y.reshape(b, t, H, DK).transpose(0, 2, 1, 3)
        Q = split_heads(x @ Wq.T)
        K = split_heads(x @ Wk.T)
        V = split_heads(x @ Wv.T)
        S = jnp.einsum('bhqd,bhkd->bhqk', Q, K) * scale
        causal = jnp.tril(jnp.ones((t, t), dtype=bool))
        S = jnp.where(causal, S, NEG)
        P = jax.nn.softmax(S, axis=-1)
        O = jnp.einsum('bhqk,bhkd->bhqd', P, V)
        out = O.transpose(0, 2, 1, 3).reshape(b, t, D) @ Wo.T
        return out

    def _L0_ffn_ref(x, router_weight, e_score_correction_bias, gate_w, up_w, down_w, shared_gate_w, shared_up_w, shared_down_w):
        import jax, jax.numpy as jnp
        import numpy as np
        H = 512
        I_MOE = 352
        E = 8
        TOP_K = 2
        NG = 4
        TOPK_G = 2
        SCALE = 2.5
        N_SHARED = 2
        I_SHARED = I_MOE * N_SHARED
        B, S = (1, 512)

        def _mlp(x, gw, uw, dw):
            return jax.nn.silu(x @ gw.T) * (x @ uw.T) @ dw.T

        def _route(x2d, rw, bias):
            T = x2d.shape[0]
            logits = x2d.astype(jnp.float32) @ rw.astype(jnp.float32).T
            scores = jax.nn.sigmoid(logits)
            sfc = scores + bias[None, :]
            grp = sfc.reshape(T, NG, E // NG)
            group_scores = jnp.sum(jax.lax.top_k(grp, 2)[0], axis=-1)
            grp_idx = jax.lax.top_k(group_scores, TOPK_G)[1]
            group_mask = jnp.zeros((T, NG), jnp.float32).at[jnp.arange(T)[:, None], grp_idx].set(1.0)
            score_mask = jnp.repeat(group_mask, E // NG, axis=1)
            masked = jnp.where(score_mask > 0, sfc, 0.0)
            topk_idx = jax.lax.top_k(masked, TOP_K)[1]
            topk_w = jnp.take_along_axis(scores, topk_idx, axis=1)
            topk_w = topk_w / (jnp.sum(topk_w, axis=-1, keepdims=True) + 1e-20)
            return (topk_idx, topk_w * SCALE)
        orig_shape = x.shape
        x2d = x.reshape(-1, H)
        T = x2d.shape[0]
        topk_idx, topk_w = _route(x2d, router_weight, e_score_correction_bias)
        cw = jnp.zeros((T, E), jnp.float32).at[jnp.arange(T)[:, None], topk_idx].add(topk_w)

        def expert_body(acc, ws):
            gw, uw, dw, cwe = ws
            y = _mlp(x2d, gw, uw, dw)
            return (acc + cwe[:, None] * y, None)
        routed, _ = jax.lax.scan(expert_body, jnp.zeros_like(x2d), (gate_w, up_w, down_w, cw.T))
        out = routed.reshape(orig_shape) + _mlp(x, shared_gate_w, shared_up_w, shared_down_w)
        return out
    x = L0_attn_x
    xn = _layernorm(x, axis=-1)
    x = x + _L0_attn_ref(xn, L0_attn_Wq, L0_attn_Wk, L0_attn_Wv, L0_attn_Wo) + _L0_ffn_ref(xn, L0_ffn_router_weight, L0_ffn_e_score_correction_bias, L0_ffn_gate_w, L0_ffn_up_w, L0_ffn_down_w, L0_ffn_shared_gate_w, L0_ffn_shared_up_w, L0_ffn_shared_down_w)
    return x

_drawn_inputs = setup_inputs


def setup_inputs(seed=0):
    import zlib

    import numpy as np

    out = dict(_drawn_inputs(seed))
    spreads = {'L0_ffn_e_score_correction_bias': (0.0, 0.28)}
    factors = {'L0_attn_Wq': 8.0, 'L0_attn_Wk': 8.0, 'L0_attn_Wv': 3.155, 'L0_attn_Wo': 3.184}
    for name, (base, spread) in spreads.items():
        noise = np.random.default_rng([zlib.crc32(name.encode()), seed]).standard_normal(out[name].shape)
        drawn = base * np.exp(spread * noise) if base else spread * noise
        out[name] = jnp.asarray(drawn.astype(out[name].dtype))
    for name, factor in factors.items():
        out[name] = (out[name] * factor).astype(out[name].dtype)
    return out
```

```python
import concourse.bass as bass
from concourse import mybir
from contextlib import ExitStack

F32 = mybir.dt.float32
F32R = mybir.dt.float32r
BF16 = mybir.dt.bfloat16
ALU = mybir.AluOpType
ACT = mybir.ActivationFunctionType
AX = mybir.AxisListType

B, S, D = 2, 1024, 512
T = B * S
H, DK = 16, 32
P = 128
NT = T // P
KC = D // P
TBW = 512
NTB = T // TBW
E, F = 8, 352
NSH = 2
NBLK = E + NSH
FCH = [(0, 128), (128, 128), (256, 96)]
EPS = 1e-5
ROUTE_SCALE = 2.5
SCALE = DK ** -0.5
MASKED = -1e30


def wait(eng, sem, value):
    if not (isinstance(value, int) and value <= 0):
        eng.wait_ge(sem, value)


def pipeline(eng, count, unroll, stages):
    deepest = max(lag for lag, _ in stages)
    first = max(1, -(-deepest // unroll))
    last = count // unroll

    def step(i, c):
        for lag, stage in stages:
            turn, at = divmod(c - lag, unroll)
            if isinstance(i, int):
                if 0 <= unroll * (i + turn) + at < count:
                    stage(i + turn, at)
            else:
                stage(i + turn, at)

    for i in range(min(first, last)):
        for c in range(unroll):
            step(i, c)
    if last > first:
        with eng.Fori(first, last) as i:
            for c in range(unroll):
                step(i, c)
    for c in range(deepest):
        step(last + c // unroll, c % unroll)


def moe_attention_kernel(nc, x, wqk, wv, wo, router, bias, gate, up, down, out):
    q_hi = nc.dram_tensor("qk_hi", [2 * D, T], F32, kind="Internal").ap()
    q_lo = nc.dram_tensor("qk_lo", [2 * D, T], F32, kind="Internal").ap()
    v_dram = nc.dram_tensor("v_heads", [H, P, NT, 2 * DK], F32, kind="Internal").ap()
    row_dram = nc.dram_tensor("max_rows", [2 * H, S], F32, kind="Internal").ap()
    with ExitStack() as ctx:
        xt_hi = ctx.enter_context(nc.sbuf_tensor("xt_hi", [P, KC, T], F32R))
        xt_lo = ctx.enter_context(nc.sbuf_tensor("xt_lo", [P, KC, T], F32R))
        ident = ctx.enter_context(nc.sbuf_tensor("ident", [P, P], F32))
        cw = ctx.enter_context(nc.sbuf_tensor("cw", [P, NT, NBLK], F32))
        norm_phase(nc, x, wv, xt_hi, xt_lo, ident, v_dram)
        project_phase(nc, wqk, router, bias, xt_hi, xt_lo, ident, cw, q_hi, q_lo)
        acc = ctx.enter_context(nc.sbuf_tensor("acc", [P, NT, D], F32))
        attend_phase(nc, ident, q_hi, q_lo, v_dram, row_dram, acc)
        out_phase(nc, x, wo, ident, acc)
        ffn_phase(nc, gate, up, down, xt_hi, xt_lo, cw, acc, out)


def allocator(nc, ctx):
    def sbuf(name, shape, dt=F32):
        return ctx.enter_context(nc.sbuf_tensor(name, shape, dt))

    def psum(name, shape):
        return ctx.enter_context(nc.psum_tensor(name, shape, F32))

    def sem(name):
        return ctx.enter_context(nc.semaphore(name))
    return sbuf, psum, sem


def norm_phase(nc, x, wv, xt_hi, xt_lo, ident, v_dram):
    with ExitStack() as ctx:
        sbuf, psum, sem = allocator(nc, ctx)
        U = 2
        x_tile = sbuf("x_tile", [P, U, D])
        stats = sbuf("stats", [P, U, 6])
        moments = sbuf("moments", [P, U, 2])
        var_eps = sbuf("var_eps", [P, U])
        std = sbuf("std", [P, U])
        rstd = sbuf("rstd", [P, U])
        xn = sbuf("xn", [P, U, D])
        tile_hi = sbuf("tile_hi", [P, U, KC, P], F32R)
        tile_lo = sbuf("tile_lo", [P, U, KC, P], F32R)
        wv_raw = sbuf("wv_raw", [P, KC, D])
        wv_hi = sbuf("wv_hi", [P, KC, D], F32R)
        wv_lo = sbuf("wv_lo", [P, KC, D], F32R)
        v_stage = sbuf("v_stage", [P, U, H, 2 * DK], F32R)
        ps_t = [psum(f"ps_t{n}", [P, KC, P]) for n in range(U)]
        ps_v = [psum(f"ps_v{n}", [P, D]) for n in range(U)]
        x_loaded = [sem(f"x_loaded{n}") for n in range(U)]
        xt_saved = [sem(f"xt_saved{n}") for n in range(U)]
        v_stored = [sem(f"v_stored{n}") for n in range(U)]
        wv_loaded = sem("wv_loaded")
        wv_hi_ready = sem("wv_hi_ready")
        wv_lo_ready = sem("wv_lo_ready")
        ident_zeroed = sem("ident_zeroed")
        ident_ready = sem("ident_ready")
        stats_ready = sem("stats_ready")
        moments_ready = sem("moments_ready")
        var_ready = sem("var_ready")
        std_ready = sem("std_ready")
        rstd_ready = sem("rstd_ready")
        xn_ready = sem("xn_ready")
        transposed = sem("transposed")
        hi_ready = sem("hi_ready")
        lo_ready = sem("lo_ready")
        v_done = sem("v_done")
        v_hi_ready = sem("v_hi_ready")
        v_lo_ready = sem("v_lo_ready")
        passed = sem("passed")

        with nc.Block() as block:
            @block.sync
            def _(sp):
                sp.dma_start(wv_raw[:, :, :], wv).then_inc(wv_loaded, 16)

                def load(i, c):
                    t = U * i + c
                    wait(sp, xn_ready, t - U + 1)
                    sp.dma_start(x_tile[:, c, :], x[bass.ds(t * P, P), :]).then_inc(x_loaded[c], 16)

                def save(i, c):
                    t = U * i + c
                    wait(sp, lo_ready, t + 1)
                    sp.dma_start(xt_hi[:, :, bass.ds(t * P, P)].bitcast(F32), tile_hi[:, c].bitcast(F32)).then_inc(xt_saved[c], 16)
                    sp.dma_start(xt_lo[:, :, bass.ds(t * P, P)].bitcast(F32), tile_lo[:, c].bitcast(F32)).then_inc(xt_saved[c], 16)

                def store_v(i, c):
                    t = U * i + c
                    wait(sp, v_lo_ready, t + 1)
                    sp.dma_start(v_dram[:, :, bass.ds(t, 1), :].rearrange("h p t d -> p h (t d)"),
                                 v_stage[:, c].bitcast(F32)).then_inc(v_stored[c], 16)

                pipeline(sp, NT, U, [(0, load), (2, save), (3, store_v)])
                for n in range(U):
                    sp.wait_ge(v_stored[n], 16 * (NT // U))
                    sp.wait_ge(xt_saved[n], 32 * (NT // U))

            @block.gpsimd
            def _(pool):
                nc.gpsimd.memset(ident[:, :], 0.0).then_inc(ident_zeroed, 1)
                pool.wait_ge(ident_zeroed, 1)
                nc.gpsimd.affine_select(out=ident[:, :], in_=ident[:, :], compare_op=ALU.not_equal,
                                        fill=1.0, base=0, pattern=[[-1, P]],
                                        channel_multiplier=1).then_inc(ident_ready, 1)

            @block.vector
            def _(dve):
                def normalize(i, c):
                    t = U * i + c
                    wait(dve, x_loaded[c], 16 * (i + 1))
                    nc.vector.bn_stats(stats[:, c, :], x_tile[:, c, :]).then_inc(stats_ready, 1)
                    wait(dve, stats_ready, t + 1)
                    dve.sem_inc(passed, 1)
                    nc.vector.bn_aggr(moments[:, c, :], stats[:, c, :]).then_inc(moments_ready, 1)
                    wait(dve, moments_ready, t + 1)
                    nc.vector.tensor_scalar(var_eps[:, c:c + 1], moments[:, c, 1:2], EPS, None,
                                            ALU.add).then_inc(var_ready, 1)

                def scale(i, c):
                    t = U * i + c
                    wait(dve, std_ready, t + 1)
                    nc.vector.reciprocal(rstd[:, c:c + 1], std[:, c:c + 1]).then_inc(rstd_ready, 1)
                    wait(dve, rstd_ready, t + 1)
                    wait(dve, transposed, t - U + 1)
                    nc.vector.tensor_scalar(xn[:, c, :], x_tile[:, c, :], moments[:, c, 0:1],
                                            rstd[:, c:c + 1], ALU.subtract,
                                            ALU.mult).then_inc(xn_ready, 1)

                def lo(i, c):
                    t = U * i + c
                    wait(dve, hi_ready, t + 1)
                    nc.vector.tensor_tensor(tile_lo[:, c], ps_t[c][:, :, :], tile_hi[:, c].bitcast(F32),
                                            ALU.subtract).then_inc(lo_ready, 1)

                def v_lo(i, c):
                    t = U * i + c
                    wait(dve, v_hi_ready, t + 1)
                    v = v_stage[:, c]
                    nc.vector.tensor_tensor(v[:, :, DK:], ps_v[c][:, :].rearrange("p (h d) -> p h d", h=H),
                                            v[:, :, 0:DK].bitcast(F32),
                                            ALU.subtract).then_inc(v_lo_ready, 1)

                dve.wait_ge(wv_hi_ready, 1)
                nc.vector.tensor_tensor(wv_lo[:, :, :], wv_raw[:, :, :], wv_hi[:, :, :].bitcast(F32),
                                        ALU.subtract).then_inc(wv_lo_ready, 1)
                pipeline(dve, NT, U, [(0, normalize), (0, scale), (1, lo), (2, v_lo)])

            @block.scalar
            def _(act):
                act.wait_ge(wv_loaded, 16)
                nc.scalar.activation(wv_hi[:, :, :], wv_raw[:, :, :], ACT.Copy).then_inc(wv_hi_ready, 1)

                def root(i, c):
                    t = U * i + c
                    wait(act, var_ready, t + 1)
                    nc.scalar.activation(std[:, c:c + 1], var_eps[:, c:c + 1],
                                         ACT.Sqrt).then_inc(std_ready, 1)

                def hi(i, c):
                    t = U * i + c
                    wait(act, transposed, t + 1)
                    wait(act, v_done, t - U + 1)
                    wait(act, xt_saved[c], 32 * i)
                    nc.scalar.activation(tile_hi[:, c], ps_t[c][:, :, :], ACT.Copy).then_inc(hi_ready, 1)

                def v_hi(i, c):
                    t = U * i + c
                    wait(act, v_done, t + 1)
                    wait(act, v_stored[c], 16 * i)
                    nc.scalar.activation(v_stage[:, c, :, 0:DK],
                                         ps_v[c][:, :].rearrange("p (h d) -> p h d", h=H),
                                         ACT.Copy).then_inc(v_hi_ready, 1)

                pipeline(act, NT, U, [(0, root), (1, hi), (2, v_hi)])

            @block.tensor
            def _(pe):
                pe.wait_ge(ident_ready, 1)

                def transpose(i, c):
                    t = U * i + c
                    wait(pe, xn_ready, t + 1)
                    wait(pe, lo_ready, t - U + 1)
                    for k in range(KC):
                        last = nc.tensor.transpose(ps_t[c][:, k, :], xn[:, c, k * P:(k + 1) * P],
                                                   ident[:, :])
                    last.then_inc(transposed, 1)

                def multiply(i, c):
                    t = U * i + c
                    wait(pe, lo_ready, t + 1)
                    wait(pe, v_lo_ready, t - U + 1)
                    n = 0
                    for k in range(KC):
                        for a, b in ((tile_hi, wv_hi), (tile_hi, wv_lo), (tile_lo, wv_hi)):
                            last = nc.tensor.matmul(ps_v[c][:, :], a[:, c, k, :], b[:, k, :],
                                                    start=(n == 0), stop=(n == 3 * KC - 1))
                            n += 1
                    last.then_inc(v_done, 1)

                def first_multiply(i, c):
                    if isinstance(i, int) and i == 0 and c == 0:
                        pe.wait_ge(wv_lo_ready, 1)
                    multiply(i, c)

                pipeline(pe, NT, U, [(0, transpose), (1, first_multiply)])


def project_phase(nc, wqk, router, bias, xt_hi, xt_lo, ident, cw, q_hi, q_lo):
    with ExitStack() as ctx:
        sbuf, psum, sem = allocator(nc, ctx)
        U = 2
        CH = 2 * D // P
        w_raw = sbuf("w_raw", [P, U, KC, P])
        w_hi = sbuf("w_hi", [P, U, KC, P], F32R)
        w_lo = sbuf("w_lo", [P, U, KC, P], F32R)
        stage_hi = sbuf("stage_hi", [P, U, T], F32R)
        stage_lo = sbuf("stage_lo", [P, U, T], F32R)
        r_raw = sbuf("r_raw", [P, KC, E])
        r_hi = sbuf("r_hi", [P, KC, E], F32R)
        r_lo = sbuf("r_lo", [P, KC, E], F32R)
        logits_t = sbuf("logits_t", [E, T])
        bias_b = sbuf("bias_b", [P, 1, E])
        score = sbuf("score", [P, NT, E])
        biased = sbuf("biased", [P, NT, E])
        G = E // 2
        group = sbuf("group", [P, NT, G])
        beats = sbuf("beats", [P, NT, E])
        rank = sbuf("rank", [P, NT, E])
        chosen = sbuf("chosen", [P, NT, E])
        total = sbuf("total", [P, NT])
        ps_q = [psum(f"ps_q{n}", [P, TBW]) for n in range(NTB)]
        ps_r = psum("ps_r", [P, TBW])
        ps_s = psum("ps_s", [P, NT, E])
        w_loaded = [sem(f"w_loaded{n}") for n in range(U)]
        stored = [sem(f"stored{n}") for n in range(U)]
        r_loaded = sem("r_loaded")
        bias_loaded = sem("bias_loaded")
        r_hi_ready = sem("r_hi_ready")
        r_lo_ready = sem("r_lo_ready")
        logits_done = sem("logits_done")
        logits_copied = sem("logits_copied")
        logits_turned = sem("logits_turned")
        score_ready = sem("score_ready")
        w_hi_ready = sem("w_hi_ready")
        w_lo_ready = sem("w_lo_ready")
        q_done = sem("q_done")
        q_hi_ready = sem("q_hi_ready")
        q_lo_ready = sem("q_lo_ready")
        routing = sem("routing")

        with nc.Block() as block:
            @block.sync
            def _(sp):
                sp.dma_start(r_raw[:, :, :], router).then_inc(r_loaded, 16)
                sp.dma_start(bias_b[:, 0, :], bias.rearrange("(a e) -> a e", a=1).broadcast_to([P, E])).then_inc(bias_loaded, 16)

                def load(i, c):
                    t = U * i + c
                    wait(sp, w_lo_ready, t - U + 1)
                    sp.dma_start(w_raw[:, c], wqk[bass.ds(t, 1)].rearrange("a p k m -> (a p) k m")
                                 ).then_inc(w_loaded[c], 16)

                def store(i, c):
                    t = U * i + c
                    wait(sp, q_lo_ready, NTB * (t + 1))
                    sp.dma_start(q_hi[bass.ds(t * P, P), :], stage_hi[:, c].bitcast(F32)).then_inc(stored[c], 16)
                    sp.dma_start(q_lo[bass.ds(t * P, P), :], stage_lo[:, c].bitcast(F32)).then_inc(stored[c], 16)

                pipeline(sp, CH, U, [(0, load), (2, store)])
                for n in range(U):
                    sp.wait_ge(stored[n], 32 * (CH // U))

            @block.scalar
            def _(act):
                act.wait_ge(r_loaded, 16)
                nc.scalar.activation(r_hi[:, :, :], r_raw[:, :, :], ACT.Copy).then_inc(r_hi_ready, 1)
                for n in range(NTB):
                    act.wait_ge(logits_done, n + 1)
                    nc.scalar.activation(logits_t[:, n * TBW:(n + 1) * TBW], ps_r[0:E, :],
                                         ACT.Copy).then_inc(logits_copied, 1)
                act.wait_ge(logits_turned, 1)
                nc.scalar.activation(score[:, :, :], ps_s[:, :, :], ACT.Sigmoid).then_inc(score_ready, 1)

                def split(i, c):
                    t = U * i + c
                    wait(act, w_loaded[c], 16 * (i + 1))
                    wait(act, q_done, NTB * (t - U + 1))
                    nc.scalar.activation(w_hi[:, c], w_raw[:, c], ACT.Copy).then_inc(w_hi_ready, 1)

                def evacuate(i, c):
                    t = U * i + c
                    wait(act, stored[c], 32 * i)
                    for n in range(NTB):
                        wait(act, q_done, NTB * t + n + 1)
                        nc.scalar.activation(stage_hi[:, c, n * TBW:(n + 1) * TBW], ps_q[n][:, :],
                                             ACT.Copy).then_inc(q_hi_ready, 1)

                pipeline(act, CH, U, [(0, split), (1, evacuate)])

            @block.tensor
            def _(pe):
                pe.wait_ge(r_lo_ready, 1)
                for n in range(NTB):
                    pe.wait_ge(logits_copied, n) if n else None
                    j = 0
                    for k in range(KC):
                        for a, b in ((r_hi, xt_hi), (r_lo, xt_hi), (r_hi, xt_lo)):
                            last = nc.tensor.matmul(ps_r[0:E, :], a[:, k, :],
                                                    b[:, k, n * TBW:(n + 1) * TBW],
                                                    start=(j == 0), stop=(j == 3 * KC - 1))
                            j += 1
                    last.then_inc(logits_done, 1)
                pe.wait_ge(logits_copied, NTB)
                for t in range(NT):
                    last = nc.tensor.transpose(ps_s[:, t, :], logits_t[:, t * P:(t + 1) * P],
                                               ident[0:E, 0:E])
                last.then_inc(logits_turned, 1)

                def multiply(i, c):
                    t = U * i + c
                    wait(pe, w_lo_ready, t + 1)
                    for n in range(NTB):
                        wait(pe, q_lo_ready, NTB * (t - 1) + n + 1)
                        j = 0
                        for k in range(KC):
                            for a, b in ((w_hi, xt_hi), (w_lo, xt_hi), (w_hi, xt_lo)):
                                last = nc.tensor.matmul(ps_q[n][:, :], a[:, c, k, :],
                                                        b[:, k, n * TBW:(n + 1) * TBW],
                                                        start=(j == 0), stop=(j == 3 * KC - 1))
                                j += 1
                        last.then_inc(q_done, 1)

                pipeline(pe, CH, U, [(0, multiply)])

            @block.vector
            def _(dve):
                dve.wait_ge(r_hi_ready, 1)
                nc.vector.tensor_tensor(r_lo[:, :, :], r_raw[:, :, :], r_hi[:, :, :].bitcast(F32),
                                        ALU.subtract).then_inc(r_lo_ready, 1)

                def split(i, c):
                    t = U * i + c
                    wait(dve, w_hi_ready, t + 1)
                    nc.vector.tensor_tensor(w_lo[:, c], w_raw[:, c], w_hi[:, c].bitcast(F32),
                                            ALU.subtract).then_inc(w_lo_ready, 1)

                def evacuate(i, c):
                    t = U * i + c
                    for n in range(NTB):
                        cols = slice(n * TBW, (n + 1) * TBW)
                        wait(dve, q_hi_ready, NTB * t + n + 1)
                        nc.vector.tensor_tensor(stage_lo[:, c, cols], ps_q[n][:, :],
                                                stage_hi[:, c, cols].bitcast(F32),
                                                ALU.subtract).then_inc(q_lo_ready, 1)

                pipeline(dve, CH, U, [(0, split), (1, evacuate)])

                steps = [0]

                def then(instruction):
                    steps[0] += 1
                    instruction.then_inc(routing, 1)
                    dve.wait_ge(routing, steps[0])

                def each(ap, n):
                    return ap.broadcast_to([P, NT, n])

                def top2(value, n, flag):
                    for e in range(n):
                        other = value[:, :, e:e + 1]
                        if e:
                            then(nc.vector.tensor_tensor(beats[:, :, 0:e], each(other, e),
                                                         value[:, :, 0:e], ALU.is_gt))
                        if e < n - 1:
                            then(nc.vector.tensor_tensor(beats[:, :, e + 1:n], each(other, n - e - 1),
                                                         value[:, :, e + 1:n], ALU.is_ge))
                        then(nc.vector.memset(beats[:, :, e:e + 1], 0.0))
                        if e:
                            then(nc.vector.tensor_tensor(rank[:, :, 0:n], rank[:, :, 0:n],
                                                         beats[:, :, 0:n], ALU.add))
                        else:
                            then(nc.vector.tensor_copy(rank[:, :, 0:n], beats[:, :, 0:n]))
                    then(nc.vector.tensor_scalar(flag, rank[:, :, 0:n], 2.0, None, ALU.is_lt))

                dve.wait_ge(score_ready, 1)
                dve.wait_ge(bias_loaded, 16)
                then(nc.vector.tensor_tensor(biased[:, :, :], score[:, :, :],
                                             bias_b[:, :, :].broadcast_to([P, NT, E]), ALU.add))
                pairs = biased[:, :, :].rearrange("p t (g j) -> p t g j", j=2)
                then(nc.vector.tensor_tensor(group[:, :, :], pairs[:, :, :, 0], pairs[:, :, :, 1],
                                             ALU.add))
                top2(group, G, group[:, :, :])
                for j in range(2):
                    then(nc.vector.tensor_tensor(pairs[:, :, :, j], pairs[:, :, :, j],
                                                 group[:, :, :], ALU.mult))
                top2(biased, E, chosen[:, :, :])
                then(nc.vector.tensor_tensor(chosen[:, :, :], chosen[:, :, :], score[:, :, :],
                                             ALU.mult))
                then(nc.vector.reduce_sum(total[:, :], chosen[:, :, :], AX.X))
                then(nc.vector.tensor_scalar(total[:, :], total[:, :], 1e-20, None, ALU.add))
                then(nc.vector.reciprocal(total[:, :], total[:, :]))
                then(nc.vector.tensor_scalar(total[:, :], total[:, :], ROUTE_SCALE, None, ALU.mult))
                then(nc.vector.tensor_tensor(cw[:, :, 0:E], chosen[:, :, :],
                                             total[:, :].rearrange("p (t a) -> p t a", a=1)
                                             .broadcast_to([P, NT, E]), ALU.mult))
                then(nc.vector.memset(cw[:, :, E:], 1.0))


def attend_phase(nc, ident, q_hi, q_lo, v_dram, row_dram, attended):
    HS = 4
    NB = 12
    U = HS * NB
    STEPS = B * H * NB
    QT = S // P
    ROWS = 3 * DK
    VW = 2 * DK + 2
    BLOCKS = [(0, kt) for kt in range(4)] + [(1, kt) for kt in range(8)]
    PIECES = [(t, 0, P * (t + 1)) for t in range(4)]
    for t in range(4, QT):
        PIECES += [(t, 0, TBW), (t, TBW, P * (t + 1) - TBW)]
    AHEAD = 2 * NB
    ON_POOL = (2, 6, 10)
    DIAGONAL = [n for n, (qb, kt) in enumerate(BLOCKS) if kt >= 4 * qb]

    def span(n):
        qb, kt = BLOCKS[n]
        first = max(0, (kt - 4 * qb) * P)
        return first, TBW - first

    def count(of, i, c):
        return len(of) * (HS * i + c // NB) + sum(n <= c % NB for n in of)

    with ExitStack() as ctx:
        sbuf, psum, sem = allocator(nc, ctx)
        qs = sbuf("qs", [P, HS, S], F32R)
        ks = sbuf("ks", [P, HS, S], F32R)
        vs = sbuf("vs", [P, HS, QT, VW], F32R)
        late = sbuf("late", [P, P], BF16)
        eye = sbuf("eye", [P, P], BF16)
        maxima = sbuf("maxima", [P, HS, QT + 4])
        row_stage = sbuf("row_stage", [QT, HS, P], F32R)
        NP = 4
        prob = sbuf("prob", [P, NP, TBW])
        prob_hi = sbuf("prob_hi", [P, NP, TBW], F32R)
        prob_lo = sbuf("prob_lo", [P, NP, TBW], F32R)
        o_copy = sbuf("o_copy", [VW, 2, TBW])
        o_part = sbuf("o_part", [P, 4, DK])
        o_sum = sbuf("o_sum", [P, 4, DK])
        o_inv = sbuf("o_inv", [P, 4, 1])
        ps_m = [psum(f"ps_m{n}", [P, TBW]) for n in range(2)]
        ps_s = [psum(f"ps_s{n}", [P, TBW]) for n in range(2)]
        ps_o = [psum(f"ps_o{n}", [P, TBW]) for n in range(2)]
        ps_ot = psum("ps_ot", [P, 4, P])
        ps_row = psum("ps_row", [P, P])
        head_loaded = [sem(f"head_loaded{n}") for n in range(HS)]
        row_saved = [sem(f"row_saved{n}") for n in range(HS)]
        row_loaded = [sem(f"row_loaded{n}") for n in range(HS)]
        consts_ready = sem("consts_ready")
        consts_zeroed = sem("consts_zeroed")
        m_done = sem("m_done")
        m_read = sem("m_read")
        max_ready = sem("max_ready")
        row_turned = sem("row_turned")
        row_ready = sem("row_ready")
        s_done = sem("s_done")
        exp_done = sem("exp_done")
        hi_ready = sem("hi_ready")
        lo_dve = sem("lo_dve")
        lo_pool = sem("lo_pool")
        pv_done = sem("pv_done")
        o_copied = sem("o_copied")
        o_turned = sem("o_turned")
        part_ready = sem("part_ready")
        sum_ready = sem("sum_ready")
        inv_ready = sem("inv_ready")
        o_ready = sem("o_ready")
        POOL_BLOCKS = list(ON_POOL)
        DVE_BLOCKS = [n for n in range(NB) if n not in ON_POOL]

        with nc.Block() as block:
            @block.sync
            def _(sp):
                def load_head(i, c):
                    h, b = 2 * i + c // 2, c % 2
                    wait(sp, pv_done, NB * (HS * (i - 1) + c + 1))
                    sp_cols = slice(b * S, (b + 1) * S)
                    for n, (q_src, k_src) in enumerate(((q_hi, q_hi), (q_hi, q_lo), (q_lo, q_hi))):
                        rows = slice(n * DK, (n + 1) * DK)
                        sp.dma_start(qs[rows, c, :].bitcast(F32), q_src[bass.ds(h * DK, DK), sp_cols]
                                     ).then_inc(head_loaded[c], 16)
                        sp.dma_start(ks[rows, c, :].bitcast(F32), k_src[bass.ds(D + h * DK, DK), sp_cols]
                                     ).then_inc(head_loaded[c], 16)
                    sp.dma_start(vs[:, c, :, 0:2 * DK].bitcast(F32),
                                 v_dram[bass.ds(h, 1), :, b * QT:(b + 1) * QT, :]
                                 .rearrange("h p t d -> (h p) t d")).then_inc(head_loaded[c], 16)

                def save_row(i, c):
                    g = HS * i + c
                    wait(sp, row_ready, g + 1)
                    sp.dma_start(row_dram[bass.ds(g, 1), :].rearrange("a (t q) -> (a t) q", t=QT),
                                 row_stage[:, c, :].bitcast(F32)).then_inc(row_saved[c], 16)
                    wait(sp, row_saved[c], 16 * (i + 1))
                    sp.dma_start(qs[ROWS:ROWS + 1, c, :].bitcast(F32), row_dram[bass.ds(g, 1), :]
                                 ).then_inc(row_loaded[c], 16)

                pipeline(sp, B * H, HS, [(0, load_head), (2, save_row)])

            @block.gpsimd
            def _(pool):
                nc.gpsimd.memset(late[:, :], 0.0).then_inc(consts_zeroed, 1)
                nc.gpsimd.memset(eye[:, :], 0.0).then_inc(consts_zeroed, 1)
                pool.wait_ge(consts_zeroed, 2)
                nc.gpsimd.affine_select(out=late[:, :], in_=late[:, :], compare_op=ALU.is_ge,
                                        fill=MASKED, base=0, pattern=[[1, P]],
                                        channel_multiplier=-1).then_inc(consts_ready, 1)
                nc.gpsimd.affine_select(out=eye[:, :], in_=eye[:, :], compare_op=ALU.not_equal,
                                        fill=1.0, base=0, pattern=[[-1, P]],
                                        channel_multiplier=1).then_inc(consts_ready, 1)
                pool.wait_ge(consts_ready, 2)
                nc.gpsimd.memset(ks[ROWS:ROWS + 1, :, :].bitcast(F32), 1.0).then_inc(consts_ready, 1)
                pool.wait_ge(consts_ready, 3)
                nc.gpsimd.memset(vs[:, :, :, 2 * DK:].bitcast(F32), 1.0).then_inc(consts_ready, 1)

                def lo(i, c):
                    n = c % NB
                    if n not in ON_POOL:
                        return
                    first, w = span(n)
                    wait(pool, hi_ready, U * i + c + 1)
                    nc.gpsimd.tensor_tensor(prob_lo[:, c % NP, 0:w], prob[:, c % NP, 0:w],
                                            prob_hi[:, c % NP, 0:w].bitcast(F32),
                                            ALU.subtract).then_inc(lo_pool, 1)

                pipeline(pool, STEPS, U, [(0, lo)])

            @block.scalar
            def _(act):
                def row(i, c):
                    if c % NB != 0:
                        return
                    g = HS * i + c // NB
                    wait(act, row_turned, g + 1)
                    wait(act, row_saved[c // NB], 16 * i)
                    nc.scalar.activation(row_stage[:, c // NB, :], ps_row[0:QT, :], ACT.Copy,
                                         scale=-1.0).then_inc(row_ready, 1)

                def exp(i, c):
                    step = U * i + c
                    first, w = span(c % NB)
                    wait(act, s_done, step + 1)
                    wait(act, lo_dve, count(DVE_BLOCKS, i, c - NP))
                    wait(act, lo_pool, count(POOL_BLOCKS, i, c - NP))
                    nc.scalar.activation(prob[:, c % NP, 0:w], ps_s[c % 2][:, 0:w], ACT.Exp,
                                         scale=SCALE).then_inc(exp_done, 1)

                def hi(i, c):
                    step = U * i + c
                    first, w = span(c % NB)
                    wait(act, exp_done, step + 1)
                    wait(act, pv_done, step - NP + 1)
                    nc.scalar.activation(prob_hi[:, c % NP, 0:w], prob[:, c % NP, 0:w],
                                         ACT.Copy).then_inc(hi_ready, 1)

                def copy_o(i, c):
                    n = c % NB
                    if n not in (3, NB - 1):
                        return
                    half = int(n == NB - 1)
                    o = 2 * (HS * i + c // NB) + half
                    wait(act, pv_done, U * i + c + 1)
                    wait(act, o_turned, o - 1)
                    nc.scalar.activation(o_copy[:, half, :], ps_o[half][0:VW, :],
                                         ACT.Copy).then_inc(o_copied, 1)

                pipeline(act, STEPS, U, [(AHEAD, exp), (AHEAD + 1, hi), (AHEAD + 4, copy_o),
                                                 (NB + 1, row)])

            @block.vector
            def _(dve):
                def maximum(i, c):
                    g = HS * i + c // NB
                    slot = c // NB
                    t, k0, w = PIECES[c % NB]
                    step = U * i + c
                    wait(dve, m_done, step + 1)
                    if c % NB == 0:
                        wait(dve, row_turned, HS * (i - 1) + slot + 1)
                    scores = ps_m[c % 2][:, 0:w]
                    at = t if k0 + w == P * (t + 1) else QT + t - 4
                    nc.vector.reduce_max(maxima[:, slot, at:at + 1], scores, AX.X).then_inc(m_read, 1)
                    if c % NB == NB - 1:
                        wait(dve, m_read, step + 1)
                        nc.vector.tensor_tensor(maxima[:, slot, 4:QT], maxima[:, slot, 4:QT],
                                                maxima[:, slot, QT:QT + 4],
                                                ALU.max).then_inc(max_ready, 1)

                def lo(i, c):
                    n = c % NB
                    if n in ON_POOL:
                        return
                    first, w = span(n)
                    wait(dve, hi_ready, U * i + c + 1)
                    nc.vector.tensor_tensor(prob_lo[:, c % NP, 0:w], prob[:, c % NP, 0:w],
                                            prob_hi[:, c % NP, 0:w].bitcast(F32),
                                            ALU.subtract).then_inc(lo_dve, 1)

                def normalize(i, c):
                    n = c % NB
                    if n not in (3, NB - 1):
                        return
                    half = int(n == NB - 1)
                    h, b = 2 * i + c // NB // 2, c // NB % 2
                    o = 2 * (HS * i + c // NB) + half
                    wait(dve, o_turned, o + 1)
                    wait(dve, o_ready, o)
                    nc.vector.reciprocal(o_inv[:, :, :], ps_ot[:, :, 2 * DK:2 * DK + 1]).then_inc(inv_ready, 1)
                    nc.vector.tensor_copy(o_part[:, :, :], ps_ot[:, :, DK:2 * DK]).then_inc(part_ready, 1)
                    wait(dve, part_ready, o + 1)
                    nc.vector.tensor_tensor(o_sum[:, :, :], ps_ot[:, :, 0:DK], o_part[:, :, :],
                                            ALU.add).then_inc(sum_ready, 1)
                    wait(dve, inv_ready, o + 1)
                    wait(dve, sum_ready, o + 1)
                    tiles = slice(b * QT + 4 * half, b * QT + 4 * half + 4)
                    nc.vector.tensor_tensor(attended[:, tiles, bass.ds(h * DK, DK)], o_sum[:, :, :],
                                            o_inv[:, :, :].broadcast_to([P, 4, DK]),
                                            ALU.mult).then_inc(o_ready, 1)

                pipeline(dve, STEPS, U, [(0, maximum),
                                                 (AHEAD + 1, lo), (AHEAD + 7, normalize)])

            @block.tensor
            def _(pe):
                pe.wait_ge(consts_ready, 4)

                def maximum(i, c):
                    slot = c // NB
                    t, k0, w = PIECES[c % NB]
                    if c % NB == 0:
                        wait(pe, head_loaded[slot], 112 * (i + 1))
                    wait(pe, m_read, U * i + c - 1)
                    diagonal = k0 + w == P * (t + 1)
                    last = nc.tensor.matmul(ps_m[c % 2][:, 0:w], qs[0:ROWS, slot, t * P:(t + 1) * P],
                                            ks[0:ROWS, slot, k0:k0 + w], start=True,
                                            stop=not diagonal)
                    if diagonal:
                        last = nc.tensor.matmul(ps_m[c % 2][:, w - P:w], late[:, :], eye[:, :],
                                                start=False, stop=True)
                    last.then_inc(m_done, 1)

                def turn_row(i, c):
                    if c % NB != 0:
                        return
                    slot = c // NB
                    g = HS * i + slot
                    wait(pe, max_ready, g + 1)
                    wait(pe, row_ready, g)
                    nc.tensor.transpose(ps_row[0:QT, :], maxima[:, slot, 0:QT],
                                        ident[:, :]).then_inc(row_turned, 1)

                def score(i, c):
                    slot = c // NB
                    qb, kt = BLOCKS[c % NB]
                    first, w = span(c % NB)
                    if c % NB == 0:
                        wait(pe, row_loaded[slot], 16 * (i + 1))
                    wait(pe, exp_done, U * i + c - 1)
                    q0 = qb * TBW + first
                    diagonal = c % NB in DIAGONAL
                    last = nc.tensor.matmul(ps_s[c % 2][:, 0:w],
                                            ks[0:ROWS + 1, slot, kt * P:(kt + 1) * P],
                                            qs[0:ROWS + 1, slot, q0:q0 + w], start=True,
                                            stop=not diagonal)
                    if diagonal:
                        last = nc.tensor.matmul(ps_s[c % 2][:, 0:P], eye[:, :], late[:, :],
                                                start=False, stop=True)
                    last.then_inc(s_done, 1)

                def value(i, c):
                    slot = c // NB
                    n = c % NB
                    qb, kt = BLOCKS[n]
                    first, w = span(n)
                    if kt == 0:
                        wait(pe, o_copied, 2 * (HS * i + slot) + qb - 1)
                    if n in ON_POOL:
                        wait(pe, lo_pool, count(POOL_BLOCKS, i, c))
                    else:
                        wait(pe, lo_dve, count(DVE_BLOCKS, i, c))
                    into = ps_o[qb][0:VW, first:first + w]
                    nc.tensor.matmul(into, vs[:, slot, kt, :], prob_hi[:, c % NP, 0:w],
                                     start=(kt == 0), stop=False)
                    nc.tensor.matmul(into, vs[:, slot, kt, :], prob_lo[:, c % NP, 0:w], start=False,
                                     stop=(kt == 4 * qb + 3)).then_inc(pv_done, 1)

                def turn_o(i, c):
                    n = c % NB
                    if n not in (3, NB - 1):
                        return
                    half = int(n == NB - 1)
                    o = 2 * (HS * i + c // NB) + half
                    wait(pe, o_copied, o + 1)
                    wait(pe, o_ready, o)
                    for q in range(4):
                        last = nc.tensor.transpose(ps_ot[:, q, 0:VW], o_copy[:, half, q * P:(q + 1) * P],
                                                   ident[0:VW, 0:VW])
                    last.then_inc(o_turned, 1)

                pipeline(pe, STEPS, U, [(0, maximum),
                                                (AHEAD, score), (AHEAD + 3, value), (AHEAD + 6, turn_o),
                                                (NB + 1, turn_row)])


def out_phase(nc, x, wo, ident, acc):
    with ExitStack() as ctx:
        sbuf, psum, sem = allocator(nc, ctx)
        U = 2
        wo_raw = sbuf("wo_raw", [P, KC, D])
        wo_hi = sbuf("wo_hi", [P, KC, D], F32R)
        wo_lo = sbuf("wo_lo", [P, KC, D], F32R)
        x_tile = sbuf("x_res", [P, U, D])
        a_tile = sbuf("a_tile", [P, U, D])
        a_hi = sbuf("a_hi", [P, U, KC, P], F32R)
        a_lo = sbuf("a_lo", [P, U, KC, P], F32R)
        ps_t = [psum(f"ps_at{n}", [P, KC, P]) for n in range(U)]
        ps_y = [psum(f"ps_ay{n}", [P, D]) for n in range(U)]
        x_loaded = [sem(f"xr_loaded{n}") for n in range(U)]
        wo_loaded = sem("wo_loaded")
        wo_hi_ready = sem("wo_hi_ready")
        wo_lo_ready = sem("wo_lo_ready")
        tile_ready = sem("a_tile_ready")
        turned = sem("a_turned")
        hi_ready = sem("a_hi_ready")
        lo_ready = sem("a_lo_ready")
        y_done = sem("a_y_done")
        added = sem("a_added")

        with nc.Block() as block:
            @block.sync
            def _(sp):
                sp.dma_start(wo_raw[:, :, :], wo).then_inc(wo_loaded, 16)

                def load(i, c):
                    t = U * i + c
                    wait(sp, added, t - U + 1)
                    sp.dma_start(x_tile[:, c, :], x[bass.ds(t * P, P), :]).then_inc(x_loaded[c], 16)
                pipeline(sp, NT, U, [(0, load)])

            @block.scalar
            def _(act):
                act.wait_ge(wo_loaded, 16)
                nc.scalar.activation(wo_hi[:, :, :], wo_raw[:, :, :], ACT.Copy).then_inc(wo_hi_ready, 1)

                def hi(i, c):
                    t = U * i + c
                    wait(act, turned, t + 1)
                    wait(act, y_done, t - U + 1)
                    nc.scalar.activation(a_hi[:, c], ps_t[c][:, :, :], ACT.Copy).then_inc(hi_ready, 1)
                pipeline(act, NT, U, [(0, hi)])

            @block.vector
            def _(dve):
                def copy(i, c):
                    t = U * i + c
                    wait(dve, turned, t - U + 1)
                    nc.vector.tensor_copy(a_tile[:, c, :], acc[:, bass.ds(t, 1), :]
                                          .rearrange("p a d -> p (a d)")).then_inc(tile_ready, 1)

                def lo(i, c):
                    t = U * i + c
                    wait(dve, hi_ready, t + 1)
                    nc.vector.tensor_tensor(a_lo[:, c], ps_t[c][:, :, :], a_hi[:, c].bitcast(F32),
                                            ALU.subtract).then_inc(lo_ready, 1)

                def add(i, c):
                    t = U * i + c
                    wait(dve, y_done, t + 1)
                    wait(dve, x_loaded[c], 16 * (i + 1))
                    nc.vector.tensor_tensor(acc[:, bass.ds(t, 1), :].rearrange("p a d -> p (a d)"),
                                            ps_y[c][:, :], x_tile[:, c, :], ALU.add).then_inc(added, 1)
                dve.wait_ge(wo_hi_ready, 1)
                nc.vector.tensor_tensor(wo_lo[:, :, :], wo_raw[:, :, :], wo_hi[:, :, :].bitcast(F32),
                                        ALU.subtract).then_inc(wo_lo_ready, 1)
                pipeline(dve, NT, U, [(0, copy), (1, lo), (2, add)])

            @block.tensor
            def _(pe):
                def turn(i, c):
                    t = U * i + c
                    wait(pe, tile_ready, t + 1)
                    wait(pe, lo_ready, t - U + 1)
                    for k in range(KC):
                        last = nc.tensor.transpose(ps_t[c][:, k, :], a_tile[:, c, k * P:(k + 1) * P],
                                                   ident[:, :])
                    last.then_inc(turned, 1)

                def multiply(i, c):
                    t = U * i + c
                    wait(pe, lo_ready, t + 1)
                    wait(pe, added, t - U + 1)
                    n = 0
                    for k in range(KC):
                        for a, b in ((a_hi, wo_hi), (a_hi, wo_lo), (a_lo, wo_hi)):
                            last = nc.tensor.matmul(ps_y[c][:, :], a[:, c, k, :], b[:, k, :],
                                                    start=(n == 0), stop=(n == 3 * KC - 1))
                            n += 1
                    last.then_inc(y_done, 1)
                pe.wait_ge(wo_lo_ready, 1)
                pipeline(pe, NT, U, [(0, turn), (1, multiply)])


def ffn_phase(nc, gate, up, down, xt_hi, xt_lo, cw, acc, out):
    with ExitStack() as ctx:
        sbuf, psum, sem = allocator(nc, ctx)
        U = 2
        NF = len(FCH)
        g_raw = sbuf("g_raw", [P, KC, F])
        u_raw = sbuf("u_raw", [P, KC, F])
        d_raw = sbuf("d_raw", [P, NF, D])
        g_hi = sbuf("g_hi", [P, U, KC, F], F32R)
        g_lo = sbuf("g_lo", [P, U, KC, F], F32R)
        u_hi = sbuf("u_hi", [P, U, KC, F], F32R)
        u_lo = sbuf("u_lo", [P, U, KC, F], F32R)
        d_hi = sbuf("d_hi", [P, U, NF, D], F32R)
        d_lo = sbuf("d_lo", [P, U, NF, D], F32R)
        silu = sbuf("silu", [P, 2, TBW])
        hid = sbuf("hid", [P, 1, TBW])
        hid_hi = sbuf("hid_hi", [P, NF, TBW], F32R)
        hid_lo = sbuf("hid_lo", [P, NF, TBW], F32R)
        ps_g = [psum(f"ps_g{n}", [P, TBW]) for n in range(2)]
        ps_u = [psum(f"ps_u{n}", [P, TBW]) for n in range(2)]
        ps_y = [psum(f"ps_y{n}", [P, D]) for n in range(4)]
        loaded = sem("ffn_loaded")
        w_hi_ready = sem("ffn_w_hi")
        w_lo_ready = sem("ffn_w_lo")
        g_done = sem("g_done")
        u_done = sem("u_done")
        silu_ready = sem("silu_ready")
        hid_ready = sem("hid_ready")
        hid_hi_ready = sem("hid_hi_ready")
        hid_lo_ready = sem("hid_lo_ready")
        y_done = sem("y_done")
        added = sem("added")
        stored = sem("out_stored")
        WEIGHTS = ((g_raw, g_hi, g_lo), (u_raw, u_hi, u_lo), (d_raw, d_hi, d_lo))
        TAIL = FCH[-1][1]

        with nc.Block() as block:
            @block.sync
            def _(sp):
                def load(i, c):
                    e = U * i + c
                    wait(sp, w_lo_ready, 4 * e)
                    for raw, src in ((g_raw, gate), (u_raw, up)):
                        sp.dma_start(raw[:, :, :], src[bass.ds(e, 1)].rearrange("a p k f -> (a p) k f")
                                     ).then_inc(loaded, 16)
                    rows = down[bass.ds(e, 1)].rearrange("a f d -> (a f) d")
                    sp.dma_start(d_raw[:, 0:2, :], rows[0:2 * P, :].rearrange("(k p) d -> p k d", p=P)
                                 ).then_inc(loaded, 16)
                    sp.dma_start(d_raw[0:TAIL, 2, :], rows[2 * P:F, :]).then_inc(loaded, 16)
                pipeline(sp, NBLK, U, [(0, load)])
                sp.wait_ge(added, NBLK * NT)
                for t in range(NT):
                    sp.dma_start(out[t * P:(t + 1) * P, :], acc[:, t, :]).then_inc(stored, 16)
                sp.wait_ge(stored, 16 * NT)

            def weight_parts(c):
                for raw, hi, lo in WEIGHTS[:2]:
                    yield raw[:, :, :], hi[:, c], lo[:, c]
                yield d_raw[:, 0:2, :], d_hi[:, c, 0:2], d_lo[:, c, 0:2]
                yield d_raw[0:TAIL, 2, :], d_hi[0:TAIL, c, 2], d_lo[0:TAIL, c, 2]

            @block.scalar
            def _(act):
                def split(i, c):
                    e = U * i + c
                    wait(act, loaded, 64 * (e + 1))
                    wait(act, y_done, NT * (e - U + 1))
                    for raw, hi, lo in weight_parts(c):
                        nc.scalar.activation(hi, raw, ACT.Copy).then_inc(w_hi_ready, 1)

                def chunks(i, c, tb):
                    e = U * i + c
                    for k, (f0, w) in enumerate(FCH):
                        n = NF * (NTB * e + tb) + k
                        wait(act, g_done, n + 1)
                        wait(act, hid_ready, n - 1)
                        s = (NF * tb + k) % 2
                        nc.scalar.activation(silu[0:w, s, :], ps_g[s][0:w, :], ACT.Silu).then_inc(silu_ready, 1)
                        wait(act, hid_ready, n + 1)
                        wait(act, y_done, 4 * (NTB * e + tb))
                        nc.scalar.activation(hid_hi[0:w, k, :], hid[0:w, 0, :], ACT.Copy).then_inc(hid_hi_ready, 1)

                def block_e(i, c):
                    for tb in range(NTB):
                        chunks(i, c, tb)
                pipeline(act, NBLK, U, [(0, split), (1, block_e)])

            @block.vector
            def _(dve):
                def split(i, c):
                    e = U * i + c
                    for n, (raw, hi, lo) in enumerate(weight_parts(c)):
                        wait(dve, w_hi_ready, 4 * e + n + 1)
                        nc.vector.tensor_tensor(lo, raw, hi.bitcast(F32), ALU.subtract).then_inc(w_lo_ready, 1)

                def add(e, i, c, tb):
                    for q in range(4):
                        t = 4 * tb + q
                        wait(dve, y_done, NT * e + t + 1)
                        nc.vector.scalar_tensor_tensor(out=acc[:, t, :], in0=ps_y[q][:, :],
                                                       scalar=cw[:, t, bass.ds(e, 1)],
                                                       in1=acc[:, t, :], op0=ALU.mult,
                                                       op1=ALU.add).then_inc(added, 1)

                def block_e(i, c):
                    e = U * i + c
                    for tb in range(NTB):
                        for k, (f0, w) in enumerate(FCH):
                            n = NF * (NTB * e + tb) + k
                            s = (NF * tb + k) % 2
                            wait(dve, silu_ready, n + 1)
                            wait(dve, u_done, n + 1)
                            wait(dve, hid_lo_ready, n)
                            nc.vector.tensor_tensor(hid[0:w, 0, :], ps_u[s][0:w, :], silu[0:w, s, :],
                                                    ALU.mult).then_inc(hid_ready, 1)
                            wait(dve, hid_hi_ready, n + 1)
                            nc.vector.tensor_tensor(hid_lo[0:w, k, :], hid[0:w, 0, :],
                                                    hid_hi[0:w, k, :].bitcast(F32),
                                                    ALU.subtract).then_inc(hid_lo_ready, 1)
                        add(e, i, c, tb)
                pipeline(dve, NBLK, U, [(0, split), (1, block_e)])

            @block.tensor
            def _(pe):
                def block_e(i, c):
                    e = U * i + c
                    wait(pe, w_lo_ready, 4 * (e + 1))
                    for tb in range(NTB):
                        toks = slice(tb * TBW, (tb + 1) * TBW)
                        for k, (f0, w) in enumerate(FCH):
                            n = NF * (NTB * e + tb) + k
                            s = (NF * tb + k) % 2
                            for ps, hi, lo, done, read in ((ps_g, g_hi, g_lo, g_done, silu_ready),
                                                           (ps_u, u_hi, u_lo, u_done, hid_ready)):
                                wait(pe, read, n - 1)
                                j = 0
                                for kc in range(KC):
                                    for a, b in ((hi, xt_hi), (lo, xt_hi), (hi, xt_lo)):
                                        last = nc.tensor.matmul(ps[s][0:w, :], a[:, c, kc, f0:f0 + w],
                                                                b[:, kc, toks], start=(j == 0),
                                                                stop=(j == 3 * KC - 1))
                                        j += 1
                                last.then_inc(done, 1)
                        wait(pe, hid_lo_ready, NF * (NTB * e + tb + 1))
                        for q in range(4):
                            t = 4 * tb + q
                            wait(pe, added, NT * e + t - 3)
                            j = 0
                            for k, (f0, w) in enumerate(FCH):
                                for a, b in ((hid_hi, d_hi), (hid_hi, d_lo), (hid_lo, d_hi)):
                                    last = nc.tensor.matmul(ps_y[q][:, :], a[0:w, k, q * P:(q + 1) * P],
                                                            b[0:w, c, k, :], start=(j == 0),
                                                            stop=(j == 3 * NF - 1))
                                    j += 1
                            last.then_inc(y_done, 1)
                pipeline(pe, NBLK, U, [(0, block_e)])


def kernel(L0_attn_x, L0_attn_Wq, L0_attn_Wk, L0_attn_Wv, L0_attn_Wo, L0_ffn_router_weight,
           L0_ffn_e_score_correction_bias, L0_ffn_gate_w, L0_ffn_up_w, L0_ffn_down_w,
           L0_ffn_shared_gate_w, L0_ffn_shared_up_w, L0_ffn_shared_down_w):
    import numpy as np
    import concourse.bacc as bacc
    from concourse.bass_utils import run_bass_kernel_spmd

    def by_partition(w):
        return w.reshape(KC, P, -1).transpose(1, 0, 2)

    def columns(w):
        return w.reshape(KC, P, D // P, P).transpose(2, 1, 0, 3)

    def expert_in(w, shared):
        w = np.concatenate([w, shared.reshape(NSH, F, D)])
        return w.reshape(NBLK, F, KC, P).transpose(0, 3, 2, 1)

    a = {k: np.asarray(v) for k, v in dict(
        x=L0_attn_x, wq=L0_attn_Wq, wk=L0_attn_Wk, wv=L0_attn_Wv, wo=L0_attn_Wo,
        r=L0_ffn_router_weight, b=L0_ffn_e_score_correction_bias, g=L0_ffn_gate_w, u=L0_ffn_up_w,
        d=L0_ffn_down_w, sg=L0_ffn_shared_gate_w, su=L0_ffn_shared_up_w,
        sd=L0_ffn_shared_down_w).items()}
    arrays = {
        "x": a["x"].reshape(T, D),
        "wqk": np.concatenate([columns(a["wq"].T), columns(a["wk"].T)]),
        "wv": by_partition(a["wv"].T),
        "wo": by_partition(a["wo"].T),
        "router": by_partition(a["r"].T),
        "bias": a["b"],
        "gate": expert_in(a["g"], a["sg"]),
        "up": expert_in(a["u"], a["su"]),
        "down": np.concatenate([a["d"].transpose(0, 2, 1), a["sd"].T.reshape(NSH, F, D)]),
    }
    arrays = {k: np.ascontiguousarray(v) for k, v in arrays.items()}
    nc = bacc.Bacc("TRN2", target_bir_lowering=False, num_devices=1)
    ins = [nc.dram_tensor(f"in_{k}", v.shape, mybir.dt.from_np(v.dtype), kind="ExternalInput").ap()
           for k, v in arrays.items()]
    out = nc.dram_tensor("out", [T, D], F32, kind="ExternalOutput").ap()
    moe_attention_kernel(nc, *ins, out)
    r = run_bass_kernel_spmd(nc, [{f"in_{k}": v for k, v in arrays.items()}], core_ids=[0])
    return r.results[0]["out"].reshape(B, S, D)
```

```python
import concourse.bass as bass
from concourse import mybir
from contextlib import ExitStack

F32 = mybir.dt.float32
F32R = mybir.dt.float32r
BF16 = mybir.dt.bfloat16
I32 = mybir.dt.int32
ALU = mybir.AluOpType
ACT = mybir.ActivationFunctionType
AX = mybir.AxisListType

B, S, D = 2, 1024, 512
T = B * S
H, DK = 16, 32
P = 128
NT = T // P
KC = D // P
TBW = 512
NTB = T // TBW
E, F = 8, 352
NSH = 2
NST = (2 * T + E * (P - 1)) // P
NSLOT = NST * P
FCH = [(0, 128), (128, 128), (256, 96)]
EPS = 1e-5
ROUTE_SCALE = 2.5
SCALE = DK ** -0.5
MASKED = -1e30


def wait(eng, sem, value):
    if not (isinstance(value, int) and value <= 0):
        eng.wait_ge(sem, value)


def pipeline(eng, count, unroll, stages, back=0):
    deepest = max(lag for lag, _ in stages)
    first = max(1, -(-(deepest + back) // unroll))
    last = count // unroll

    def step(i, c):
        for lag, stage in stages:
            turn, at = divmod(c - lag, unroll)
            if isinstance(i, int):
                if 0 <= unroll * (i + turn) + at < count:
                    stage(i + turn, at)
            else:
                stage(i + turn, at)

    for i in range(min(first, last)):
        for c in range(unroll):
            step(i, c)
    if last > first:
        with eng.Fori(first, last) as i:
            for c in range(unroll):
                step(i, c)
    for c in range(count - unroll * last + deepest):
        step(last + c // unroll, c % unroll)


def moe_attention_kernel(nc, x, wqk, wv, wo, router, bias, gate, up, down, sgate, sup, sdown, out):
    qk_hi = nc.dram_tensor("qk_hi", [2 * D, T], F32, kind="Internal").ap()
    qk_lo = nc.dram_tensor("qk_lo", [2 * D, T], F32, kind="Internal").ap()
    v_dram = nc.dram_tensor("v_heads", [H, P, NT, 2 * DK], F32, kind="Internal").ap()
    row_dram = nc.dram_tensor("max_rows", [2 * H, S], F32, kind="Internal").ap()
    xn_dram = nc.dram_tensor("xn_rows", [T + P, D], F32, kind="Internal").ap()
    slots_dram = nc.dram_tensor("slots", [NSLOT, 2], F32, kind="Internal").ap()
    with ExitStack() as ctx:
        ident = ctx.enter_context(nc.sbuf_tensor("ident", [P, P], F32))
        slot_of = ctx.enter_context(nc.sbuf_tensor("slot_of", [P, NT, 2], I32))
        entry = ctx.enter_context(nc.sbuf_tensor("entry", [P, NT, 2, 2], F32))
        slot_table = ctx.enter_context(nc.sbuf_tensor("slot_table", [P, NST, 2], F32))
        expert_of = ctx.enter_context(nc.sbuf_tensor("expert_of", [P, NST], I32))
        with nc.sbuf_tensor("xt_hi", [P, KC, T], F32R) as xt_hi, \
                nc.sbuf_tensor("xt_lo", [P, KC, T], F32R) as xt_lo:
            norm_phase(nc, x, wv, xt_hi, xt_lo, ident, v_dram, xn_dram, out)
            project_phase(nc, wqk, router, bias, xt_hi, xt_lo, ident, slot_of, entry, slot_table,
                          expert_of, qk_hi, qk_lo)
            shared_phase(nc, x, sgate, sup, sdown, xt_hi, xt_lo, slot_of, entry, slot_table,
                         slots_dram, out)
        g_sb = ctx.enter_context(nc.sbuf_tensor("g_sb", [P, E * KC, F], F32))
        u_sb = ctx.enter_context(nc.sbuf_tensor("u_sb", [P, E * KC, F], F32))
        with nc.sbuf_tensor("attended", [P, NT, D], F32) as attended:
            attend_phase(nc, ident, qk_hi, qk_lo, v_dram, row_dram, gate, up, g_sb, u_sb, attended)
            with nc.sbuf_tensor("d_sb", [P, E * len(FCH), D], F32) as d_sb:
                out_phase(nc, wo, down, ident, attended, d_sb, out)
                routed_phase(nc, ident, g_sb, u_sb, d_sb, slot_table, expert_of, xn_dram, attended,
                             out)


def allocator(nc, ctx):
    def sbuf(name, shape, dt=F32):
        return ctx.enter_context(nc.sbuf_tensor(name, shape, dt))

    def psum(name, shape):
        return ctx.enter_context(nc.psum_tensor(name, shape, F32))

    def sem(name):
        return ctx.enter_context(nc.semaphore(name))
    return sbuf, psum, sem


def norm_phase(nc, x, wv, xt_hi, xt_lo, ident, v_dram, xn_dram, out):
    with ExitStack() as ctx:
        sbuf, psum, sem = allocator(nc, ctx)
        U = 2
        x_tile = sbuf("x_tile", [P, U, D])
        stats = sbuf("stats", [P, U, 6])
        moments = sbuf("moments", [P, U, 2])
        var_eps = sbuf("var_eps", [P, U])
        std = sbuf("std", [P, U])
        rstd = sbuf("rstd", [P, U])
        xn = sbuf("xn", [P, U, D])
        zeros = sbuf("zeros", [P, D])
        tile_hi = sbuf("tile_hi", [P, U, KC, P], F32R)
        tile_lo = sbuf("tile_lo", [P, U, KC, P], F32R)
        wv_raw = sbuf("wv_raw", [P, KC, D])
        wv_hi = sbuf("wv_hi", [P, KC, D], F32R)
        wv_lo = sbuf("wv_lo", [P, KC, D], F32R)
        v_stage = sbuf("v_stage", [P, U, H, 2 * DK], F32R)
        ps_t = [psum(f"ps_t{n}", [P, KC, P]) for n in range(U)]
        ps_v = [psum(f"ps_v{n}", [P, D]) for n in range(U)]
        x_loaded = [sem(f"x_loaded{n}") for n in range(U)]
        xt_saved = [sem(f"xt_saved{n}") for n in range(U)]
        v_stored = [sem(f"v_stored{n}") for n in range(U)]
        wv_loaded = sem("wv_loaded")
        wv_hi_ready = sem("wv_hi_ready")
        wv_lo_ready = sem("wv_lo_ready")
        ident_zeroed = sem("ident_zeroed")
        ident_ready = sem("ident_ready")
        stats_ready = sem("stats_ready")
        moments_ready = sem("moments_ready")
        var_ready = sem("var_ready")
        std_ready = sem("std_ready")
        rstd_ready = sem("rstd_ready")
        xn_ready = sem("xn_ready")
        transposed = sem("transposed")
        hi_ready = sem("hi_ready")
        lo_ready = sem("lo_ready")
        v_done = sem("v_done")
        v_hi_ready = sem("v_hi_ready")
        v_lo_ready = sem("v_lo_ready")
        passed = sem("passed")
        xn_stored = [sem(f"xn_stored{n}") for n in range(U)]
        zeros_ready = sem("zeros_ready")
        zeros_stored = sem("zeros_stored")

        with nc.Block() as block:
            @block.sync
            def _(sp):
                sp.dma_start(wv_raw[:, :, :], wv).then_inc(wv_loaded, 16)

                def load(i, c):
                    t = U * i + c
                    wait(sp, xn_ready, t - U + 1)
                    sp.dma_start(x_tile[:, c, :], x[bass.ds(t * P, P), :]).then_inc(x_loaded[c], 16)

                def save(i, c):
                    t = U * i + c
                    wait(sp, lo_ready, t + 1)
                    sp.dma_start(xt_hi[:, :, bass.ds(t * P, P)].bitcast(F32), tile_hi[:, c].bitcast(F32)).then_inc(xt_saved[c], 16)
                    sp.dma_start(xt_lo[:, :, bass.ds(t * P, P)].bitcast(F32), tile_lo[:, c].bitcast(F32)).then_inc(xt_saved[c], 16)

                def store_xn(i, c):
                    t = U * i + c
                    wait(sp, xn_ready, t + 1)
                    sp.dma_start(xn_dram[bass.ds(t * P, P), :], xn[:, c, :]).then_inc(xn_stored[c], 16)

                def store_v(i, c):
                    t = U * i + c
                    wait(sp, v_lo_ready, t + 1)
                    sp.dma_start(v_dram[:, :, bass.ds(t, 1), :].rearrange("h p t d -> p h (t d)"),
                                 v_stage[:, c].bitcast(F32)).then_inc(v_stored[c], 16)

                sp.wait_ge(zeros_ready, 1)
                sp.dma_start(xn_dram[T:, :], zeros[:, :]).then_inc(zeros_stored, 16)
                sp.dma_start(out[T:, :], zeros[:, :]).then_inc(zeros_stored, 16)
                pipeline(sp, NT, U, [(0, load), (1, store_xn), (2, save), (3, store_v)])
                sp.wait_ge(zeros_stored, 32)
                for n in range(U):
                    sp.wait_ge(xn_stored[n], 16 * (NT // U))
                    sp.wait_ge(v_stored[n], 16 * (NT // U))
                    sp.wait_ge(xt_saved[n], 32 * (NT // U))

            @block.gpsimd
            def _(pool):
                nc.gpsimd.memset(ident[:, :], 0.0).then_inc(ident_zeroed, 1)
                pool.wait_ge(ident_zeroed, 1)
                nc.gpsimd.affine_select(out=ident[:, :], in_=ident[:, :], compare_op=ALU.not_equal,
                                        fill=1.0, base=0, pattern=[[-1, P]],
                                        channel_multiplier=1).then_inc(ident_ready, 1)

            @block.vector
            def _(dve):
                def normalize(i, c):
                    t = U * i + c
                    wait(dve, x_loaded[c], 16 * (i + 1))
                    nc.vector.bn_stats(stats[:, c, :], x_tile[:, c, :]).then_inc(stats_ready, 1)
                    wait(dve, stats_ready, t + 1)
                    dve.sem_inc(passed, 1)
                    nc.vector.bn_aggr(moments[:, c, :], stats[:, c, :]).then_inc(moments_ready, 1)
                    wait(dve, moments_ready, t + 1)
                    nc.vector.tensor_scalar(var_eps[:, c:c + 1], moments[:, c, 1:2], EPS, None,
                                            ALU.add).then_inc(var_ready, 1)

                def scale(i, c):
                    t = U * i + c
                    wait(dve, std_ready, t + 1)
                    nc.vector.reciprocal(rstd[:, c:c + 1], std[:, c:c + 1]).then_inc(rstd_ready, 1)
                    wait(dve, rstd_ready, t + 1)
                    wait(dve, transposed, t - U + 1)
                    wait(dve, xn_stored[c], 16 * i)
                    nc.vector.tensor_scalar(xn[:, c, :], x_tile[:, c, :], moments[:, c, 0:1],
                                            rstd[:, c:c + 1], ALU.subtract,
                                            ALU.mult).then_inc(xn_ready, 1)

                def lo(i, c):
                    t = U * i + c
                    wait(dve, hi_ready, t + 1)
                    nc.vector.tensor_tensor(tile_lo[:, c], ps_t[c][:, :, :], tile_hi[:, c].bitcast(F32),
                                            ALU.subtract).then_inc(lo_ready, 1)

                def v_lo(i, c):
                    t = U * i + c
                    wait(dve, v_hi_ready, t + 1)
                    v = v_stage[:, c]
                    nc.vector.tensor_tensor(v[:, :, DK:], ps_v[c][:, :].rearrange("p (h d) -> p h d", h=H),
                                            v[:, :, 0:DK].bitcast(F32),
                                            ALU.subtract).then_inc(v_lo_ready, 1)

                nc.vector.memset(zeros[:, :], 0.0).then_inc(zeros_ready, 1)
                dve.wait_ge(wv_hi_ready, 1)
                nc.vector.tensor_tensor(wv_lo[:, :, :], wv_raw[:, :, :], wv_hi[:, :, :].bitcast(F32),
                                        ALU.subtract).then_inc(wv_lo_ready, 1)
                pipeline(dve, NT, U, [(0, normalize), (0, scale), (1, lo), (2, v_lo)])

            @block.scalar
            def _(act):
                act.wait_ge(wv_loaded, 16)
                nc.scalar.activation(wv_hi[:, :, :], wv_raw[:, :, :], ACT.Copy).then_inc(wv_hi_ready, 1)

                def root(i, c):
                    t = U * i + c
                    wait(act, var_ready, t + 1)
                    nc.scalar.activation(std[:, c:c + 1], var_eps[:, c:c + 1],
                                         ACT.Sqrt).then_inc(std_ready, 1)

                def hi(i, c):
                    t = U * i + c
                    wait(act, transposed, t + 1)
                    wait(act, v_done, t - U + 1)
                    wait(act, xt_saved[c], 32 * i)
                    nc.scalar.activation(tile_hi[:, c], ps_t[c][:, :, :], ACT.Copy).then_inc(hi_ready, 1)

                def v_hi(i, c):
                    t = U * i + c
                    wait(act, v_done, t + 1)
                    wait(act, v_stored[c], 16 * i)
                    nc.scalar.activation(v_stage[:, c, :, 0:DK],
                                         ps_v[c][:, :].rearrange("p (h d) -> p h d", h=H),
                                         ACT.Copy).then_inc(v_hi_ready, 1)

                pipeline(act, NT, U, [(0, root), (1, hi), (2, v_hi)])

            @block.tensor
            def _(pe):
                pe.wait_ge(ident_ready, 1)

                def transpose(i, c):
                    t = U * i + c
                    wait(pe, xn_ready, t + 1)
                    wait(pe, lo_ready, t - U + 1)
                    for k in range(KC):
                        last = nc.tensor.transpose(ps_t[c][:, k, :], xn[:, c, k * P:(k + 1) * P],
                                                   ident[:, :])
                    last.then_inc(transposed, 1)

                def multiply(i, c):
                    t = U * i + c
                    wait(pe, lo_ready, t + 1)
                    wait(pe, v_lo_ready, t - U + 1)
                    n = 0
                    for k in range(KC):
                        for a, b in ((tile_hi, wv_hi), (tile_hi, wv_lo), (tile_lo, wv_hi)):
                            last = nc.tensor.matmul(ps_v[c][:, :], a[:, c, k, :], b[:, k, :],
                                                    start=(n == 0), stop=(n == 3 * KC - 1))
                            n += 1
                    last.then_inc(v_done, 1)

                def first_multiply(i, c):
                    if isinstance(i, int) and i == 0 and c == 0:
                        pe.wait_ge(wv_lo_ready, 1)
                    multiply(i, c)

                pipeline(pe, NT, U, [(0, transpose), (1, first_multiply)])


def project_phase(nc, wqk, router, bias, xt_hi, xt_lo, ident, slot_of, entry, slot_table,
                  expert_of, qk_hi, qk_lo):
    with ExitStack() as ctx:
        sbuf, psum, sem = allocator(nc, ctx)
        U = 2
        CH = 2 * D // P
        w_raw = sbuf("w_raw", [P, U, KC, P])
        w_hi = sbuf("w_hi", [P, U, KC, P], F32R)
        w_lo = sbuf("w_lo", [P, U, KC, P], F32R)
        stage_hi = sbuf("stage_hi", [P, U, T], F32R)
        stage_lo = sbuf("stage_lo", [P, U, T], F32R)
        r_raw = sbuf("r_raw", [P, KC, E])
        r_hi = sbuf("r_hi", [P, KC, E], F32R)
        r_lo = sbuf("r_lo", [P, KC, E], F32R)
        logits_t = sbuf("logits_t", [E, T])
        bias_b = sbuf("bias_b", [P, 1, E])
        score = sbuf("score", [P, NT, E])
        biased = sbuf("biased", [P, NT, E])
        G = E // 2
        group = sbuf("group", [P, NT, G])
        beats = sbuf("beats", [P, NT, E])
        rank = sbuf("rank", [P, NT, E])
        chosen = sbuf("chosen", [P, NT, E])
        total = sbuf("total", [P, NT])
        weight = sbuf("weight", [P, NT, E])
        earlier = sbuf("earlier", [P, P])
        ones = sbuf("ones", [P, P])
        tile_no = sbuf("tile_no", [P, NST, 1])
        pads = sbuf("pads", [P, 1], I32)
        tokens = sbuf("tokens", [P, NT], I32)
        tile_int = sbuf("tile_int", [P, NST], I32)
        n_tiles = sbuf("n_tiles", [P, 1, E])
        first_tile = sbuf("first_tile", [P, 1, E])
        over = sbuf("over", [P, E, NT])
        started = sbuf("started", [P, NST, E])
        expert_f = sbuf("expert_f", [P, NST])
        slot = sbuf("slot", [P, NT, E])
        slot_a = sbuf("slot_a", [P, NT])
        slot_b = sbuf("slot_b", [P, NT])
        ps_q = [psum(f"ps_q{n}", [P, TBW]) for n in range(NTB)]
        ps_r = psum("ps_r", [P, TBW])
        ps_s = psum("ps_s", [P, NT, E])
        ps_rank = psum("ps_rank", [P, NT, E])
        ps_count = psum("ps_count", [P, 1, E])
        w_loaded = [sem(f"w_loaded{n}") for n in range(U)]
        stored = [sem(f"stored{n}") for n in range(U)]
        r_loaded = sem("r_loaded")
        bias_loaded = sem("bias_loaded")
        r_hi_ready = sem("r_hi_ready")
        r_lo_ready = sem("r_lo_ready")
        logits_done = sem("logits_done")
        logits_copied = sem("logits_copied")
        logits_turned = sem("logits_turned")
        score_ready = sem("score_ready")
        w_hi_ready = sem("w_hi_ready")
        w_lo_ready = sem("w_lo_ready")
        q_done = sem("q_done")
        q_hi_ready = sem("q_hi_ready")
        q_lo_ready = sem("q_lo_ready")
        routing = sem("routing")
        consts_zeroed = sem("r_consts_zeroed")
        consts_ready = sem("r_consts_ready")
        chosen_ready = sem("chosen_ready")
        ranks_done = sem("ranks_done")

        with nc.Block() as block:
            @block.sync
            def _(sp):
                sp.dma_start(r_raw[:, :, :], router).then_inc(r_loaded, 16)
                sp.dma_start(bias_b[:, 0, :], bias.rearrange("(a e) -> a e", a=1).broadcast_to([P, E])).then_inc(bias_loaded, 16)

                def load(i, c):
                    t = U * i + c
                    wait(sp, w_lo_ready, t - U + 1)
                    sp.dma_start(w_raw[:, c], wqk[bass.ds(t, 1)].rearrange("a p k m -> (a p) k m")
                                 ).then_inc(w_loaded[c], 16)

                def store(i, c):
                    t = U * i + c
                    wait(sp, q_lo_ready, NTB * (t + 1))
                    sp.dma_start(qk_hi[bass.ds(t * P, P), :], stage_hi[:, c].bitcast(F32)).then_inc(stored[c], 16)
                    sp.dma_start(qk_lo[bass.ds(t * P, P), :], stage_lo[:, c].bitcast(F32)).then_inc(stored[c], 16)

                pipeline(sp, CH, U, [(0, load), (2, store)])
                for n in range(U):
                    sp.wait_ge(stored[n], 32 * (CH // U))

            @block.scalar
            def _(act):
                act.wait_ge(r_loaded, 16)
                nc.scalar.activation(r_hi[:, :, :], r_raw[:, :, :], ACT.Copy).then_inc(r_hi_ready, 1)
                for n in range(NTB):
                    act.wait_ge(logits_done, n + 1)
                    nc.scalar.activation(logits_t[:, n * TBW:(n + 1) * TBW], ps_r[0:E, :],
                                         ACT.Copy).then_inc(logits_copied, 1)
                act.wait_ge(logits_turned, 1)
                nc.scalar.activation(score[:, :, :], ps_s[:, :, :], ACT.Sigmoid).then_inc(score_ready, 1)

                def split(i, c):
                    t = U * i + c
                    wait(act, w_loaded[c], 16 * (i + 1))
                    wait(act, q_done, NTB * (t - U + 1))
                    nc.scalar.activation(w_hi[:, c], w_raw[:, c], ACT.Copy).then_inc(w_hi_ready, 1)

                def evacuate(i, c):
                    t = U * i + c
                    wait(act, stored[c], 32 * i)
                    for n in range(NTB):
                        wait(act, q_done, NTB * t + n + 1)
                        nc.scalar.activation(stage_hi[:, c, n * TBW:(n + 1) * TBW], ps_q[n][:, :],
                                             ACT.Copy).then_inc(q_hi_ready, 1)

                pipeline(act, CH, U, [(0, split), (1, evacuate)])

            @block.tensor
            def _(pe):
                pe.wait_ge(r_lo_ready, 1)
                for n in range(NTB):
                    pe.wait_ge(logits_copied, n) if n else None
                    j = 0
                    for k in range(KC):
                        for a, b in ((r_hi, xt_hi), (r_lo, xt_hi), (r_hi, xt_lo)):
                            last = nc.tensor.matmul(ps_r[0:E, :], a[:, k, :],
                                                    b[:, k, n * TBW:(n + 1) * TBW],
                                                    start=(j == 0), stop=(j == 3 * KC - 1))
                            j += 1
                    last.then_inc(logits_done, 1)
                pe.wait_ge(logits_copied, NTB)
                for t in range(NT):
                    last = nc.tensor.transpose(ps_s[:, t, :], logits_t[:, t * P:(t + 1) * P],
                                               ident[0:E, 0:E])
                last.then_inc(logits_turned, 1)

                def multiply(i, c):
                    t = U * i + c
                    wait(pe, w_lo_ready, t + 1)
                    for n in range(NTB):
                        wait(pe, q_lo_ready, NTB * (t - 1) + n + 1)
                        j = 0
                        for k in range(KC):
                            for a, b in ((w_hi, xt_hi), (w_lo, xt_hi), (w_hi, xt_lo)):
                                last = nc.tensor.matmul(ps_q[n][:, :], a[:, c, k, :],
                                                        b[:, k, n * TBW:(n + 1) * TBW],
                                                        start=(j == 0), stop=(j == 3 * KC - 1))
                                j += 1
                        last.then_inc(q_done, 1)

                pipeline(pe, CH, U, [(0, multiply)])

                pe.wait_ge(chosen_ready, 1)
                pe.wait_ge(consts_ready, 5)
                nc.tensor.matmul(ps_rank[:, :, :], earlier[:, :], chosen[:, :, :], start=True,
                                 stop=False)
                for t in range(NT - 1):
                    later = NT - 1 - t
                    nc.tensor.matmul(ps_rank[:, t + 1:, :], ones[:, :],
                                     chosen[:, t:t + 1, :].broadcast_to([P, later, E]),
                                     start=False, stop=(t == NT - 2))
                for t in range(NT):
                    last = nc.tensor.matmul(ps_count[:, :, :], ones[:, :], chosen[:, t:t + 1, :],
                                            start=(t == 0), stop=(t == NT - 1))
                last.then_inc(ranks_done, 1)

            @block.gpsimd
            def _(pool):
                nc.gpsimd.memset(ones[:, :], 1.0).then_inc(consts_zeroed, 1)
                pool.wait_ge(consts_zeroed, 1)
                nc.gpsimd.affine_select(out=earlier[:, :], in_=ones[:, :], compare_op=ALU.is_gt,
                                        fill=0.0, base=0, pattern=[[1, P]],
                                        channel_multiplier=-1).then_inc(consts_ready, 1)
                nc.gpsimd.iota(tokens[:, :], pattern=[[P, NT]], base=0,
                               channel_multiplier=1).then_inc(consts_ready, 1)
                nc.gpsimd.iota(tile_int[:, :], pattern=[[1, NST]], base=0,
                               channel_multiplier=0).then_inc(consts_ready, 1)
                nc.gpsimd.iota(pads[:, :], pattern=[[0, 1]], base=T,
                               channel_multiplier=1).then_inc(consts_ready, 1)
                pool.wait_ge(consts_ready, 4)
                nc.gpsimd.tensor_copy(tile_no[:, :, 0], tile_int[:, :]).then_inc(consts_ready, 1)

            @block.vector
            def _(dve):
                dve.wait_ge(r_hi_ready, 1)
                nc.vector.tensor_tensor(r_lo[:, :, :], r_raw[:, :, :], r_hi[:, :, :].bitcast(F32),
                                        ALU.subtract).then_inc(r_lo_ready, 1)

                def split(i, c):
                    t = U * i + c
                    wait(dve, w_hi_ready, t + 1)
                    nc.vector.tensor_tensor(w_lo[:, c], w_raw[:, c], w_hi[:, c].bitcast(F32),
                                            ALU.subtract).then_inc(w_lo_ready, 1)

                def evacuate(i, c):
                    t = U * i + c
                    for n in range(NTB):
                        cols = slice(n * TBW, (n + 1) * TBW)
                        wait(dve, q_hi_ready, NTB * t + n + 1)
                        nc.vector.tensor_tensor(stage_lo[:, c, cols], ps_q[n][:, :],
                                                stage_hi[:, c, cols].bitcast(F32),
                                                ALU.subtract).then_inc(q_lo_ready, 1)

                pipeline(dve, CH, U, [(0, split), (1, evacuate)])

                steps = [0]

                def then(instruction):
                    steps[0] += 1
                    instruction.then_inc(routing, 1)
                    dve.wait_ge(routing, steps[0])

                def each(ap, n):
                    return ap.broadcast_to([P, NT, n])

                def column(ap):
                    return ap[:, :].rearrange("p (t a) -> p t a", a=1)

                def top2(value, n, flag):
                    for e in range(n):
                        other = value[:, :, e:e + 1]
                        if e:
                            then(nc.vector.tensor_tensor(beats[:, :, 0:e], each(other, e),
                                                         value[:, :, 0:e], ALU.is_gt))
                        if e < n - 1:
                            then(nc.vector.tensor_tensor(beats[:, :, e + 1:n], each(other, n - e - 1),
                                                         value[:, :, e + 1:n], ALU.is_ge))
                        then(nc.vector.memset(beats[:, :, e:e + 1], 0.0))
                        if e:
                            then(nc.vector.tensor_tensor(rank[:, :, 0:n], rank[:, :, 0:n],
                                                         beats[:, :, 0:n], ALU.add))
                        else:
                            then(nc.vector.tensor_copy(rank[:, :, 0:n], beats[:, :, 0:n]))
                    then(nc.vector.tensor_scalar(flag, rank[:, :, 0:n], 2.0, None, ALU.is_lt))

                dve.wait_ge(score_ready, 1)
                dve.wait_ge(bias_loaded, 16)
                then(nc.vector.tensor_tensor(biased[:, :, :], score[:, :, :],
                                             bias_b[:, :, :].broadcast_to([P, NT, E]), ALU.add))
                pairs = biased[:, :, :].rearrange("p t (g j) -> p t g j", j=2)
                then(nc.vector.tensor_tensor(group[:, :, :], pairs[:, :, :, 0], pairs[:, :, :, 1],
                                             ALU.add))
                top2(group, G, group[:, :, :])
                for j in range(2):
                    then(nc.vector.tensor_tensor(pairs[:, :, :, j], pairs[:, :, :, j],
                                                 group[:, :, :], ALU.mult))
                top2(biased, E, chosen[:, :, :])
                dve.sem_inc(chosen_ready, 1)
                then(nc.vector.tensor_tensor(weight[:, :, :], chosen[:, :, :], score[:, :, :],
                                             ALU.mult))
                then(nc.vector.reduce_sum(total[:, :], weight[:, :, :], AX.X))
                then(nc.vector.tensor_scalar(total[:, :], total[:, :], 1e-20, None, ALU.add))
                then(nc.vector.reciprocal(total[:, :], total[:, :]))
                then(nc.vector.tensor_scalar(total[:, :], total[:, :], ROUTE_SCALE, None, ALU.mult))
                then(nc.vector.tensor_tensor(weight[:, :, :], weight[:, :, :], each(column(total), E),
                                             ALU.mult))

                dve.wait_ge(ranks_done, 1)
                dve.wait_ge(consts_ready, 5)
                then(nc.vector.tensor_scalar(total[:, :], tile_no[:, 0:NT, 0], float(P), None,
                                             ALU.mult))
                then(nc.vector.tensor_tensor(
                    over[:, :, :], ps_count[:, :, :].rearrange("p a e -> p e a")
                    .broadcast_to([P, E, NT]),
                    total[:, :].rearrange("p (a t) -> p a t", a=1).broadcast_to([P, E, NT]),
                    ALU.is_gt))
                then(nc.vector.reduce_sum(n_tiles[:, 0, :], over[:, :, :], AX.X))
                then(nc.vector.memset(first_tile[:, :, 0:1], 0.0))
                for e in range(1, E):
                    then(nc.vector.tensor_tensor(first_tile[:, :, e:e + 1], first_tile[:, :, e - 1:e],
                                                 n_tiles[:, :, e - 1:e], ALU.add))
                then(nc.vector.tensor_tensor(started[:, :, :], tile_no[:, :, :]
                                             .broadcast_to([P, NST, E]),
                                             first_tile[:, :, :].broadcast_to([P, NST, E]),
                                             ALU.is_ge))
                then(nc.vector.reduce_sum(expert_f[:, :], started[:, :, :], AX.X))
                then(nc.vector.tensor_scalar(expert_f[:, :], expert_f[:, :], -1.0, None, ALU.add))
                then(nc.vector.tensor_copy(expert_of[:, :], expert_f[:, :]))
                then(nc.vector.tensor_scalar(first_tile[:, :, :], first_tile[:, :, :], float(P), None,
                                             ALU.mult))
                then(nc.vector.tensor_tensor(slot[:, :, :], ps_rank[:, :, :],
                                             first_tile[:, :, :].broadcast_to([P, NT, E]), ALU.add))
                for fill, pick, into in ((-1.0, ALU.max, slot_b), (float(NSLOT), ALU.min, slot_a)):
                    then(nc.vector.tensor_scalar(rank[:, :, :], slot[:, :, :], -fill, None, ALU.add))
                    then(nc.vector.tensor_tensor(rank[:, :, :], rank[:, :, :], chosen[:, :, :],
                                                 ALU.mult))
                    then(nc.vector.tensor_scalar(rank[:, :, :], rank[:, :, :], fill, None, ALU.add))
                    then(nc.vector.tensor_reduce(into[:, :], rank[:, :, :], AX.X, pick))
                for n, of in enumerate((slot_a, slot_b)):
                    then(nc.vector.tensor_tensor(beats[:, :, :], slot[:, :, :], each(column(of), E),
                                                 ALU.is_equal))
                    then(nc.vector.tensor_tensor(beats[:, :, :], beats[:, :, :], weight[:, :, :],
                                                 ALU.mult))
                    then(nc.vector.reduce_sum(entry[:, :, n, 1], beats[:, :, :], AX.X))
                    then(nc.vector.tensor_copy(slot_of[:, :, n], of[:, :]))
                    then(nc.vector.tensor_copy(entry[:, :, n, 0].bitcast(I32), tokens[:, :]))
                then(nc.vector.memset(slot_table[:, :, 1], 0.0))
                then(nc.vector.tensor_copy(slot_table[:, :, 0].bitcast(I32),
                                           pads[:, :].broadcast_to([P, NST])))


def attend_phase(nc, ident, q_hi, q_lo, v_dram, row_dram, gate, up, g_sb, u_sb, attended):
    HS = 4
    NB = 12
    U = HS * NB
    STEPS = B * H * NB
    QT = S // P
    ROWS = 3 * DK
    VW = 2 * DK + 2
    BLOCKS = [(0, 0), (1, 0), (1, 2), (1, 7), (0, 1), (1, 3), (0, 3), (1, 4), (0, 2), (1, 1), (1, 6),
              (1, 5)]
    PIECES = [(t, k0, min(TBW, P * (t + 1) - k0)) for t, k0 in (
        (0, 0), (3, 0), (7, 0), (6, 0), (4, 0), (5, 0), (7, TBW), (5, TBW), (6, TBW), (1, 0), (2, 0),
        (4, TBW))]
    AHEAD = 2 * NB
    LO_POOL = [0, 1, 2, 3, 4, 5, 6, 8, 9, 11]
    LO_DVE = [n for n in range(NB) if n not in LO_POOL]
    HI_DVE = [1, 10]
    HI_ACT = [n for n in range(NB) if n not in HI_DVE]
    EXP, HI, LO, VALUE = AHEAD, AHEAD + 2, AHEAD + 4, AHEAD + 7
    COPY, TURN, NORM = AHEAD + 7, AHEAD + 9, AHEAD + 10
    ROW = NB + 2
    ROW_LATER = 1
    STARTS = [min(n for n in range(NB) if BLOCKS[n][0] == half) for half in range(2)]
    ENDS = [max(n for n in range(NB) if BLOCKS[n][0] == half) for half in range(2)]
    assert all(BLOCKS[n][1] == 0 for n in STARTS) and ENDS[1] == NB - 1
    ROWS_BEFORE = {n: (n + TURN - ROW - ROW_LATER) // NB + 1 for n in ENDS}
    TURNS_BEFORE = sum((ROW - n - TURN - 1 + ROW_LATER) // NB + 1 for n in ENDS)
    DIAGONAL = [n for n, (qb, kt) in enumerate(BLOCKS) if kt >= 4 * qb]

    def span(n):
        qb, kt = BLOCKS[n]
        first = max(0, (kt - 4 * qb) * P)
        return first, TBW - first

    def count(of, i, c):
        return len(of) * (HS * i + c // NB) + sum(n <= c % NB for n in of)

    with ExitStack() as ctx:
        sbuf, psum, sem = allocator(nc, ctx)
        qs = sbuf("qs", [P, HS, S], F32R)
        ks = sbuf("ks", [P, HS, S], F32R)
        vs = sbuf("vs", [P, HS, QT, VW], F32R)
        late = sbuf("late", [P, P], BF16)
        eye = sbuf("eye", [P, P], BF16)
        maxima = sbuf("maxima", [P, HS, QT + 4])
        row_stage = sbuf("row_stage", [QT, HS, P], F32R)
        NP = 6
        prob = sbuf("prob", [P, NP, TBW])
        prob_hi = sbuf("prob_hi", [P, NP, TBW], F32R)
        prob_lo = sbuf("prob_lo", [P, NP, TBW], F32R)
        o_copy = sbuf("o_copy", [VW, 2, TBW])
        o_part = sbuf("o_part", [P, 4, DK])
        o_sum = sbuf("o_sum", [P, 4, DK])
        o_inv = sbuf("o_inv", [P, 4, 1])
        NM = 3
        ps_m = [psum(f"ps_m{n}", [P, TBW]) for n in range(NM)]
        NS = 2
        ps_s = [psum(f"ps_s{n}", [P, TBW]) for n in range(NS)]
        ps_o = [psum(f"ps_o{n}", [P, TBW]) for n in range(2)]
        ps_x = psum("ps_x", [P, TBW])
        ps_ot = ps_x[:, 0:4 * VW].rearrange("p (q w) -> p q w", q=4)
        ps_row = ps_x[:, TBW - P:]
        head_loaded = [sem(f"head_loaded{n}") for n in range(HS)]
        values_loaded = [sem(f"values_loaded{n}") for n in range(HS)]
        row_saved = [sem(f"row_saved{n}") for n in range(HS)]
        row_loaded = [sem(f"row_loaded{n}") for n in range(HS)]
        consts_ready = sem("consts_ready")
        consts_zeroed = sem("consts_zeroed")
        experts_loaded = sem("experts_loaded")
        m_done = sem("m_done")
        m_read = sem("m_read")
        max_ready = sem("max_ready")
        row_turned = sem("row_turned")
        row_ready = sem("row_ready")
        s_done = sem("s_done")
        exp_done = sem("exp_done")
        hi_act = sem("hi_act")
        hi_dve = sem("hi_dve")
        lo_dve = sem("lo_dve")
        lo_pool = sem("lo_pool")
        pv_done = sem("pv_done")
        o_copied = sem("o_copied")
        o_turned = sem("o_turned")
        part_ready = sem("part_ready")
        sum_ready = sem("sum_ready")
        inv_ready = sem("inv_ready")
        o_ready = sem("o_ready")

        def wait_hi(eng, i, c):
            if c % NB in HI_DVE:
                wait(eng, hi_dve, count(HI_DVE, i, c))
            else:
                wait(eng, hi_act, count(HI_ACT, i, c))

        with nc.Block() as block:
            @block.sync
            def _(sp):
                def load_head(i, c):
                    h, b = 2 * i + c // 2, c % 2
                    wait(sp, s_done, NB * (HS * (i - 1) + c + 1))
                    sp_cols = slice(b * S, (b + 1) * S)
                    for n, (q_src, k_src) in enumerate(((q_hi, q_hi), (q_hi, q_lo), (q_lo, q_hi))):
                        rows = slice(n * DK, (n + 1) * DK)
                        sp.dma_start(qs[rows, c, :].bitcast(F32), q_src[bass.ds(h * DK, DK), sp_cols]
                                     ).then_inc(head_loaded[c], 16)
                        sp.dma_start(ks[rows, c, :].bitcast(F32), k_src[bass.ds(D + h * DK, DK), sp_cols]
                                     ).then_inc(head_loaded[c], 16)

                def load_values(i, c):
                    h, b = 2 * i + c // 2, c % 2
                    wait(sp, pv_done, NB * (HS * (i - 1) + c + 1))
                    sp.dma_start(vs[:, c, :, 0:2 * DK].bitcast(F32),
                                 v_dram[bass.ds(h, 1), :, b * QT:(b + 1) * QT, :]
                                 .rearrange("h p t d -> (h p) t d")).then_inc(values_loaded[c], 16)

                def load_experts(i, c):
                    g = HS * i + c
                    for dst, src in ((g_sb, gate), (u_sb, up)):
                        sp.dma_start(dst[:, bass.ds(g, 1), :], src[bass.ds(g, 1)]
                                     .rearrange("a p f -> p a f")).then_inc(experts_loaded, 16)

                pipeline(sp, B * H, HS, [(0, load_head), (1, load_values), (1, load_experts)])
                assert E * KC == B * H
                sp.wait_ge(experts_loaded, 32 * E * KC)

            @block.gpsimd
            def _(pool):
                nc.gpsimd.memset(late[:, :], 0.0).then_inc(consts_zeroed, 1)
                nc.gpsimd.memset(eye[:, :], 0.0).then_inc(consts_zeroed, 1)
                pool.wait_ge(consts_zeroed, 2)
                nc.gpsimd.affine_select(out=late[:, :], in_=late[:, :], compare_op=ALU.is_ge,
                                        fill=MASKED, base=0, pattern=[[1, P]],
                                        channel_multiplier=-1).then_inc(consts_ready, 1)
                nc.gpsimd.affine_select(out=eye[:, :], in_=eye[:, :], compare_op=ALU.not_equal,
                                        fill=1.0, base=0, pattern=[[-1, P]],
                                        channel_multiplier=1).then_inc(consts_ready, 1)
                pool.wait_ge(consts_ready, 2)
                nc.gpsimd.memset(ks[ROWS:ROWS + 1, :, :].bitcast(F32), 1.0).then_inc(consts_ready, 1)
                pool.wait_ge(consts_ready, 3)
                nc.gpsimd.memset(vs[:, :, :, 2 * DK:].bitcast(F32), 1.0).then_inc(consts_ready, 1)

                def lo(i, c):
                    n = c % NB
                    if n not in LO_POOL:
                        return
                    first, w = span(n)
                    wait_hi(pool, i, c)
                    nc.gpsimd.tensor_tensor(prob_lo[:, c % NP, 0:w], prob[:, c % NP, 0:w],
                                            prob_hi[:, c % NP, 0:w].bitcast(F32),
                                            ALU.subtract).then_inc(lo_pool, 1)

                pipeline(pool, STEPS, U, [(0, lo)])

            @block.scalar
            def _(act):
                def row(i, c):
                    if c % NB != 0:
                        return
                    g = HS * i + c // NB
                    wait(act, row_turned, g + 1)
                    wait(act, row_saved[c // NB], 16 * i)
                    nc.scalar.activation(row_stage[:, c // NB, :], ps_row[0:QT, :], ACT.Copy,
                                         scale=-1.0).then_inc(row_ready, 1)
                    wait(act, row_ready, g + 1)
                    act.dma_start(row_dram[bass.ds(g, 1), :].rearrange("a (t q) -> (a t) q", t=QT),
                                  row_stage[:, c // NB, :].bitcast(F32)
                                  ).then_inc(row_saved[c // NB], 16)

                def load_row(i, c):
                    if c % NB != 0:
                        return
                    g = HS * i + c // NB
                    wait(act, row_saved[c // NB], 16 * (i + 1))
                    act.dma_start(qs[ROWS:ROWS + 1, c // NB, :].bitcast(F32),
                                  row_dram[bass.ds(g, 1), :]).then_inc(row_loaded[c // NB], 16)

                def exp(i, c):
                    step = U * i + c
                    first, w = span(c % NB)
                    wait(act, s_done, step + 1)
                    wait(act, lo_dve, count(LO_DVE, i, c - NP))
                    wait(act, lo_pool, count(LO_POOL, i, c - NP))
                    nc.scalar.activation(prob[:, c % NP, 0:w], ps_s[c % NS][:, 0:w], ACT.Exp,
                                         scale=SCALE).then_inc(exp_done, 1)

                def hi(i, c):
                    step = U * i + c
                    if c % NB in HI_DVE:
                        return
                    first, w = span(c % NB)
                    wait(act, exp_done, step + 1)
                    wait(act, pv_done, step - NP + 1)
                    nc.scalar.activation(prob_hi[:, c % NP, 0:w], prob[:, c % NP, 0:w],
                                         ACT.Copy).then_inc(hi_act, 1)

                def copy_o(i, c):
                    n = c % NB
                    if n not in ENDS:
                        return
                    half = BLOCKS[n][0]
                    o = 2 * (HS * i + c // NB) + half
                    wait(act, pv_done, U * i + c + 1)
                    wait(act, o_turned, o - 1)
                    nc.scalar.activation(o_copy[:, half, :], ps_o[half][0:VW, :],
                                         ACT.Copy).then_inc(o_copied, 1)

                pipeline(act, STEPS, U, [(HI, hi), (EXP, exp), (ROW + 1, row), (COPY, copy_o),
                                         (ROW + 4, load_row)])

            @block.vector
            def _(dve):
                def maximum(i, c):
                    g = HS * i + c // NB
                    slot = c // NB
                    t, k0, w = PIECES[c % NB]
                    step = U * i + c
                    wait(dve, m_done, step + 1)
                    if c % NB == 0:
                        wait(dve, row_turned, HS * (i - 1) + slot + 1)
                    scores = ps_m[c % NM][:, 0:w]
                    at = t if k0 + w == P * (t + 1) else QT + t - 4
                    nc.vector.reduce_max(maxima[:, slot, at:at + 1], scores, AX.X).then_inc(m_read, 1)
                    if c % NB == NB - 1:
                        wait(dve, m_read, step + 1)
                        nc.vector.tensor_tensor(maxima[:, slot, 4:QT], maxima[:, slot, 4:QT],
                                                maxima[:, slot, QT:QT + 4],
                                                ALU.max).then_inc(max_ready, 1)

                def lo(i, c):
                    n = c % NB
                    if n in LO_POOL:
                        return
                    first, w = span(n)
                    wait_hi(dve, i, c)
                    nc.vector.tensor_tensor(prob_lo[:, c % NP, 0:w], prob[:, c % NP, 0:w],
                                            prob_hi[:, c % NP, 0:w].bitcast(F32),
                                            ALU.subtract).then_inc(lo_dve, 1)

                def hi(i, c):
                    step = U * i + c
                    if c % NB not in HI_DVE:
                        return
                    first, w = span(c % NB)
                    wait(dve, exp_done, step + 1)
                    wait(dve, pv_done, step - NP + 1)
                    nc.vector.tensor_copy(prob_hi[:, c % NP, 0:w], prob[:, c % NP, 0:w]
                                          ).then_inc(hi_dve, 1)

                def normalize(i, c):
                    n = c % NB
                    if n not in ENDS:
                        return
                    half = BLOCKS[n][0]
                    h, b = 2 * i + c // NB // 2, c // NB % 2
                    o = 2 * (HS * i + c // NB) + half
                    wait(dve, o_turned, o + 1)
                    wait(dve, o_ready, o)
                    nc.vector.reciprocal(o_inv[:, :, :], ps_ot[:, :, 2 * DK:2 * DK + 1]).then_inc(inv_ready, 1)
                    nc.vector.tensor_copy(o_part[:, :, :], ps_ot[:, :, DK:2 * DK]).then_inc(part_ready, 1)
                    wait(dve, part_ready, o + 1)
                    nc.vector.tensor_tensor(o_sum[:, :, :], ps_ot[:, :, 0:DK], o_part[:, :, :],
                                            ALU.add).then_inc(sum_ready, 1)
                    wait(dve, inv_ready, o + 1)
                    wait(dve, sum_ready, o + 1)
                    tiles = slice(b * QT + 4 * half, b * QT + 4 * half + 4)
                    nc.vector.tensor_tensor(attended[:, tiles, bass.ds(h * DK, DK)], o_sum[:, :, :],
                                            o_inv[:, :, :].broadcast_to([P, 4, DK]),
                                            ALU.mult).then_inc(o_ready, 1)

                pipeline(dve, STEPS, U, [(LO, lo), (HI, hi), (NORM, normalize), (0, maximum)])

            @block.tensor
            def _(pe):
                pe.wait_ge(consts_ready, 4)

                def maximum(i, c):
                    slot = c // NB
                    t, k0, w = PIECES[c % NB]
                    if c % NB == 0:
                        wait(pe, head_loaded[slot], 96 * (i + 1))
                    wait(pe, m_read, U * i + c - NM + 1)
                    diagonal = k0 + w == P * (t + 1)
                    last = nc.tensor.matmul(ps_m[c % NM][:, 0:w], qs[0:ROWS, slot, t * P:(t + 1) * P],
                                            ks[0:ROWS, slot, k0:k0 + w], start=True,
                                            stop=not diagonal)
                    if diagonal:
                        last = nc.tensor.matmul(ps_m[c % NM][:, w - P:w], late[:, :], eye[:, :],
                                                start=False, stop=True)
                    last.then_inc(m_done, 1)

                def turn_row(i, c):
                    if c % NB != 0:
                        return
                    slot = c // NB
                    g = HS * i + slot
                    wait(pe, max_ready, g + 1)
                    wait(pe, row_ready, g)
                    wait(pe, o_ready, 2 * g + TURNS_BEFORE)
                    nc.tensor.transpose(ps_row[0:QT, :], maxima[:, slot, 0:QT],
                                        ident[:, :]).then_inc(row_turned, 1)

                def score(i, c):
                    slot = c // NB
                    qb, kt = BLOCKS[c % NB]
                    first, w = span(c % NB)
                    if c % NB == 0:
                        wait(pe, row_loaded[slot], 16 * (i + 1))
                    wait(pe, exp_done, U * i + c - NS + 1)
                    q0 = qb * TBW + first
                    diagonal = c % NB in DIAGONAL
                    last = nc.tensor.matmul(ps_s[c % NS][:, 0:w],
                                            ks[0:ROWS + 1, slot, kt * P:(kt + 1) * P],
                                            qs[0:ROWS + 1, slot, q0:q0 + w], start=True,
                                            stop=not diagonal)
                    if diagonal:
                        last = nc.tensor.matmul(ps_s[c % NS][:, 0:P], eye[:, :], late[:, :],
                                                start=False, stop=True)
                    last.then_inc(s_done, 1)

                def value(i, c):
                    slot = c // NB
                    n = c % NB
                    qb, kt = BLOCKS[n]
                    first, w = span(n)
                    if n == 0:
                        wait(pe, values_loaded[slot], 16 * (i + 1))
                    if n in STARTS:
                        wait(pe, o_copied, 2 * (HS * i + slot) + qb - 1)
                    if n in LO_POOL:
                        wait(pe, lo_pool, count(LO_POOL, i, c))
                    else:
                        wait(pe, lo_dve, count(LO_DVE, i, c))
                    into = ps_o[qb][0:VW, first:first + w]
                    nc.tensor.matmul(into, vs[:, slot, kt, :], prob_hi[:, c % NP, 0:w],
                                     start=n in STARTS, stop=False)
                    nc.tensor.matmul(into, vs[:, slot, kt, :], prob_lo[:, c % NP, 0:w], start=False,
                                     stop=n in ENDS).then_inc(pv_done, 1)

                def turn_o(i, c):
                    n = c % NB
                    if n not in ENDS:
                        return
                    half = BLOCKS[n][0]
                    o = 2 * (HS * i + c // NB) + half
                    wait(pe, o_copied, o + 1)
                    wait(pe, o_ready, o)
                    rows = HS * i + c // NB + ROWS_BEFORE[n]
                    wait(pe, row_ready, min(rows, B * H) if isinstance(rows, int) else rows)
                    for q in range(4):
                        last = nc.tensor.transpose(ps_ot[:, q, 0:VW], o_copy[:, half, q * P:(q + 1) * P],
                                                   ident[0:VW, 0:VW])
                    last.then_inc(o_turned, 1)

                pipeline(pe, STEPS, U, [(AHEAD, score), (0, maximum), (VALUE, value), (TURN, turn_o),
                                        (ROW, turn_row)])


def out_phase(nc, wo, down, ident, attended, d_sb, out):
    with ExitStack() as ctx:
        sbuf, psum, sem = allocator(nc, ctx)
        U = 2
        work = sbuf("work", [P, 2 * U, D])
        wo_raw = work
        wo_hi = sbuf("wo_hi", [P, KC, D], F32R)
        wo_lo = sbuf("wo_lo", [P, KC, D], F32R)
        x_tile = work[:, 0:U, :]
        a_tile = work[:, U:2 * U, :]
        y_tile = sbuf("y_tile", [P, U, D])
        a_hi = sbuf("a_hi", [P, U, KC, P], F32R)
        a_lo = sbuf("a_lo", [P, U, KC, P], F32R)
        ps_t = [psum(f"ps_at{n}", [P, KC, P]) for n in range(U)]
        ps_y = [psum(f"ps_ay{n}", [P, D]) for n in range(U)]
        x_loaded = [sem(f"xr_loaded{n}") for n in range(U)]
        y_stored = [sem(f"y_stored{n}") for n in range(U)]
        wo_loaded = sem("wo_loaded")
        down_loaded = sem("down_loaded")
        wo_hi_ready = sem("wo_hi_ready")
        wo_lo_ready = sem("wo_lo_ready")
        tile_ready = sem("a_tile_ready")
        turned = sem("a_turned")
        hi_ready = sem("a_hi_ready")
        lo_ready = sem("a_lo_ready")
        y_done = sem("a_y_done")
        added = sem("a_added")

        with nc.Block() as block:
            @block.sync
            def _(sp):
                sp.dma_start(wo_raw[:, :, :], wo).then_inc(wo_loaded, 16)
                TAIL = FCH[-1][1]
                for e in range(E):
                    at = len(FCH) * e
                    sp.dma_start(d_sb[:, at:at + 2, :], down[e, 0:2 * P, :]
                                 .rearrange("(k p) d -> p k d", p=P)).then_inc(down_loaded, 16)
                    sp.dma_start(d_sb[0:TAIL, at + 2, :], down[e, 2 * P:F, :]
                                 ).then_inc(down_loaded, 16)
                sp.wait_ge(wo_lo_ready, 1)

                def load(i, c):
                    t = U * i + c
                    wait(sp, added, t - U + 1)
                    sp.dma_start(x_tile[:, c, :], out[bass.ds(t * P, P), :]).then_inc(x_loaded[c], 16)

                def store(i, c):
                    t = U * i + c
                    wait(sp, added, t + 1)
                    sp.dma_start(out[bass.ds(t * P, P), :], y_tile[:, c, :]).then_inc(y_stored[c], 16)
                pipeline(sp, NT, U, [(0, load), (3, store)])
                sp.wait_ge(down_loaded, 32 * E)
                for n in range(U):
                    sp.wait_ge(y_stored[n], 16 * (NT // U))

            @block.scalar
            def _(act):
                act.wait_ge(wo_loaded, 16)
                nc.scalar.activation(wo_hi[:, :, :], wo_raw[:, :, :], ACT.Copy).then_inc(wo_hi_ready, 1)

                def hi(i, c):
                    t = U * i + c
                    wait(act, turned, t + 1)
                    wait(act, y_done, t - U + 1)
                    nc.scalar.activation(a_hi[:, c], ps_t[c][:, :, :], ACT.Copy).then_inc(hi_ready, 1)
                pipeline(act, NT, U, [(0, hi)])

            @block.vector
            def _(dve):
                def copy(i, c):
                    t = U * i + c
                    wait(dve, turned, t - U + 1)
                    nc.vector.tensor_copy(a_tile[:, c, :], attended[:, bass.ds(t, 1), :]
                                          .rearrange("p a d -> p (a d)")).then_inc(tile_ready, 1)

                def lo(i, c):
                    t = U * i + c
                    wait(dve, hi_ready, t + 1)
                    nc.vector.tensor_tensor(a_lo[:, c], ps_t[c][:, :, :], a_hi[:, c].bitcast(F32),
                                            ALU.subtract).then_inc(lo_ready, 1)

                def add(i, c):
                    t = U * i + c
                    wait(dve, y_done, t + 1)
                    wait(dve, x_loaded[c], 16 * (i + 1))
                    wait(dve, y_stored[c], 16 * i)
                    nc.vector.tensor_tensor(y_tile[:, c, :], ps_y[c][:, :], x_tile[:, c, :],
                                            ALU.add).then_inc(added, 1)
                dve.wait_ge(wo_hi_ready, 1)
                nc.vector.tensor_tensor(wo_lo[:, :, :], wo_raw[:, :, :], wo_hi[:, :, :].bitcast(F32),
                                        ALU.subtract).then_inc(wo_lo_ready, 1)
                dve.wait_ge(wo_lo_ready, 1)
                pipeline(dve, NT, U, [(0, copy), (1, lo), (2, add)])

            @block.tensor
            def _(pe):
                def turn(i, c):
                    t = U * i + c
                    wait(pe, tile_ready, t + 1)
                    wait(pe, lo_ready, t - U + 1)
                    for k in range(KC):
                        last = nc.tensor.transpose(ps_t[c][:, k, :], a_tile[:, c, k * P:(k + 1) * P],
                                                   ident[:, :])
                    last.then_inc(turned, 1)

                def multiply(i, c):
                    t = U * i + c
                    wait(pe, lo_ready, t + 1)
                    wait(pe, added, t - U + 1)
                    n = 0
                    for k in range(KC):
                        for a, b in ((a_hi, wo_hi), (a_hi, wo_lo), (a_lo, wo_hi)):
                            last = nc.tensor.matmul(ps_y[c][:, :], a[:, c, k, :], b[:, k, :],
                                                    start=(n == 0), stop=(n == 3 * KC - 1))
                            n += 1
                    last.then_inc(y_done, 1)
                pe.wait_ge(wo_lo_ready, 1)
                pipeline(pe, NT, U, [(0, turn), (1, multiply)])


def shared_phase(nc, x, gate, up, down, xt_hi, xt_lo, slot_of, entry, slot_table, slots_dram, out):
    with ExitStack() as ctx:
        sbuf, psum, sem = allocator(nc, ctx)
        U = 2
        NF = len(FCH)
        acc = sbuf("acc", [P, NT, D])
        g_raw = sbuf("g_raw", [P, KC, F])
        u_raw = sbuf("u_raw", [P, KC, F])
        d_raw = sbuf("d_raw", [P, NF, D])
        g_hi = sbuf("g_hi", [P, U, KC, F], F32R)
        g_lo = sbuf("g_lo", [P, U, KC, F], F32R)
        u_hi = sbuf("u_hi", [P, U, KC, F], F32R)
        u_lo = sbuf("u_lo", [P, U, KC, F], F32R)
        d_hi = sbuf("d_hi", [P, U, NF, D], F32R)
        d_lo = sbuf("d_lo", [P, U, NF, D], F32R)
        silu = sbuf("silu", [P, 2, TBW])
        hid = sbuf("hid", [P, 1, TBW])
        hid_hi = sbuf("hid_hi", [P, NF, TBW], F32R)
        hid_lo = sbuf("hid_lo", [P, NF, TBW], F32R)
        ps_g = [psum(f"ps_g{n}", [P, TBW]) for n in range(2)]
        ps_u = [psum(f"ps_u{n}", [P, TBW]) for n in range(2)]
        ps_y = [psum(f"ps_y{n}", [P, D]) for n in range(4)]
        loaded = sem("ffn_loaded")
        w_hi_ready = sem("ffn_w_hi")
        w_lo_ready = sem("ffn_w_lo")
        g_done = sem("g_done")
        u_done = sem("u_done")
        silu_ready = sem("silu_ready")
        hid_ready = sem("hid_ready")
        hid_hi_ready = sem("hid_hi_ready")
        hid_lo_ready = sem("hid_lo_ready")
        y_done = sem("y_done")
        added = sem("added")
        stored = sem("out_stored")
        x_loaded = sem("acc_loaded")
        pads_stored = sem("pads_stored")
        entries_stored = sem("entries_stored")
        table_loaded = sem("table_loaded")
        WEIGHTS = ((g_raw, g_hi, g_lo), (u_raw, u_hi, u_lo), (d_raw, d_hi, d_lo))
        TAIL = FCH[-1][1]

        with nc.Block() as block:
            @block.sync
            def _(sp):
                def load(i, c):
                    e = U * i + c
                    wait(sp, w_lo_ready, 4 * e)
                    for raw, src in ((g_raw, gate), (u_raw, up)):
                        sp.dma_start(raw[:, :, :], src[bass.ds(e, 1)].rearrange("a p k f -> (a p) k f")
                                     ).then_inc(loaded, 16)
                    rows = down[bass.ds(e, 1)].rearrange("a f d -> (a f) d")
                    sp.dma_start(d_raw[:, 0:2, :], rows[0:2 * P, :].rearrange("(k p) d -> p k d", p=P)
                                 ).then_inc(loaded, 16)
                    sp.dma_start(d_raw[0:TAIL, 2, :], rows[2 * P:F, :]).then_inc(loaded, 16)
                sp.dma_start(slots_dram.rearrange("(j p) a -> p j a", p=P), slot_table[:, :, :]
                             ).then_inc(pads_stored, 16)
                sp.dma_start(acc[:, :, :], x.rearrange("(t p) d -> p t d", p=P)).then_inc(x_loaded, 16)
                pipeline(sp, NSH, U, [(0, load)])
                sp.wait_ge(added, NSH * NT)
                for t in range(NT):
                    sp.dma_start(out[t * P:(t + 1) * P, :], acc[:, t, :]).then_inc(stored, 16)
                sp.wait_ge(stored, 16 * NT)

            @block.gpsimd
            def _(pool):
                pool.wait_ge(pads_stored, 16)
                n = 0
                for t in range(NT):
                    for k in range(2):
                        nc.gpsimd.indirect_dma_start(
                            slots_dram, bass.IndirectOffsetOnAxis(slot_of[:, t, k:k + 1], 0),
                            entry[:, t, k, :], None).then_inc(entries_stored, 16)
                        n += 16
                pool.wait_ge(entries_stored, n)
                pool.dma_start(slot_table[:, :, :], slots_dram.rearrange("(j p) a -> p j a", p=P)
                               ).then_inc(table_loaded, 16)
                pool.wait_ge(table_loaded, 16)

            def weight_parts(c):
                for raw, hi, lo in WEIGHTS[:2]:
                    yield raw[:, :, :], hi[:, c], lo[:, c]
                yield d_raw[:, 0:2, :], d_hi[:, c, 0:2], d_lo[:, c, 0:2]
                yield d_raw[0:TAIL, 2, :], d_hi[0:TAIL, c, 2], d_lo[0:TAIL, c, 2]

            @block.scalar
            def _(act):
                def split(i, c):
                    e = U * i + c
                    wait(act, loaded, 64 * (e + 1))
                    wait(act, y_done, NT * (e - U + 1))
                    for raw, hi, lo in weight_parts(c):
                        nc.scalar.activation(hi, raw, ACT.Copy).then_inc(w_hi_ready, 1)

                def chunks(i, c, tb):
                    e = U * i + c
                    for k, (f0, w) in enumerate(FCH):
                        n = NF * (NTB * e + tb) + k
                        wait(act, g_done, n + 1)
                        wait(act, hid_ready, n - 1)
                        s = (NF * tb + k) % 2
                        nc.scalar.activation(silu[0:w, s, :], ps_g[s][0:w, :], ACT.Silu).then_inc(silu_ready, 1)
                        wait(act, hid_ready, n + 1)
                        wait(act, y_done, 4 * (NTB * e + tb))
                        nc.scalar.activation(hid_hi[0:w, k, :], hid[0:w, 0, :], ACT.Copy).then_inc(hid_hi_ready, 1)

                def block_e(i, c):
                    for tb in range(NTB):
                        chunks(i, c, tb)
                pipeline(act, NSH, U, [(0, split), (1, block_e)])

            @block.vector
            def _(dve):
                def split(i, c):
                    e = U * i + c
                    for n, (raw, hi, lo) in enumerate(weight_parts(c)):
                        wait(dve, w_hi_ready, 4 * e + n + 1)
                        nc.vector.tensor_tensor(lo, raw, hi.bitcast(F32), ALU.subtract).then_inc(w_lo_ready, 1)

                def add(e, i, c, tb):
                    for q in range(4):
                        t = 4 * tb + q
                        wait(dve, y_done, NT * e + t + 1)
                        wait(dve, added, NT * (e - 1) + t + 1)
                        nc.vector.tensor_tensor(acc[:, t, :], ps_y[q][:, :], acc[:, t, :],
                                                ALU.add).then_inc(added, 1)

                def block_e(i, c):
                    e = U * i + c
                    for tb in range(NTB):
                        for k, (f0, w) in enumerate(FCH):
                            n = NF * (NTB * e + tb) + k
                            s = (NF * tb + k) % 2
                            wait(dve, silu_ready, n + 1)
                            wait(dve, u_done, n + 1)
                            wait(dve, hid_lo_ready, n)
                            nc.vector.tensor_tensor(hid[0:w, 0, :], ps_u[s][0:w, :], silu[0:w, s, :],
                                                    ALU.mult).then_inc(hid_ready, 1)
                            wait(dve, hid_hi_ready, n + 1)
                            nc.vector.tensor_tensor(hid_lo[0:w, k, :], hid[0:w, 0, :],
                                                    hid_hi[0:w, k, :].bitcast(F32),
                                                    ALU.subtract).then_inc(hid_lo_ready, 1)
                        add(e, i, c, tb)
                dve.wait_ge(x_loaded, 16)
                pipeline(dve, NSH, U, [(0, split), (1, block_e)])

            @block.tensor
            def _(pe):
                def block_e(i, c):
                    e = U * i + c
                    wait(pe, w_lo_ready, 4 * (e + 1))
                    for tb in range(NTB):
                        toks = slice(tb * TBW, (tb + 1) * TBW)
                        for k, (f0, w) in enumerate(FCH):
                            n = NF * (NTB * e + tb) + k
                            s = (NF * tb + k) % 2
                            for ps, hi, lo, done, read in ((ps_g, g_hi, g_lo, g_done, silu_ready),
                                                           (ps_u, u_hi, u_lo, u_done, hid_ready)):
                                wait(pe, read, n - 1)
                                j = 0
                                for kc in range(KC):
                                    for a, b in ((hi, xt_hi), (lo, xt_hi), (hi, xt_lo)):
                                        last = nc.tensor.matmul(ps[s][0:w, :], a[:, c, kc, f0:f0 + w],
                                                                b[:, kc, toks], start=(j == 0),
                                                                stop=(j == 3 * KC - 1))
                                        j += 1
                                last.then_inc(done, 1)
                        wait(pe, hid_lo_ready, NF * (NTB * e + tb + 1))
                        for q in range(4):
                            t = 4 * tb + q
                            wait(pe, added, NT * e + t - 3)
                            j = 0
                            for k, (f0, w) in enumerate(FCH):
                                for a, b in ((hid_hi, d_hi), (hid_hi, d_lo), (hid_lo, d_hi)):
                                    last = nc.tensor.matmul(ps_y[q][:, :], a[0:w, k, q * P:(q + 1) * P],
                                                            b[0:w, c, k, :], start=(j == 0),
                                                            stop=(j == 3 * NF - 1))
                                    j += 1
                            last.then_inc(y_done, 1)
                pipeline(pe, NSH, U, [(0, block_e)])


def routed_phase(nc, ident, g_sb, u_sb, d_sb, slot_table, expert_of, xn_dram, work, out):
    with ExitStack() as ctx:
        sbuf, psum, sem = allocator(nc, ctx)
        U = 8
        R = 4
        NF = len(FCH)
        rows = sbuf("rows", [P, U], I32)
        xg = work[:, 0:R, :]
        y = work[:, R:2 * R, :]
        xg_t = work[:, 2 * R:3 * R, :].rearrange("p u (k t) -> p u k t", k=KC)
        silu = sbuf("silu_r", [P, R, F])
        hid = sbuf("hid_r", [P, R, F])
        hid_t = sbuf("hid_t", [P, R, NF, P])
        ps_t = psum("ps_xt", [P, KC, P])
        ps_g = [psum(f"ps_rg{n}", [P, TBW]) for n in range(2)]
        ps_u = [psum(f"ps_ru{n}", [P, TBW]) for n in range(2)]
        ps_h = psum("ps_ht", [P, NF, P])
        ps_y = [psum(f"ps_ry{n}", [P, D]) for n in range(2)]
        rows_ready = sem("rows_ready")
        gathered = [sem(f"gathered{n}") for n in range(R)]
        x_turned = sem("x_turned")
        x_ready = sem("x_ready")
        gu_done = sem("gu_done")
        silu_ready = sem("rsilu_ready")
        hid_ready = sem("rhid_ready")
        h_turned = sem("h_turned")
        h_ready = sem("h_ready")
        y_done = sem("ry_done")
        y_ready = sem("y_ready")
        scattered = sem("scattered")
        passed = sem("r_passed")

        with nc.Block() as block:
            @block.gpsimd
            def _(pool):
                def gather(i, c):
                    j = U * i + c
                    wait(pool, x_turned, j - R + 1)
                    wait(pool, rows_ready, j + 1)
                    pool.sem_inc(passed, 1)
                    nc.gpsimd.indirect_dma_start(
                        xg[:, c % R, :], None, xn_dram,
                        bass.IndirectOffsetOnAxis(rows[:, c:c + 1], 0)).then_inc(gathered[c % R], 16)

                def scatter(i, c):
                    j = U * i + c
                    wait(pool, scattered, 16 * j)
                    wait(pool, y_ready, j + 1)
                    pool.sem_inc(passed, 1)
                    nc.gpsimd.indirect_dma_start(
                        out, bass.IndirectOffsetOnAxis(rows[:, c:c + 1], 0), y[:, c % R, :], None,
                        compute_op=ALU.add).then_inc(scattered, 16)
                pipeline(pool, NST, U, [(0, gather), (3, scatter)])
                pool.wait_ge(scattered, 16 * NST)

            @block.scalar
            def _(act):
                def turn_x(i, c):
                    j = U * i + c
                    wait(act, x_turned, j + 1)
                    wait(act, gu_done, j - R + 1)
                    nc.scalar.activation(xg_t[:, c % R], ps_t[:, :, :], ACT.Copy).then_inc(x_ready, 1)

                def gate_unit(i, c):
                    j = U * i + c
                    wait(act, gu_done, j + 1)
                    wait(act, hid_ready, j - R + 1)
                    nc.scalar.activation(silu[:, c % R, :], ps_g[c % 2][:, 0:F], ACT.Silu
                                         ).then_inc(silu_ready, 1)
                pipeline(act, NST, U, [(0, turn_x), (1, gate_unit)], back=R)

            @block.vector
            def _(dve):
                def row_numbers(i, c):
                    j = U * i + c
                    wait(dve, scattered, 16 * (j - U + 1))
                    nc.vector.tensor_copy(rows[:, c:c + 1],
                                          slot_table[:, bass.ds(j, 1), 0].bitcast(I32)
                                          ).then_inc(rows_ready, 1)

                def hidden(i, c):
                    j = U * i + c
                    wait(dve, silu_ready, j + 1)
                    wait(dve, h_turned, j - R + 1)
                    nc.vector.tensor_tensor(hid[:, c % R, :], ps_u[c % 2][:, 0:F], silu[:, c % R, :],
                                            ALU.mult).then_inc(hid_ready, 1)

                def turn_h(i, c):
                    j = U * i + c
                    wait(dve, h_turned, j + 1)
                    wait(dve, y_done, j - R + 1)
                    nc.vector.tensor_copy(hid_t[:, c % R, 0:2, :], ps_h[:, 0:2, :]).then_inc(h_ready, 1)
                    w = FCH[-1][1]
                    nc.vector.tensor_copy(hid_t[0:w, c % R, 2, :], ps_h[0:w, 2, :]).then_inc(h_ready, 1)

                def weigh(i, c):
                    j = U * i + c
                    wait(dve, y_done, j + 1)
                    wait(dve, scattered, 16 * (j - R + 1))
                    nc.vector.tensor_scalar(y[:, c % R, :], ps_y[c % 2][:, :],
                                            slot_table[:, bass.ds(j, 1), 1], None,
                                            ALU.mult).then_inc(y_ready, 1)
                pipeline(dve, NST, U, [(0, row_numbers), (4, turn_h), (3, hidden), (4, weigh)], back=U)

            @block.tensor
            def _(pe):
                def turn_x(i, c):
                    j = U * i + c
                    wait(pe, gathered[c % R], 16 * (U // R * i + c // R + 1))
                    wait(pe, x_ready, j)
                    for k in range(KC):
                        last = nc.tensor.transpose(ps_t[:, k, :], xg[:, c % R, k * P:(k + 1) * P],
                                                   ident[:, :])
                    last.then_inc(x_turned, 1)

                def expert(j):
                    return pe.value_load(expert_of[0:1, bass.ds(j, 1)], min_val=0, max_val=E - 1)

                def gate_up(i, c):
                    j = U * i + c
                    e = expert(j)
                    wait(pe, x_ready, j + 1)
                    wait(pe, hid_ready, j - 1)
                    for ps, w in ((ps_g, g_sb), (ps_u, u_sb)):
                        for k in range(KC):
                            last = nc.tensor.matmul(
                                ps[c % 2][:, 0:F], xg_t[:, c % R, k, :],
                                w[:, bass.ds(e * KC + k, 1), :].rearrange("p a f -> p (a f)"),
                                start=(k == 0), stop=(k == KC - 1))
                    last.then_inc(gu_done, 1)

                def turn_h(i, c):
                    j = U * i + c
                    wait(pe, hid_ready, j + 1)
                    wait(pe, h_ready, 2 * j)
                    for k, (f0, w) in enumerate(FCH):
                        last = nc.tensor.transpose(ps_h[0:w, k, :], hid[:, c % R, f0:f0 + w], ident[:, :])
                    last.then_inc(h_turned, 1)

                def down(i, c):
                    j = U * i + c
                    e = expert(j)
                    wait(pe, h_ready, 2 * (j + 1))
                    wait(pe, y_ready, j - 1)
                    for k, (f0, w) in enumerate(FCH):
                        last = nc.tensor.matmul(
                            ps_y[c % 2][:, :], hid_t[0:w, c % R, k, :],
                            d_sb[0:w, bass.ds(e * NF + k, 1), :].rearrange("p a d -> p (a d)"),
                            start=(k == 0), stop=(k == NF - 1))
                    last.then_inc(y_done, 1)
                pipeline(pe, NST, U, [(2, turn_h), (0, turn_x), (1, gate_up), (2, down)], back=R)


def kernel(L0_attn_x, L0_attn_Wq, L0_attn_Wk, L0_attn_Wv, L0_attn_Wo, L0_ffn_router_weight,
           L0_ffn_e_score_correction_bias, L0_ffn_gate_w, L0_ffn_up_w, L0_ffn_down_w,
           L0_ffn_shared_gate_w, L0_ffn_shared_up_w, L0_ffn_shared_down_w):
    import numpy as np
    import concourse.bacc as bacc
    from concourse.bass_utils import run_bass_kernel_spmd

    def by_partition(w):
        return w.reshape(KC, P, -1).transpose(1, 0, 2)

    def columns(w):
        return w.reshape(KC, P, D // P, P).transpose(2, 1, 0, 3)

    def blocks_in(w):
        return w.reshape(-1, F, KC, P).transpose(0, 3, 2, 1)

    def pieces_in(w):
        return w.reshape(E, F, KC, P).transpose(0, 2, 3, 1).reshape(E * KC, P, F)

    a = {k: np.asarray(v) for k, v in dict(
        x=L0_attn_x, wq=L0_attn_Wq, wk=L0_attn_Wk, wv=L0_attn_Wv, wo=L0_attn_Wo,
        r=L0_ffn_router_weight, b=L0_ffn_e_score_correction_bias, g=L0_ffn_gate_w, u=L0_ffn_up_w,
        d=L0_ffn_down_w, sg=L0_ffn_shared_gate_w, su=L0_ffn_shared_up_w,
        sd=L0_ffn_shared_down_w).items()}
    arrays = {
        "x": a["x"].reshape(T, D),
        "wqk": np.concatenate([columns(a["wq"].T), columns(a["wk"].T)]),
        "wv": by_partition(a["wv"].T),
        "wo": by_partition(a["wo"].T),
        "router": by_partition(a["r"].T),
        "bias": a["b"],
        "gate": pieces_in(a["g"]),
        "up": pieces_in(a["u"]),
        "down": a["d"].transpose(0, 2, 1),
        "sgate": blocks_in(a["sg"]),
        "sup": blocks_in(a["su"]),
        "sdown": a["sd"].T.reshape(NSH, F, D),
    }
    arrays = {k: np.ascontiguousarray(v) for k, v in arrays.items()}
    nc = bacc.Bacc("TRN2", target_bir_lowering=False, num_devices=1)
    ins = [nc.dram_tensor(f"in_{k}", v.shape, mybir.dt.from_np(v.dtype), kind="ExternalInput").ap()
           for k, v in arrays.items()]
    out = nc.dram_tensor("out", [T + P, D], F32, kind="ExternalOutput").ap()
    moe_attention_kernel(nc, *ins, out)
    r = run_bass_kernel_spmd(nc, [{f"in_{k}": v for k, v in arrays.items()}], core_ids=[0])
    return r.results[0]["out"][:T].reshape(B, S, D)
```

```python
import concourse.bass as bass
from concourse import mybir
from contextlib import ExitStack

F32 = mybir.dt.float32
F32R = mybir.dt.float32r
BF16 = mybir.dt.bfloat16
I32 = mybir.dt.int32
ALU = mybir.AluOpType
ACT = mybir.ActivationFunctionType
AX = mybir.AxisListType

B, S, D = 2, 1024, 512
T = B * S
H, DK = 16, 32
P = 128
NT = T // P
KC = D // P
TBW = 512
NTB = T // TBW
E, F = 8, 352
NSH = 2
NST = (2 * T + E * (P - 1)) // P
NSLOT = NST * P
FCH = [(0, 128), (128, 128), (256, 96)]
NORM_SLOTS, YS = 4, 4
ROW_SLOTS, GS = 8, 4
EPS = 1e-5
ROUTE_SCALE = 2.5
SCALE = DK ** -0.5
MASKED = -1e30


def wait(eng, sem, value):
    if not (isinstance(value, int) and value <= 0):
        eng.wait_ge(sem, value)


def pipeline(eng, count, unroll, stages, back=0):
    deepest = max(lag for lag, _ in stages)
    first = max(1, -(-(deepest + back) // unroll))
    last = count // unroll

    def step(i, c):
        for lag, stage in stages:
            turn, at = divmod(c - lag, unroll)
            if isinstance(i, int):
                if 0 <= unroll * (i + turn) + at < count:
                    stage(i + turn, at)
            else:
                stage(i + turn, at)

    for i in range(min(first, last)):
        for c in range(unroll):
            step(i, c)
    if last > first:
        with eng.Fori(first, last) as i:
            for c in range(unroll):
                step(i, c)
    for c in range(count - unroll * last + deepest):
        step(last + c // unroll, c % unroll)


def moe_attention_kernel(nc, x, wqk, wv, wo, router, bias, gate, up, down, sgate, sup, sdown, out):
    qk_hi = nc.dram_tensor("qk_hi", [2 * D, T], F32, kind="Internal").ap()
    qk_lo = nc.dram_tensor("qk_lo", [2 * D, T], F32, kind="Internal").ap()
    v_dram = nc.dram_tensor("v_rows", [P, NT, H, 2 * DK], F32, kind="Internal").ap()
    row_dram = nc.dram_tensor("max_rows", [2 * H, S], F32, kind="Internal").ap()
    xn_dram = nc.dram_tensor("xn_rows", [T + P, D], F32, kind="Internal").ap()
    slots_dram = nc.dram_tensor("slots", [NSLOT, 2], F32, kind="Internal").ap()
    with ExitStack() as ctx:
        ident = ctx.enter_context(nc.sbuf_tensor("ident", [P, P], F32))
        slot_of = ctx.enter_context(nc.sbuf_tensor("slot_of", [P, NT, 2], I32))
        entry = ctx.enter_context(nc.sbuf_tensor("entry", [P, NT, 2, 2], F32))
        slot_table = ctx.enter_context(nc.sbuf_tensor("slot_table", [P, NST, 2], F32))
        expert_of = ctx.enter_context(nc.sbuf_tensor("expert_of", [P, NST], I32))
        work = ctx.enter_context(nc.sbuf_tensor("work", [P, NT, D], F32))
        r_hi = ctx.enter_context(nc.sbuf_tensor("r_hi", [P, KC, E], F32R))
        r_lo = ctx.enter_context(nc.sbuf_tensor("r_lo", [P, KC, E], F32R))

        def counters(name, n):
            return [ctx.enter_context(nc.semaphore(f"{name}{k}")) for k in range(n)]
        v_stored = counters("v_stored", NORM_SLOTS)
        xn_stored = counters("xn_stored", NORM_SLOTS)
        zeros_stored, out_stored = counters("edge_stored", 2)
        qk_stored = counters("qk_stored", 2)
        y_stored = counters("y_stored", YS)
        rows = ctx.enter_context(nc.sbuf_tensor("rows", [P, ROW_SLOTS], I32))
        rows_ready, down_loaded = counters("routed_input", 2)
        gathered = counters("gathered", GS)
        with nc.sbuf_tensor("xt_hi", [P, KC, T], F32R) as xt_hi, \
                nc.sbuf_tensor("xt_lo", [P, KC, T], F32R) as xt_lo:
            norm_phase(nc, x, wv, xt_hi, xt_lo, ident, v_dram, xn_dram, out, work, v_stored,
                       xn_stored, zeros_stored, router, r_hi, r_lo)
            with nc.sbuf_tensor("chosen", [P, NT, E], F32) as chosen, \
                    nc.sbuf_tensor("weight", [P, NT, E], F32) as weight, \
                    nc.sbuf_tensor("earlier_of", [P, NT, E], F32) as earlier_of, \
                    nc.sbuf_tensor("count_of", [P, 1, E], F32) as count_of, \
                    ExitStack() as weights_ctx:
                shared_w = []
                for name, chunks, width in (("sg", KC, F), ("su", KC, F), ("sd", len(FCH), D)):
                    shared_w.append(tuple(
                        weights_ctx.enter_context(nc.sbuf_tensor(name + part, shape, dt))
                        for part, shape, dt in (("_raw", [P, chunks, width], F32),
                                                ("_hi", [P, NSH, chunks, width], F32R),
                                                ("_lo", [P, NSH, chunks, width], F32R))))
                project_phase(nc, wqk, r_hi, r_lo, bias, xt_hi, xt_lo, ident, chosen, weight,
                              earlier_of, count_of, shared_w, sgate, sup, sdown, qk_hi, qk_lo, work,
                              v_stored + xn_stored, zeros_stored, qk_stored)
                shared_phase(nc, x, sgate, sup, sdown, shared_w, xt_hi, xt_lo, chosen, weight,
                             earlier_of, count_of, slot_of, entry, slot_table, expert_of,
                             slots_dram, out, work, qk_stored, out_stored)
        gu_sb = ctx.enter_context(nc.sbuf_tensor("gu_sb", [P, E * KC, 2 * F], F32))
        attend_phase(nc, ident, qk_hi, qk_lo, v_dram, row_dram, gate, up, gu_sb, work,
                     out_stored)
        with nc.sbuf_tensor("d_sb", [P, E * len(FCH), D], F32) as d_sb, \
                nc.sbuf_tensor("y_tile", [P, YS, D], F32) as y_tile:
            out_phase(nc, wo, down, ident, work, d_sb, out, y_tile, y_stored, slot_table, rows,
                      rows_ready, xn_dram, gathered, down_loaded)
            routed_phase(nc, ident, gu_sb, d_sb, slot_table, expert_of, xn_dram, work, out,
                         y_stored, rows, rows_ready, gathered, down_loaded)


def allocator(nc, ctx):
    def sbuf(name, shape, dt=F32):
        return ctx.enter_context(nc.sbuf_tensor(name, shape, dt))

    def psum(name, shape):
        return ctx.enter_context(nc.psum_tensor(name, shape, F32))

    def sem(name):
        return ctx.enter_context(nc.semaphore(name))
    return sbuf, psum, sem


def load_shared_block(sp, e, shared_w, gate, up, down, loaded):
    for (raw, _, _), src in zip(shared_w, (gate, up)):
        sp.dma_start(raw[:, :, :], src[e]).then_inc(loaded, 16)
    raw = shared_w[2][0]
    sp.dma_start(raw[:, 0:2, :], down[e, 0:2 * P, :].rearrange("(k p) d -> p k d", p=P)
                 ).then_inc(loaded, 16)
    sp.dma_start(raw[0:FCH[-1][1], 2, :], down[e, 2 * P:F, :]).then_inc(loaded, 16)


def shared_parts(shared_w, e):
    for raw, hi, lo in shared_w[:2]:
        yield raw[:, :, :], hi[:, e], lo[:, e]
    raw, hi, lo = shared_w[2]
    w = FCH[-1][1]
    yield raw[:, 0:2, :], hi[:, e, 0:2], lo[:, e, 0:2]
    yield raw[0:w, 2, :], hi[0:w, e, 2], lo[0:w, e, 2]


def norm_phase(nc, x, wv, xt_hi, xt_lo, ident, v_dram, xn_dram, out, work, v_stored,
               xn_stored, zeros_stored, router, r_hi, r_lo):
    with ExitStack() as ctx:
        sbuf, psum, sem = allocator(nc, ctx)
        U = NORM_SLOTS
        x_tile = sbuf("x_tile", [P, U, D])
        stats = sbuf("stats", [P, U, 6])
        moments = sbuf("moments", [P, U, 2])
        var_eps = sbuf("var_eps", [P, U])
        std = sbuf("std", [P, U])
        rstd = sbuf("rstd", [P, U])
        v_rows = U * H * 2 * DK // D
        xn = work[:, v_rows:v_rows + U, :]
        zeros = work[:, v_rows + U, :]
        tile_hi = sbuf("tile_hi", [P, U, KC, P], F32R)
        tile_lo = sbuf("tile_lo", [P, U, KC, P], F32R)
        wv_raw = sbuf("wv_raw", [P, KC, D])
        r_raw = sbuf("r_raw", [P, KC, E])
        wv_hi = sbuf("wv_hi", [P, KC, D], F32R)
        wv_lo = sbuf("wv_lo", [P, KC, D], F32R)
        v_stage = work[:, 0:v_rows, :].bitcast(F32R).rearrange(
            "p (u a) (h d) -> p u (a h) d", u=U, d=2 * DK)
        ps_t = [psum(f"ps_t{n}", [P, KC, P]) for n in range(U)]
        ps_v = [psum(f"ps_v{n}", [P, D]) for n in range(U)]
        x_loaded = [sem(f"x_loaded{n}") for n in range(U)]
        hi_saved = sem("hi_saved")
        lo_saved = sem("lo_saved")
        wv_loaded = sem("wv_loaded")
        wv_hi_ready = sem("wv_hi_ready")
        wv_lo_ready = sem("wv_lo_ready")
        ident_zeroed = sem("ident_zeroed")
        ident_ready = sem("ident_ready")
        stats_ready = sem("stats_ready")
        moments_ready = sem("moments_ready")
        var_ready = sem("var_ready")
        std_ready = sem("std_ready")
        rstd_ready = sem("rstd_ready")
        xn_ready = sem("xn_ready")
        transposed = sem("transposed")
        hi_ready = sem("hi_ready")
        lo_ready = sem("lo_ready")
        v_done = sem("v_done")
        r_loaded = sem("r_loaded")
        r_hi_ready = sem("r_hi_ready")
        r_lo_ready = sem("r_lo_ready")
        v_hi_ready = sem("v_hi_ready")
        v_lo_ready = sem("v_lo_ready")
        passed = sem("passed")
        zeros_ready = sem("zeros_ready")

        with nc.Block() as block:
            @block.sync
            def _(sp):
                def load(i, c):
                    t = U * i + c
                    if isinstance(i, int) and i == 0 and c == U - 1:
                        sp.dma_start(wv_raw[:, :, :], wv).then_inc(wv_loaded, 16)
                    wait(sp, xn_ready, t - U + 1)
                    sp.dma_start(x_tile[:, c, :], x[bass.ds(t * P, P), :]).then_inc(x_loaded[c], 16)

                def store_xn(i, c):
                    t = U * i + c
                    wait(sp, xn_ready, t + 1)
                    sp.dma_start(xn_dram[bass.ds(t * P, P), :], xn[:, c, :]).then_inc(xn_stored[c], 16)

                def store_v(i, c):
                    t = U * i + c
                    wait(sp, v_lo_ready, t + 1)
                    sp.dma_start(v_dram[:, bass.ds(t, 1)].rearrange("p a h d -> p (a h) d"),
                                 v_stage[:, c].bitcast(F32)).then_inc(v_stored[c], 16)

                def store_zeros(i, c):
                    if isinstance(i, int) and i == 1 and c == 0:
                        sp.wait_ge(zeros_ready, 1)
                        sp.dma_start(xn_dram[T:, :], zeros).then_inc(zeros_stored, 16)
                        sp.dma_start(out[T:, :], zeros).then_inc(zeros_stored, 16)
                        sp.dma_start(r_raw[:, :, :], router).then_inc(r_loaded, 16)

                pipeline(sp, NT, U, [(0, load), (0, store_zeros), (3, store_xn), (5, store_v)])

            @block.gpsimd
            def _(pool):
                nc.gpsimd.memset(ident[:, :], 0.0).then_inc(ident_zeroed, 1)
                pool.wait_ge(ident_zeroed, 1)
                nc.gpsimd.affine_select(out=ident[:, :], in_=ident[:, :], compare_op=ALU.not_equal,
                                        fill=1.0, base=0, pattern=[[-1, P]],
                                        channel_multiplier=1).then_inc(ident_ready, 1)

            @block.vector
            def _(dve):
                def statistics(i, c):
                    wait(dve, x_loaded[c], 16 * (i + 1))
                    nc.vector.bn_stats(stats[:, c, :], x_tile[:, c, :]).then_inc(stats_ready, 1)

                def mean_and_variance(i, c):
                    t = U * i + c
                    wait(dve, stats_ready, t + 1)
                    dve.sem_inc(passed, 1)
                    nc.vector.bn_aggr(moments[:, c, :], stats[:, c, :]).then_inc(moments_ready, 1)

                def add_eps(i, c):
                    t = U * i + c
                    wait(dve, moments_ready, t + 1)
                    nc.vector.tensor_scalar(var_eps[:, c:c + 1], moments[:, c, 1:2], EPS, None,
                                            ALU.add).then_inc(var_ready, 1)

                def invert(i, c):
                    t = U * i + c
                    wait(dve, std_ready, t + 1)
                    nc.vector.reciprocal(rstd[:, c:c + 1], std[:, c:c + 1]).then_inc(rstd_ready, 1)

                def scale(i, c):
                    t = U * i + c
                    wait(dve, rstd_ready, t + 1)
                    wait(dve, transposed, t - U + 1)
                    wait(dve, xn_stored[c], 16 * i)
                    nc.vector.tensor_scalar(xn[:, c, :], x_tile[:, c, :], moments[:, c, 0:1],
                                            rstd[:, c:c + 1], ALU.subtract,
                                            ALU.mult).then_inc(xn_ready, 1)

                def lo(i, c):
                    t = U * i + c
                    wait(dve, hi_ready, t + 1)
                    wait(dve, v_done, t - U + 1)
                    wait(dve, lo_saved, t - U + 1)
                    nc.vector.tensor_tensor(tile_lo[:, c], ps_t[c][:, :, :], tile_hi[:, c].bitcast(F32),
                                            ALU.subtract).then_inc(lo_ready, 1)

                def save_lo(i, c):
                    t = U * i + c
                    wait(dve, lo_ready, t + 1)
                    nc.vector.tensor_copy(xt_lo[:, :, bass.ds(t * P, P)], tile_lo[:, c]
                                          ).then_inc(lo_saved, 1)

                def v_lo(i, c):
                    t = U * i + c
                    wait(dve, v_hi_ready, t + 1)
                    v = v_stage[:, c]
                    nc.vector.tensor_tensor(v[:, :, DK:], ps_v[c][:, :].rearrange("p (h d) -> p h d", h=H),
                                            v[:, :, 0:DK].bitcast(F32),
                                            ALU.subtract).then_inc(v_lo_ready, 1)

                nc.vector.memset(zeros, 0.0).then_inc(zeros_ready, 1)
                def split_wv(i, c):
                    if isinstance(i, int) and i == 0 and c == 0:
                        dve.wait_ge(wv_hi_ready, 1)
                        nc.vector.tensor_tensor(wv_lo[:, :, :], wv_raw[:, :, :],
                                                wv_hi[:, :, :].bitcast(F32),
                                                ALU.subtract).then_inc(wv_lo_ready, 1)

                pipeline(dve, NT, U, [
                    (1, invert), (0, statistics), (1, scale), (2, lo), (0, mean_and_variance),
                    (2, split_wv), (4, v_lo), (0, add_eps), (2, save_lo)], back=U)

                dve.wait_ge(r_hi_ready, 1)
                nc.vector.tensor_tensor(r_lo[:, :, :], r_raw[:, :, :], r_hi[:, :, :].bitcast(F32),
                                        ALU.subtract).then_inc(r_lo_ready, 1)

            @block.scalar
            def _(act):
                def split_wv(i, c):
                    if isinstance(i, int) and i == 0 and c == 0:
                        act.wait_ge(wv_loaded, 16)
                        nc.scalar.activation(wv_hi[:, :, :], wv_raw[:, :, :],
                                             ACT.Copy).then_inc(wv_hi_ready, 1)

                def root(i, c):
                    t = U * i + c
                    wait(act, var_ready, t + 1)
                    nc.scalar.activation(std[:, c:c + 1], var_eps[:, c:c + 1],
                                         ACT.Sqrt).then_inc(std_ready, 1)

                def hi(i, c):
                    t = U * i + c
                    wait(act, transposed, t + 1)
                    wait(act, v_done, t - U + 1)
                    wait(act, hi_saved, t - U + 1)
                    nc.scalar.activation(tile_hi[:, c], ps_t[c][:, :, :], ACT.Copy).then_inc(hi_ready, 1)

                def save_hi(i, c):
                    t = U * i + c
                    wait(act, hi_ready, t + 1)
                    nc.scalar.activation(xt_hi[:, :, bass.ds(t * P, P)], tile_hi[:, c],
                                         ACT.Copy).then_inc(hi_saved, 1)

                def v_hi(i, c):
                    t = U * i + c
                    wait(act, v_done, t + 1)
                    wait(act, v_stored[c], 16 * i)
                    nc.scalar.activation(v_stage[:, c, :, 0:DK],
                                         ps_v[c][:, :].rearrange("p (h d) -> p h d", h=H),
                                         ACT.Copy).then_inc(v_hi_ready, 1)

                pipeline(act, NT, U, [(0, root), (1, hi), (1, split_wv), (1, save_hi), (3, v_hi)])
                act.wait_ge(r_loaded, 16)
                nc.scalar.activation(r_hi[:, :, :], r_raw[:, :, :], ACT.Copy).then_inc(r_hi_ready, 1)

            @block.tensor
            def _(pe):
                pe.wait_ge(ident_ready, 1)

                def transpose(i, c):
                    t = U * i + c
                    wait(pe, xn_ready, t + 1)
                    wait(pe, lo_ready, t - U + 1)
                    for k in range(KC):
                        last = nc.tensor.transpose(ps_t[c][:, k, :], xn[:, c, k * P:(k + 1) * P],
                                                   ident[:, :])
                    last.then_inc(transposed, 1)

                def multiply(i, c):
                    t = U * i + c
                    wait(pe, lo_ready, t + 1)
                    wait(pe, v_lo_ready, t - U + 1)
                    n = 0
                    for k in range(KC):
                        for a, b in ((tile_hi, wv_hi), (tile_hi, wv_lo), (tile_lo, wv_hi)):
                            last = nc.tensor.matmul(ps_v[c][:, :], a[:, c, k, :], b[:, k, :],
                                                    start=(n == 0), stop=(n == 3 * KC - 1))
                            n += 1
                    last.then_inc(v_done, 1)

                def first_multiply(i, c):
                    if isinstance(i, int) and i == 0 and c == 0:
                        pe.wait_ge(wv_lo_ready, 1)
                    multiply(i, c)

                pipeline(pe, NT, U, [(0, transpose), (1, first_multiply)])


def project_phase(nc, wqk, r_hi, r_lo, bias, xt_hi, xt_lo, ident, chosen, weight, earlier_of, count_of,
                  shared_w, sgate, sup, sdown, qk_hi, qk_lo, work, norm_stored, zeros_stored,
                  qk_stored):
    with ExitStack() as ctx:
        sbuf, psum, sem = allocator(nc, ctx)
        U = 2
        CH = 2 * D // P
        w_raw = sbuf("w_raw", [P, U, KC, P])
        w_hi = sbuf("w_hi", [P, U, KC, P], F32R)
        w_lo = sbuf("w_lo", [P, U, KC, P], F32R)
        stage_hi, stage_lo = [
            work[:, n * NT // 2:(n + 1) * NT // 2, :].bitcast(F32R).rearrange(
                "p (u a) d -> p u (a d)", u=U) for n in range(2)]
        logits_t = stage_lo[0:E, U - 1, :].bitcast(F32)
        bias_b = sbuf("bias_b", [P, 1, E])
        score = sbuf("score", [P, NT, E])
        biased = sbuf("biased", [P, NT, E])
        G = E // 2
        group = sbuf("group", [P, NT, G])
        beats = sbuf("beats", [P, NT, E])
        rank = sbuf("rank", [P, NT, E])
        lead = sbuf("lead", [P, NT, E])
        total = sbuf("total", [P, NT])
        chosen_bf = sbuf("chosen_bf", [P, NT, E], BF16)
        earlier = sbuf("earlier", [P, P], BF16)
        ones = sbuf("ones", [P, P], BF16)
        ps_q = [psum(f"ps_q{n}", [P, TBW]) for n in range(NTB)]
        ps_r = psum("ps_r", [P, TBW])
        ps_s = psum("ps_s", [P, NT, E])
        ps_rank = psum("ps_rank", [P, NT, E])
        ps_count = psum("ps_count", [P, 1, E])
        w_loaded = [sem(f"w_loaded{n}") for n in range(U)]
        stored = qk_stored
        bias_loaded = sem("bias_loaded")
        logits_done = sem("logits_done")
        logits_copied = sem("logits_copied")
        logits_turned = sem("logits_turned")
        score_ready = sem("score_ready")
        w_hi_ready = sem("w_hi_ready")
        w_lo_ready = sem("w_lo_ready")
        q_done = sem("q_done")
        q_hi_ready = sem("q_hi_ready")
        q_lo_ready = sem("q_lo_ready")
        routing = sem("routing")
        weighing = sem("weighing")
        shared_loaded = sem("shared_loaded")
        shared_hi_ready = sem("shared_hi_ready")
        shared_lo_ready = sem("shared_lo_ready")
        ones_ready = sem("ones_ready")
        earlier_ready = sem("earlier_ready")
        chosen_ready = sem("chosen_ready")
        ranks_done = sem("ranks_done")

        with nc.Block() as block:
            @block.sync
            def _(sp):
                sp.dma_start(bias_b[:, 0, :], bias.rearrange("(a e) -> a e", a=1)
                             .broadcast_to([P, E])).then_inc(bias_loaded, 16)

                def load(i, c):
                    t = U * i + c
                    wait(sp, w_lo_ready, t - U + 1)
                    sp.dma_start(w_raw[:, c], wqk[bass.ds(t, 1)].rearrange("a p k m -> (a p) k m")
                                 ).then_inc(w_loaded[c], 16)

                def store(i, c):
                    t = U * i + c
                    wait(sp, q_lo_ready, NTB * (t + 1))
                    sp.dma_start(qk_hi[bass.ds(t * P, P), :], stage_hi[:, c].bitcast(F32)
                                 ).then_inc(stored[c], 16)
                    sp.dma_start(qk_lo[bass.ds(t * P, P), :], stage_lo[:, c].bitcast(F32)
                                 ).then_inc(stored[c], 16)

                def load_shared(i, c):
                    if isinstance(i, int) and i == 0 and c == U - 1:
                        load_shared_block(sp, 0, shared_w, sgate, sup, sdown, shared_loaded)

                pipeline(sp, CH, U, [(0, load), (0, load_shared), (2, store)])

            @block.scalar
            def _(act):
                act.wait_ge(zeros_stored, 32)
                for slot_stored in norm_stored:
                    act.wait_ge(slot_stored, 16 * (NT // NORM_SLOTS))
                for n in range(NTB):
                    act.wait_ge(logits_done, n + 1)
                    nc.scalar.activation(logits_t[:, n * TBW:(n + 1) * TBW], ps_r[0:E, :],
                                         ACT.Copy).then_inc(logits_copied, 1)
                act.wait_ge(logits_turned, 1)
                nc.scalar.activation(score[:, :, :], ps_s[:, :, :], ACT.Sigmoid).then_inc(score_ready, 1)

                def split(i, c):
                    t = U * i + c
                    wait(act, w_loaded[c], 16 * (i + 1))
                    wait(act, q_done, NTB * (t - U + 1))
                    nc.scalar.activation(w_hi[:, c], w_raw[:, c], ACT.Copy).then_inc(w_hi_ready, 1)

                def evacuate(i, c):
                    t = U * i + c
                    wait(act, stored[c], 32 * i)
                    for n in range(NTB):
                        wait(act, q_done, NTB * t + n + 1)
                        nc.scalar.activation(stage_hi[:, c, n * TBW:(n + 1) * TBW], ps_q[n][:, :],
                                             ACT.Copy).then_inc(q_hi_ready, 1)

                pipeline(act, CH, U, [(0, split), (1, evacuate)])

            @block.tensor
            def _(pe):
                for n in range(NTB):
                    pe.wait_ge(logits_copied, n) if n else None
                    j = 0
                    for k in range(KC):
                        for a, b in ((r_hi, xt_hi), (r_lo, xt_hi), (r_hi, xt_lo)):
                            last = nc.tensor.matmul(ps_r[0:E, :], a[:, k, :],
                                                    b[:, k, n * TBW:(n + 1) * TBW],
                                                    start=(j == 0), stop=(j == 3 * KC - 1))
                            j += 1
                    last.then_inc(logits_done, 1)
                pe.wait_ge(logits_copied, NTB)
                for t in range(NT):
                    last = nc.tensor.transpose(ps_s[:, t, :], logits_t[:, t * P:(t + 1) * P],
                                               ident[0:E, 0:E])
                last.then_inc(logits_turned, 1)

                def multiply(i, c):
                    t = U * i + c
                    wait(pe, w_lo_ready, t + 1)
                    for n in range(NTB):
                        wait(pe, q_lo_ready, NTB * (t - 1) + n + 1)
                        j = 0
                        for k in range(KC):
                            for a, b in ((w_hi, xt_hi), (w_lo, xt_hi), (w_hi, xt_lo)):
                                last = nc.tensor.matmul(ps_q[n][:, :], a[:, c, k, :],
                                                        b[:, k, n * TBW:(n + 1) * TBW],
                                                        start=(j == 0), stop=(j == 3 * KC - 1))
                                j += 1
                        last.then_inc(q_done, 1)

                pipeline(pe, CH, U, [(0, multiply)])

                pe.wait_ge(chosen_ready, 1)
                pe.wait_ge(earlier_ready, 1)
                nc.tensor.matmul(ps_rank[:, :, :], earlier[:, :], chosen_bf[:, :, :], start=True,
                                 stop=False)
                for t in range(NT - 1):
                    later = NT - 1 - t
                    nc.tensor.matmul(ps_rank[:, t + 1:, :], ones[:, :],
                                     chosen_bf[:, t:t + 1, :].broadcast_to([P, later, E]),
                                     start=False, stop=(t == NT - 2))
                for t in range(NT):
                    last = nc.tensor.matmul(ps_count[:, :, :], ones[:, :], chosen_bf[:, t:t + 1, :],
                                            start=(t == 0), stop=(t == NT - 1))
                last.then_inc(ranks_done, 1)

            @block.gpsimd
            def _(pool):
                nc.gpsimd.memset(ones[:, :], 1.0).then_inc(ones_ready, 1)
                pool.wait_ge(ones_ready, 1)
                nc.gpsimd.affine_select(out=earlier[:, :], in_=ones[:, :], compare_op=ALU.is_gt,
                                        fill=0.0, base=0, pattern=[[1, P]],
                                        channel_multiplier=-1).then_inc(earlier_ready, 1)
                steps = [0]

                def then(instruction):
                    steps[0] += 1
                    instruction.then_inc(routing, 1)
                    pool.wait_ge(routing, steps[0])

                def top2(value, n, flag):
                    then(nc.gpsimd.memset(rank[:, :, 0:n], 0.0))
                    for e in range(n):
                        then(nc.gpsimd.tensor_tensor(
                            lead[:, :, 0:n], value[:, :, e:e + 1].broadcast_to([P, NT, n]),
                            value[:, :, 0:n], ALU.subtract))
                        if e:
                            then(nc.gpsimd.tensor_scalar(beats[:, :, 0:e], lead[:, :, 0:e], 0.0, None,
                                                         ALU.is_gt))
                        then(nc.gpsimd.tensor_scalar(beats[:, :, e:n], lead[:, :, e:n], 0.0, None,
                                                     ALU.is_ge))
                        then(nc.gpsimd.tensor_tensor(rank[:, :, 0:n], rank[:, :, 0:n],
                                                     beats[:, :, 0:n], ALU.add))
                    then(nc.gpsimd.tensor_scalar(flag, rank[:, :, 0:n], 3.0, None, ALU.is_lt))

                pool.wait_ge(score_ready, 1)
                pool.wait_ge(bias_loaded, 16)
                then(nc.gpsimd.tensor_tensor(biased[:, :, :], score[:, :, :],
                                             bias_b[:, :, :].broadcast_to([P, NT, E]), ALU.add))
                pairs = biased[:, :, :].rearrange("p t (g j) -> p t g j", j=2)
                then(nc.gpsimd.tensor_tensor(group[:, :, :], pairs[:, :, :, 0], pairs[:, :, :, 1],
                                             ALU.add))
                top2(group, G, group[:, :, :])
                for j in range(2):
                    then(nc.gpsimd.tensor_tensor(pairs[:, :, :, j], pairs[:, :, :, j],
                                                 group[:, :, :], ALU.mult))
                top2(biased, E, chosen[:, :, :])
                nc.gpsimd.tensor_copy(chosen_bf[:, :, :], chosen[:, :, :]).then_inc(chosen_ready, 1)

                pool.wait_ge(shared_loaded, 64)
                for n, (raw, hi, lo) in enumerate(shared_parts(shared_w, 0)):
                    nc.gpsimd.tensor_copy(hi, raw).then_inc(shared_hi_ready, 1)
                    pool.wait_ge(shared_hi_ready, n + 1)
                    nc.gpsimd.tensor_tensor(lo, raw, hi.bitcast(F32),
                                            ALU.subtract).then_inc(shared_lo_ready, 1)

            @block.vector
            def _(dve):
                def split(i, c):
                    t = U * i + c
                    wait(dve, w_hi_ready, t + 1)
                    nc.vector.tensor_tensor(w_lo[:, c], w_raw[:, c], w_hi[:, c].bitcast(F32),
                                            ALU.subtract).then_inc(w_lo_ready, 1)

                def evacuate(i, c):
                    t = U * i + c
                    for n in range(NTB):
                        cols = slice(n * TBW, (n + 1) * TBW)
                        wait(dve, q_hi_ready, NTB * t + n + 1)
                        nc.vector.tensor_tensor(stage_lo[:, c, cols], ps_q[n][:, :],
                                                stage_hi[:, c, cols].bitcast(F32),
                                                ALU.subtract).then_inc(q_lo_ready, 1)

                pipeline(dve, CH, U, [(0, split), (1, evacuate)])

                steps = [0]

                def then(instruction):
                    steps[0] += 1
                    instruction.then_inc(weighing, 1)
                    dve.wait_ge(weighing, steps[0])

                dve.wait_ge(chosen_ready, 1)
                then(nc.vector.tensor_tensor(weight[:, :, :], chosen[:, :, :], score[:, :, :],
                                             ALU.mult))
                then(nc.vector.reduce_sum(total[:, :], weight[:, :, :], AX.X))
                then(nc.vector.tensor_scalar(total[:, :], total[:, :], 1e-20, None, ALU.add))
                then(nc.vector.reciprocal(total[:, :], total[:, :]))
                then(nc.vector.tensor_scalar(total[:, :], total[:, :], ROUTE_SCALE, None, ALU.mult))
                then(nc.vector.tensor_tensor(
                    weight[:, :, :], weight[:, :, :],
                    total[:, :].rearrange("p (t a) -> p t a", a=1).broadcast_to([P, NT, E]), ALU.mult))
                dve.wait_ge(ranks_done, 1)
                then(nc.vector.tensor_copy(earlier_of[:, :, :], ps_rank[:, :, :]))
                then(nc.vector.tensor_copy(count_of[:, :, :], ps_count[:, :, :]))


def attend_phase(nc, ident, q_hi, q_lo, v_dram, row_dram, gate, up, gu_sb, attended,
                 out_stored):
    HS = 4
    NB = 12
    U = HS * NB
    STEPS = B * H * NB
    QT = S // P
    ROWS = 3 * DK
    VW = 2 * DK + 2
    BLOCKS = [
        (0, 0), (1, 0), (0, 3), (1, 6), (1, 4), (1, 3), (0, 1), (0, 2), (1, 2), (1, 7), (1, 1),
        (1, 5)]
    PIECES = [(t, k0, min(TBW, P * (t + 1) - k0)) for t, k0 in (
        (6, 0), (5, 0), (6, TBW), (7, 0), (7, TBW), (2, 0), (4, 0), (3, 0), (1, 0), (0, 0),
        (4, TBW), (5, TBW))]
    AHEAD = 2 * NB
    LO_POOL = [0, 1, 2, 3, 4, 5, 7, 8, 9, 11]
    LO_DVE = [n for n in range(NB) if n not in LO_POOL]
    HI_DVE = [6, 11]
    HI_ACT = [n for n in range(NB) if n not in HI_DVE]
    EXP, HI, LO, VALUE = AHEAD + 1, AHEAD + 2, AHEAD + 4, AHEAD + 8
    COPY, TURN, NORM = AHEAD + 8, AHEAD + 10, AHEAD + 11
    ROW = NB + 1
    ROW_LATER = 1
    STARTS = [min(n for n in range(NB) if BLOCKS[n][0] == half) for half in range(2)]
    ENDS = [max(n for n in range(NB) if BLOCKS[n][0] == half) for half in range(2)]
    assert all(BLOCKS[n][1] == 0 for n in STARTS) and ENDS[1] == NB - 1
    ROWS_BEFORE = {n: (n + TURN - ROW - ROW_LATER) // NB + 1 for n in ENDS}
    TURNS_BEFORE = sum((ROW - n - TURN - 1 + ROW_LATER) // NB + 1 for n in ENDS)
    DIAGONAL = [n for n, (qb, kt) in enumerate(BLOCKS) if kt >= 4 * qb]

    def span(n):
        qb, kt = BLOCKS[n]
        first = max(0, (kt - 4 * qb) * P)
        return first, TBW - first

    def count(of, i, c):
        return len(of) * (HS * i + c // NB) + sum(n <= c % NB for n in of)

    with ExitStack() as ctx:
        sbuf, psum, sem = allocator(nc, ctx)
        qs = sbuf("qs", [P, HS, S], F32R)
        ks = sbuf("ks", [P, HS, S], F32R)
        vs = sbuf("vs", [P, HS, QT, VW], F32R)
        late = sbuf("late", [P, P], BF16)
        eye = sbuf("eye", [P, P], BF16)
        maxima = sbuf("maxima", [P, HS, QT + 4])
        row_stage = sbuf("row_stage", [QT, HS, P], F32R)
        NP = 6
        prob = sbuf("prob", [P, NP, TBW])
        prob_hi = sbuf("prob_hi", [P, NP, TBW], F32R)
        prob_lo = sbuf("prob_lo", [P, NP, TBW], F32R)
        o_copy = sbuf("o_copy", [VW, 2, TBW])
        o_part = sbuf("o_part", [P, 4, DK])
        o_sum = sbuf("o_sum", [P, 4, DK])
        o_inv = sbuf("o_inv", [P, 4, 1])
        NM = 3
        ps_m = [psum(f"ps_m{n}", [P, TBW]) for n in range(NM)]
        NS = 2
        ps_s = [psum(f"ps_s{n}", [P, TBW]) for n in range(NS)]
        ps_o = [psum(f"ps_o{n}", [P, TBW]) for n in range(2)]
        ps_x = psum("ps_x", [P, TBW])
        ps_ot = ps_x[:, 0:4 * VW].rearrange("p (q w) -> p q w", q=4)
        ps_row = ps_x[:, TBW - P:]
        head_loaded = [sem(f"head_loaded{n}") for n in range(HS)]
        values_loaded = [sem(f"values_loaded{n}") for n in range(HS)]
        row_saved = [sem(f"row_saved{n}") for n in range(HS)]
        row_loaded = [sem(f"row_loaded{n}") for n in range(HS)]
        consts_ready = sem("consts_ready")
        consts_zeroed = sem("consts_zeroed")
        experts_loaded = sem("experts_loaded")
        m_done = sem("m_done")
        m_read = sem("m_read")
        max_ready = sem("max_ready")
        row_turned = sem("row_turned")
        row_ready = sem("row_ready")
        s_done = sem("s_done")
        exp_done = sem("exp_done")
        hi_act = sem("hi_act")
        hi_dve = sem("hi_dve")
        lo_dve = sem("lo_dve")
        lo_pool = sem("lo_pool")
        pv_done = sem("pv_done")
        o_copied = sem("o_copied")
        o_turned = sem("o_turned")
        part_ready = sem("part_ready")
        sum_ready = sem("sum_ready")
        inv_ready = sem("inv_ready")
        o_ready = sem("o_ready")

        def wait_hi(eng, i, c):
            if c % NB in HI_DVE:
                wait(eng, hi_dve, count(HI_DVE, i, c))
            else:
                wait(eng, hi_act, count(HI_ACT, i, c))

        with nc.Block() as block:
            @block.sync
            def _(sp):
                def load_head(i, c):
                    h, b = 2 * i + c // 2, c % 2
                    wait(sp, s_done, NB * (HS * (i - 1) + c + 1))
                    sp_cols = slice(b * S, (b + 1) * S)
                    for n, (q_src, k_src) in enumerate(((q_hi, q_hi), (q_hi, q_lo), (q_lo, q_hi))):
                        rows = slice(n * DK, (n + 1) * DK)
                        sp.dma_start(qs[rows, c, :].bitcast(F32), q_src[bass.ds(h * DK, DK), sp_cols]
                                     ).then_inc(head_loaded[c], 16)
                        sp.dma_start(ks[rows, c, :].bitcast(F32), k_src[bass.ds(D + h * DK, DK), sp_cols]
                                     ).then_inc(head_loaded[c], 16)

                def load_values(i, c):
                    h, b = 2 * i + c // 2, c % 2
                    wait(sp, pv_done, NB * (HS * (i - 1) + c + 1))
                    sp.dma_start(vs[:, c, :, 0:2 * DK].bitcast(F32),
                                 v_dram[:, b * QT:(b + 1) * QT, bass.ds(h, 1), :]
                                 .rearrange("p t h d -> p (t h) d")).then_inc(values_loaded[c], 16)

                def load_experts(i, c):
                    g = HS * i + c
                    for n, src in enumerate((gate, up)):
                        sp.dma_start(gu_sb[:, bass.ds(g, 1), n * F:(n + 1) * F], src[bass.ds(g, 1)]
                                     .rearrange("a p f -> p a f")).then_inc(experts_loaded, 16)

                pipeline(sp, B * H, HS, [(0, load_head), (1, load_values), (1, load_experts)])
                assert E * KC == B * H
                sp.wait_ge(experts_loaded, 32 * E * KC)

            @block.gpsimd
            def _(pool):
                nc.gpsimd.memset(late[:, :], 0.0).then_inc(consts_zeroed, 1)
                nc.gpsimd.memset(eye[:, :], 0.0).then_inc(consts_zeroed, 1)
                pool.wait_ge(consts_zeroed, 2)
                nc.gpsimd.affine_select(out=late[:, :], in_=late[:, :], compare_op=ALU.is_ge,
                                        fill=MASKED, base=0, pattern=[[1, P]],
                                        channel_multiplier=-1).then_inc(consts_ready, 1)
                nc.gpsimd.affine_select(out=eye[:, :], in_=eye[:, :], compare_op=ALU.not_equal,
                                        fill=1.0, base=0, pattern=[[-1, P]],
                                        channel_multiplier=1).then_inc(consts_ready, 1)

                def lo(i, c):
                    n = c % NB
                    if n not in LO_POOL:
                        return
                    first, w = span(n)
                    wait_hi(pool, i, c)
                    nc.gpsimd.tensor_tensor(prob_lo[:, c % NP, 0:w], prob[:, c % NP, 0:w],
                                            prob_hi[:, c % NP, 0:w].bitcast(F32),
                                            ALU.subtract).then_inc(lo_pool, 1)

                pipeline(pool, STEPS, U, [(0, lo)])

            @block.scalar
            def _(act):
                def row(i, c):
                    if c % NB != 0:
                        return
                    g = HS * i + c // NB
                    wait(act, row_turned, g + 1)
                    wait(act, row_saved[c // NB], 16 * i)
                    nc.scalar.activation(row_stage[:, c // NB, :], ps_row[0:QT, :], ACT.Copy,
                                         scale=-1.0).then_inc(row_ready, 1)
                    wait(act, row_ready, g + 1)
                    act.dma_start(row_dram[bass.ds(g, 1), :].rearrange("a (t q) -> (a t) q", t=QT),
                                  row_stage[:, c // NB, :].bitcast(F32)
                                  ).then_inc(row_saved[c // NB], 16)

                def load_row(i, c):
                    if c % NB != 0:
                        return
                    g = HS * i + c // NB
                    wait(act, row_saved[c // NB], 16 * (i + 1))
                    act.dma_start(qs[ROWS:ROWS + 1, c // NB, :].bitcast(F32),
                                  row_dram[bass.ds(g, 1), :]).then_inc(row_loaded[c // NB], 16)

                def exp(i, c):
                    step = U * i + c
                    first, w = span(c % NB)
                    wait(act, s_done, step + 1)
                    wait(act, lo_dve, count(LO_DVE, i, c - NP))
                    wait(act, lo_pool, count(LO_POOL, i, c - NP))
                    nc.scalar.activation(prob[:, c % NP, 0:w], ps_s[c % NS][:, 0:w], ACT.Exp,
                                         scale=SCALE).then_inc(exp_done, 1)

                def hi(i, c):
                    step = U * i + c
                    if c % NB in HI_DVE:
                        return
                    first, w = span(c % NB)
                    wait(act, exp_done, step + 1)
                    wait(act, pv_done, step - NP + 1)
                    nc.scalar.activation(prob_hi[:, c % NP, 0:w], prob[:, c % NP, 0:w],
                                         ACT.Copy).then_inc(hi_act, 1)

                def copy_o(i, c):
                    n = c % NB
                    if n not in ENDS:
                        return
                    half = BLOCKS[n][0]
                    o = 2 * (HS * i + c // NB) + half
                    wait(act, pv_done, U * i + c + 1)
                    wait(act, o_turned, o - 1)
                    nc.scalar.activation(o_copy[:, half, :], ps_o[half][0:VW, :],
                                         ACT.Copy).then_inc(o_copied, 1)

                pipeline(act, STEPS, U, [
                    (EXP, exp), (ROW + 1, row), (COPY, copy_o), (HI, hi), (ROW + 4, load_row)])

            @block.vector
            def _(dve):
                def maximum(i, c):
                    g = HS * i + c // NB
                    slot = c // NB
                    t, k0, w = PIECES[c % NB]
                    step = U * i + c
                    wait(dve, m_done, step + 1)
                    if c % NB == 0:
                        wait(dve, row_turned, HS * (i - 1) + slot + 1)
                    scores = ps_m[c % NM][:, 0:w]
                    at = t if k0 + w == P * (t + 1) else QT + t - 4
                    nc.vector.reduce_max(maxima[:, slot, at:at + 1], scores, AX.X).then_inc(m_read, 1)
                    if c % NB == NB - 1:
                        wait(dve, m_read, step + 1)
                        nc.vector.tensor_tensor(maxima[:, slot, 4:QT], maxima[:, slot, 4:QT],
                                                maxima[:, slot, QT:QT + 4],
                                                ALU.max).then_inc(max_ready, 1)

                def lo(i, c):
                    n = c % NB
                    if n in LO_POOL:
                        return
                    first, w = span(n)
                    wait_hi(dve, i, c)
                    nc.vector.tensor_tensor(prob_lo[:, c % NP, 0:w], prob[:, c % NP, 0:w],
                                            prob_hi[:, c % NP, 0:w].bitcast(F32),
                                            ALU.subtract).then_inc(lo_dve, 1)

                def hi(i, c):
                    step = U * i + c
                    if c % NB not in HI_DVE:
                        return
                    first, w = span(c % NB)
                    wait(dve, exp_done, step + 1)
                    wait(dve, pv_done, step - NP + 1)
                    nc.vector.tensor_copy(prob_hi[:, c % NP, 0:w], prob[:, c % NP, 0:w]
                                          ).then_inc(hi_dve, 1)

                def normalize(i, c):
                    n = c % NB
                    if n not in ENDS:
                        return
                    half = BLOCKS[n][0]
                    h, b = 2 * i + c // NB // 2, c // NB % 2
                    o = 2 * (HS * i + c // NB) + half
                    wait(dve, o_turned, o + 1)
                    wait(dve, o_ready, o)
                    if isinstance(o, int) and o == 0:
                        dve.wait_ge(out_stored, 16 * NT)
                    nc.vector.reciprocal(o_inv[:, :, :], ps_ot[:, :, 2 * DK:2 * DK + 1]
                                         ).then_inc(inv_ready, 1)
                    nc.vector.tensor_copy(o_part[:, :, :], ps_ot[:, :, DK:2 * DK]
                                          ).then_inc(part_ready, 1)
                    wait(dve, part_ready, o + 1)
                    nc.vector.tensor_tensor(o_sum[:, :, :], ps_ot[:, :, 0:DK], o_part[:, :, :],
                                            ALU.add).then_inc(sum_ready, 1)
                    wait(dve, inv_ready, o + 1)
                    wait(dve, sum_ready, o + 1)
                    tiles = slice(b * QT + 4 * half, b * QT + 4 * half + 4)
                    nc.vector.tensor_tensor(attended[:, tiles, bass.ds(h * DK, DK)], o_sum[:, :, :],
                                            o_inv[:, :, :].broadcast_to([P, 4, DK]),
                                            ALU.mult).then_inc(o_ready, 1)

                nc.vector.memset(ks[ROWS:ROWS + 1, :, :].bitcast(F32), 1.0).then_inc(consts_ready, 1)
                nc.vector.memset(vs[:, :, :, 2 * DK:].bitcast(F32), 1.0).then_inc(consts_ready, 1)
                pipeline(dve, STEPS, U, [(NORM, normalize), (0, maximum), (HI, hi), (LO, lo)])

            @block.tensor
            def _(pe):
                pe.wait_ge(consts_ready, 4)

                def maximum(i, c):
                    slot = c // NB
                    t, k0, w = PIECES[c % NB]
                    if c % NB == 0:
                        wait(pe, head_loaded[slot], 96 * (i + 1))
                    wait(pe, m_read, U * i + c - NM + 1)
                    diagonal = k0 + w == P * (t + 1)
                    last = nc.tensor.matmul(ps_m[c % NM][:, 0:w], qs[0:ROWS, slot, t * P:(t + 1) * P],
                                            ks[0:ROWS, slot, k0:k0 + w], start=True,
                                            stop=not diagonal)
                    if diagonal:
                        last = nc.tensor.matmul(ps_m[c % NM][:, w - P:w], late[:, :], eye[:, :],
                                                start=False, stop=True)
                    last.then_inc(m_done, 1)

                def turn_row(i, c):
                    if c % NB != 0:
                        return
                    slot = c // NB
                    g = HS * i + slot
                    wait(pe, max_ready, g + 1)
                    wait(pe, row_ready, g)
                    wait(pe, o_ready, 2 * g + TURNS_BEFORE)
                    nc.tensor.transpose(ps_row[0:QT, :], maxima[:, slot, 0:QT],
                                        ident[:, :]).then_inc(row_turned, 1)

                def score(i, c):
                    slot = c // NB
                    qb, kt = BLOCKS[c % NB]
                    first, w = span(c % NB)
                    if c % NB == 0:
                        wait(pe, row_loaded[slot], 16 * (i + 1))
                    wait(pe, exp_done, U * i + c - NS + 1)
                    q0 = qb * TBW + first
                    diagonal = c % NB in DIAGONAL
                    last = nc.tensor.matmul(ps_s[c % NS][:, 0:w],
                                            ks[0:ROWS + 1, slot, kt * P:(kt + 1) * P],
                                            qs[0:ROWS + 1, slot, q0:q0 + w], start=True,
                                            stop=not diagonal)
                    if diagonal:
                        last = nc.tensor.matmul(ps_s[c % NS][:, 0:P], eye[:, :], late[:, :],
                                                start=False, stop=True)
                    last.then_inc(s_done, 1)

                def value(i, c):
                    slot = c // NB
                    n = c % NB
                    qb, kt = BLOCKS[n]
                    first, w = span(n)
                    if n == 0:
                        wait(pe, values_loaded[slot], 16 * (i + 1))
                    if n in STARTS:
                        wait(pe, o_copied, 2 * (HS * i + slot) + qb - 1)
                    if n in LO_POOL:
                        wait(pe, lo_pool, count(LO_POOL, i, c))
                    else:
                        wait(pe, lo_dve, count(LO_DVE, i, c))
                    into = ps_o[qb][0:VW, first:first + w]
                    nc.tensor.matmul(into, vs[:, slot, kt, :], prob_hi[:, c % NP, 0:w],
                                     start=n in STARTS, stop=False)
                    nc.tensor.matmul(into, vs[:, slot, kt, :], prob_lo[:, c % NP, 0:w], start=False,
                                     stop=n in ENDS).then_inc(pv_done, 1)

                def turn_o(i, c):
                    n = c % NB
                    if n not in ENDS:
                        return
                    half = BLOCKS[n][0]
                    o = 2 * (HS * i + c // NB) + half
                    wait(pe, o_copied, o + 1)
                    wait(pe, o_ready, o)
                    rows = HS * i + c // NB + ROWS_BEFORE[n]
                    wait(pe, row_ready, min(rows, B * H) if isinstance(rows, int) else rows)
                    for q in range(4):
                        last = nc.tensor.transpose(ps_ot[:, q, 0:VW], o_copy[:, half, q * P:(q + 1) * P],
                                                   ident[0:VW, 0:VW])
                    last.then_inc(o_turned, 1)

                pipeline(pe, STEPS, U, [
                    (0, maximum), (TURN, turn_o), (VALUE, value), (AHEAD, score), (ROW, turn_row)])


def out_phase(nc, wo, down, ident, attended, d_sb, out, y_tile, y_stored, slot_table, rows,
              rows_ready, xn_dram, gathered, down_loaded):
    with ExitStack() as ctx:
        sbuf, psum, sem = allocator(nc, ctx)
        U = YS
        R = 2
        wo_raw = d_sb[:, E * len(FCH) - KC:, :]
        wo_hi = sbuf("wo_hi", [P, KC, D], F32R)
        wo_lo = sbuf("wo_lo", [P, KC, D], F32R)
        a_tile = sbuf("a_tile", [P, R, D])
        a_hi = sbuf("a_hi", [P, R, KC, P], F32R)
        a_lo = sbuf("a_lo", [P, R, KC, P], F32R)
        ps_t = [psum(f"ps_at{n}", [P, KC, P]) for n in range(R)]
        ps_y = [psum(f"ps_ay{n}", [P, D]) for n in range(R)]
        x_loaded = [sem(f"xr_loaded{n}") for n in range(U)]
        wo_loaded = [sem(f"wo_loaded{k}") for k in range(KC)]
        wo_hi_ready = sem("wo_hi_ready")
        wo_lo_ready = sem("wo_lo_ready")
        tile_ready = sem("a_tile_ready")
        turned = sem("a_turned")
        hi_ready = sem("a_hi_ready")
        lo_ready = sem("a_lo_ready")
        y_done = sem("a_y_done")
        added = sem("a_added")
        passed = sem("a_passed")

        with nc.Block() as block:
            @block.sync
            def _(sp):
                for k in range(KC):
                    sp.dma_start(wo_raw[:, k, :], wo[:, k, :]).then_inc(wo_loaded[k], 16)
                TAIL = FCH[-1][1]

                def load(i, c):
                    t = U * i + c
                    wait(sp, y_stored[c], 16 * i)
                    sp.dma_start(y_tile[:, c, :], out[bass.ds(t * P, P), :]).then_inc(x_loaded[c], 16)

                def store(i, c):
                    t = U * i + c
                    wait(sp, added, t + 1)
                    sp.dma_start(out[bass.ds(t * P, P), :], y_tile[:, c, :]).then_inc(y_stored[c], 16)
                def load_down(i, c):
                    x = U // 2 * i + c // 2
                    if not isinstance(i, int):
                        sp.wait_ge(wo_lo_ready, KC)
                    e = bass.ds(x, 1)
                    if c % 2 == 0:
                        sp.dma_start(d_sb[:, bass.ds(len(FCH) * x, 2), :],
                                     down[e, 0:2 * P, :].rearrange("a (k p) d -> p (a k) d", p=P)
                                     ).then_inc(down_loaded, 16)
                    else:
                        sp.dma_start(d_sb[0:TAIL, bass.ds(len(FCH) * x + 2, 1), :],
                                     down[e, 2 * P:F, :].rearrange("a p d -> p a d")
                                     ).then_inc(down_loaded, 16)
                assert 2 * E == NT

                pipeline(sp, NT, U, [(0, load), (0, load_down), (2, store)])

            @block.gpsimd
            def _(pool):
                pool.wait_ge(rows_ready, GS)
                for j in range(GS):
                    pool.wait_ge(tile_ready, j + 1)
                    pool.sem_inc(passed, 1)
                    nc.gpsimd.indirect_dma_start(
                        attended[:, j, :], None, xn_dram,
                        bass.IndirectOffsetOnAxis(rows[:, j:j + 1], 0)).then_inc(gathered[j], 16)

            @block.scalar
            def _(act):
                def hi(i, c):
                    t = U * i + c
                    wait(act, turned, t + 1)
                    wait(act, y_done, t - R + 1)
                    nc.scalar.activation(a_hi[:, c % R], ps_t[c % R][:, :, :], ACT.Copy).then_inc(hi_ready, 1)

                def split_wo(i, c):
                    if isinstance(i, int) and i == 0 and c == 0:
                        for k in range(KC):
                            act.wait_ge(wo_loaded[k], 16)
                            nc.scalar.activation(wo_hi[:, k, :], wo_raw[:, k, :],
                                                 ACT.Copy).then_inc(wo_hi_ready, 1)
                pipeline(act, NT, U, [(0, hi), (0, split_wo)])

            @block.vector
            def _(dve):
                for j in range(GS):
                    nc.vector.tensor_copy(rows[:, j:j + 1], slot_table[:, j:j + 1, 0].bitcast(I32)
                                          ).then_inc(rows_ready, 1)

                def copy(i, c):
                    t = U * i + c
                    wait(dve, turned, t - R + 1)
                    nc.vector.tensor_copy(a_tile[:, c % R, :], attended[:, bass.ds(t, 1), :]
                                          .rearrange("p a d -> p (a d)")).then_inc(tile_ready, 1)

                def lo(i, c):
                    t = U * i + c
                    wait(dve, hi_ready, t + 1)
                    nc.vector.tensor_tensor(a_lo[:, c % R], ps_t[c % R][:, :, :],
                                            a_hi[:, c % R].bitcast(F32),
                                            ALU.subtract).then_inc(lo_ready, 1)

                def add(i, c):
                    t = U * i + c
                    wait(dve, y_done, t + 1)
                    wait(dve, x_loaded[c], 16 * (i + 1))
                    nc.vector.tensor_tensor(y_tile[:, c, :], ps_y[c % R][:, :], y_tile[:, c, :],
                                            ALU.add).then_inc(added, 1)

                def split_wo(i, c):
                    if isinstance(i, int) and i == 0 and c == 0:
                        for k in range(KC):
                            dve.wait_ge(wo_hi_ready, k + 1)
                            nc.vector.tensor_tensor(wo_lo[:, k, :], wo_raw[:, k, :],
                                                    wo_hi[:, k, :].bitcast(F32),
                                                    ALU.subtract).then_inc(wo_lo_ready, 1)
                pipeline(dve, NT, U, [(0, copy), (1, lo), (1, split_wo), (2, add)])

            @block.tensor
            def _(pe):
                def turn(i, c):
                    t = U * i + c
                    wait(pe, tile_ready, t + 1)
                    wait(pe, lo_ready, t - R + 1)
                    for k in range(KC):
                        last = nc.tensor.transpose(ps_t[c % R][:, k, :], a_tile[:, c % R, k * P:(k + 1) * P],
                                                   ident[:, :])
                    last.then_inc(turned, 1)

                def multiply(i, c):
                    t = U * i + c
                    wait(pe, lo_ready, t + 1)
                    wait(pe, added, t - R + 1)
                    n = 0
                    for k in range(KC):
                        if isinstance(i, int) and i == 0 and c == 0:
                            pe.wait_ge(wo_lo_ready, k + 1)
                        for a, b in ((a_hi, wo_hi), (a_hi, wo_lo), (a_lo, wo_hi)):
                            last = nc.tensor.matmul(ps_y[c % R][:, :], a[:, c % R, k, :], b[:, k, :],
                                                    start=(n == 0), stop=(n == 3 * KC - 1))
                            n += 1
                    last.then_inc(y_done, 1)
                pipeline(pe, NT, U, [(0, turn), (1, multiply)])


def shared_phase(nc, x, gate, up, down, shared_w, xt_hi, xt_lo, chosen, weight, earlier_of,
                 count_of, slot_of, entry, slot_table, expert_of, slots_dram, out, acc, qk_stored,
                 out_stored):
    with ExitStack() as ctx:
        sbuf, psum, sem = allocator(nc, ctx)
        U = 2
        NF = len(FCH)
        (_, g_hi, g_lo), (_, u_hi, u_lo), (_, d_hi, d_lo) = shared_w
        silu = sbuf("silu", [P, 2, TBW])
        hid = sbuf("hid", [P, 1, TBW])
        hid_hi = sbuf("hid_hi", [P, NF, TBW], F32R)
        hid_lo = sbuf("hid_lo", [P, NF, TBW], F32R)
        tile_int = sbuf("tile_int", [P, NST], I32)
        tile_no = sbuf("tile_no", [P, NST, 1])
        pads = sbuf("pads", [P, 1], I32)
        tokens = sbuf("tokens", [P, NT], I32)
        first_slot = sbuf("first_slot", [P, NT])
        over = sbuf("over", [P, E, NT])
        first_tile = sbuf("first_tile", [P, 1, E])
        started = sbuf("started", [P, NST, E])
        slot = sbuf("slot", [P, NT, E])
        pick = sbuf("pick", [P, NT, E])
        before = sbuf("before", [P, NT, E])
        slot_ab = sbuf("slot_ab", [P, NT, 2])
        ps_g = [psum(f"ps_g{n}", [P, TBW]) for n in range(2)]
        ps_u = [psum(f"ps_u{n}", [P, TBW]) for n in range(2)]
        ps_y = [psum(f"ps_y{n}", [P, D]) for n in range(4)]
        placing = sem("placing")
        table_padded = sem("table_padded")
        loaded = sem("ffn_loaded")
        w_hi_ready = sem("ffn_w_hi")
        w_lo_ready = sem("ffn_w_lo")
        g_done = sem("g_done")
        u_done = sem("u_done")
        silu_ready = sem("silu_ready")
        hid_ready = sem("hid_ready")
        hid_hi_ready = sem("hid_hi_ready")
        hid_lo_ready = sem("hid_lo_ready")
        y_done = sem("y_done")
        added = sem("added")
        x_loaded = sem("acc_loaded")
        pads_stored = sem("pads_stored")
        entries_stored = sem("entries_stored")
        table_loaded = sem("table_loaded")
        assert NSH == 2

        with nc.Block() as block:
            @block.sync
            def _(sp):
                load_shared_block(sp, 1, shared_w, gate, up, down, loaded)
                for stored in qk_stored:
                    sp.wait_ge(stored, 32 * (2 * D // P // len(qk_stored)))
                sp.dma_start(acc[:, :, :], x.rearrange("(t p) d -> p t d", p=P)).then_inc(x_loaded, 16)
                sp.wait_ge(table_padded, 1)
                sp.dma_start(slots_dram.rearrange("(j p) a -> p j a", p=P), slot_table[:, :, :]
                             ).then_inc(pads_stored, 16)
                for tb in range(NTB):
                    sp.wait_ge(added, (NSH - 1) * NT + 4 * (tb + 1))
                    for t in range(4 * tb, 4 * (tb + 1)):
                        sp.dma_start(out[t * P:(t + 1) * P, :], acc[:, t, :]).then_inc(out_stored, 16)

            @block.gpsimd
            def _(pool):
                steps = [0]

                def then(instruction):
                    steps[0] += 1
                    instruction.then_inc(placing, 1)
                    pool.wait_ge(placing, steps[0])

                def fold(of, n, into):
                    while n > 2:
                        n //= 2
                        then(nc.gpsimd.tensor_tensor(of[:, :, 0:n], of[:, :, 0:n], of[:, :, n:2 * n],
                                                     ALU.add))
                    then(nc.gpsimd.tensor_tensor(into, of[:, :, 0:1], of[:, :, 1:2], ALU.add))

                then(nc.gpsimd.iota(pads[:, :], pattern=[[0, 1]], base=T, channel_multiplier=1))
                then(nc.gpsimd.memset(slot_table[:, :, 1], 0.0))
                nc.gpsimd.tensor_copy(slot_table[:, :, 0].bitcast(I32),
                                      pads[:, :].broadcast_to([P, NST])).then_inc(table_padded, 1)
                then(nc.gpsimd.iota(tokens[:, :], pattern=[[P, NT]], base=0, channel_multiplier=1))
                then(nc.gpsimd.iota(tile_int[:, :], pattern=[[1, NST]], base=0,
                                    channel_multiplier=0))
                then(nc.gpsimd.tensor_copy(tile_no[:, :, 0], tile_int[:, :]))

                then(nc.gpsimd.tensor_scalar(first_slot[:, :], tile_no[:, 0:NT, 0], float(P), None,
                                             ALU.mult))
                then(nc.gpsimd.tensor_tensor(
                    over[:, :, :], count_of[:, :, :].rearrange("p a e -> p e a")
                    .broadcast_to([P, E, NT]),
                    first_slot[:, :].rearrange("p (a t) -> p a t", a=1).broadcast_to([P, E, NT]),
                    ALU.subtract))
                then(nc.gpsimd.tensor_scalar(over[:, :, :], over[:, :, :], 0.0, None, ALU.is_gt))
                fold(over, NT, over[:, :, 0:1])
                then(nc.gpsimd.memset(first_tile[:, :, 0:1], 0.0))
                for e in range(1, E):
                    then(nc.gpsimd.tensor_tensor(first_tile[:, :, e:e + 1],
                                                 first_tile[:, :, e - 1:e], over[:, e - 1:e, 0:1],
                                                 ALU.add))
                then(nc.gpsimd.tensor_tensor(started[:, :, :], tile_no[:, :, :]
                                             .broadcast_to([P, NST, E]),
                                             first_tile[:, :, :].broadcast_to([P, NST, E]),
                                             ALU.subtract))
                then(nc.gpsimd.tensor_scalar(started[:, :, :], started[:, :, :], 0.0, None,
                                             ALU.is_ge))
                fold(started, E, started[:, :, 0:1])
                then(nc.gpsimd.tensor_scalar(started[:, :, 0:1], started[:, :, 0:1], -1.0, None,
                                             ALU.add))
                then(nc.gpsimd.tensor_copy(expert_of[:, :], started[:, :, 0]))
                then(nc.gpsimd.tensor_scalar(first_tile[:, :, :], first_tile[:, :, :], float(P),
                                             None, ALU.mult))
                then(nc.gpsimd.tensor_tensor(slot[:, :, :], earlier_of[:, :, :],
                                             first_tile[:, :, :].broadcast_to([P, NT, E]), ALU.add))
                then(nc.gpsimd.memset(before[:, :, 0:1], 0.0))
                for e in range(1, E):
                    then(nc.gpsimd.tensor_tensor(before[:, :, e:e + 1], before[:, :, e - 1:e],
                                                 chosen[:, :, e - 1:e], ALU.add))
                then(nc.gpsimd.tensor_tensor(before[:, :, :], before[:, :, :], chosen[:, :, :],
                                             ALU.mult))
                for n in (1, 0):
                    for of, into in ((weight, entry[:, :, n, 1:2]), (slot, slot_ab[:, :, n:n + 1])):
                        then(nc.gpsimd.tensor_tensor(pick[:, :, :], of[:, :, :], before[:, :, :],
                                                     ALU.mult))
                        fold(pick, E, into)
                    if n:
                        then(nc.gpsimd.tensor_tensor(before[:, :, :], chosen[:, :, :],
                                                     before[:, :, :], ALU.subtract))
                    then(nc.gpsimd.tensor_copy(entry[:, :, n, 0].bitcast(I32), tokens[:, :]))
                then(nc.gpsimd.tensor_copy(slot_of[:, :, :], slot_ab[:, :, :]))

                pool.wait_ge(pads_stored, 16)
                n = 0
                for t in range(NT):
                    for k in range(2):
                        nc.gpsimd.indirect_dma_start(
                            slots_dram, bass.IndirectOffsetOnAxis(slot_of[:, t, k:k + 1], 0),
                            entry[:, t, k, :], None).then_inc(entries_stored, 16)
                        n += 16
                pool.wait_ge(entries_stored, n)
                pool.dma_start(slot_table[:, :, :], slots_dram.rearrange("(j p) a -> p j a", p=P)
                               ).then_inc(table_loaded, 16)
                pool.wait_ge(table_loaded, 16)

            @block.scalar
            def _(act):
                def split_next():
                    act.wait_ge(loaded, 64)
                    for raw, hi, lo in shared_parts(shared_w, 1):
                        nc.scalar.activation(hi, raw, ACT.Copy).then_inc(w_hi_ready, 1)

                def chunks(i, c, tb):
                    e = U * i + c
                    for k, (f0, w) in enumerate(FCH):
                        n = NF * (NTB * e + tb) + k
                        wait(act, g_done, n + 1)
                        wait(act, hid_ready, n - 1)
                        s = (NF * tb + k) % 2
                        nc.scalar.activation(silu[0:w, s, :], ps_g[s][0:w, :], ACT.Silu).then_inc(silu_ready, 1)
                        wait(act, hid_ready, n + 1)
                        wait(act, y_done, 4 * (NTB * e + tb))
                        nc.scalar.activation(hid_hi[0:w, k, :], hid[0:w, 0, :], ACT.Copy).then_inc(hid_hi_ready, 1)

                def block_e(i, c):
                    for tb in range(NTB):
                        chunks(i, c, tb)
                        if c == 0 and tb == 0:
                            split_next()
                pipeline(act, NSH, U, [(0, block_e)])

            @block.vector
            def _(dve):
                def split_next():
                    for n, (raw, hi, lo) in enumerate(shared_parts(shared_w, 1)):
                        dve.wait_ge(w_hi_ready, n + 1)
                        nc.vector.tensor_tensor(lo, raw, hi.bitcast(F32), ALU.subtract).then_inc(w_lo_ready, 1)

                def add(e, i, c, tb):
                    for q in range(4):
                        t = 4 * tb + q
                        wait(dve, y_done, NT * e + t + 1)
                        wait(dve, added, NT * (e - 1) + t + 1)
                        nc.vector.tensor_tensor(acc[:, t, :], ps_y[q][:, :], acc[:, t, :],
                                                ALU.add).then_inc(added, 1)

                def block_e(i, c):
                    e = U * i + c
                    for tb in range(NTB):
                        for k, (f0, w) in enumerate(FCH):
                            n = NF * (NTB * e + tb) + k
                            s = (NF * tb + k) % 2
                            wait(dve, silu_ready, n + 1)
                            wait(dve, u_done, n + 1)
                            wait(dve, hid_lo_ready, n)
                            nc.vector.tensor_tensor(hid[0:w, 0, :], ps_u[s][0:w, :], silu[0:w, s, :],
                                                    ALU.mult).then_inc(hid_ready, 1)
                            wait(dve, hid_hi_ready, n + 1)
                            nc.vector.tensor_tensor(hid_lo[0:w, k, :], hid[0:w, 0, :],
                                                    hid_hi[0:w, k, :].bitcast(F32),
                                                    ALU.subtract).then_inc(hid_lo_ready, 1)
                        if c == 0 and tb == 0:
                            dve.wait_ge(x_loaded, 16)
                        add(e, i, c, tb)
                        if c == 0 and tb == 0:
                            split_next()
                pipeline(dve, NSH, U, [(0, block_e)])

            @block.tensor
            def _(pe):
                def block_e(i, c):
                    e = U * i + c
                    wait(pe, w_lo_ready, 4 * e)
                    for tb in range(NTB):
                        toks = slice(tb * TBW, (tb + 1) * TBW)
                        for k, (f0, w) in enumerate(FCH):
                            n = NF * (NTB * e + tb) + k
                            s = (NF * tb + k) % 2
                            for ps, hi, lo, done, read in ((ps_g, g_hi, g_lo, g_done, silu_ready),
                                                           (ps_u, u_hi, u_lo, u_done, hid_ready)):
                                wait(pe, read, n - 1)
                                j = 0
                                for kc in range(KC):
                                    for a, b in ((hi, xt_hi), (lo, xt_hi), (hi, xt_lo)):
                                        last = nc.tensor.matmul(ps[s][0:w, :], a[:, c, kc, f0:f0 + w],
                                                                b[:, kc, toks], start=(j == 0),
                                                                stop=(j == 3 * KC - 1))
                                        j += 1
                                last.then_inc(done, 1)
                        for chunks in (range(NF - 1), (NF - 1,)):
                            wait(pe, hid_lo_ready, NF * (NTB * e + tb) + chunks[-1] + 1)
                            for q in range(4):
                                wait(pe, added, NT * e + 4 * tb + q - 3)
                                for k in chunks:
                                    w = FCH[k][1]
                                    for a, b in ((hid_hi, d_hi), (hid_hi, d_lo), (hid_lo, d_hi)):
                                        last = nc.tensor.matmul(
                                            ps_y[q][:, :], a[0:w, k, q * P:(q + 1) * P],
                                            b[0:w, c, k, :], start=(k == 0 and a is hid_hi and b is d_hi),
                                            stop=(k == NF - 1 and a is hid_lo))
                                if k == NF - 1:
                                    last.then_inc(y_done, 1)
                pipeline(pe, NSH, U, [(0, block_e)])


def routed_phase(nc, ident, gu_sb, d_sb, slot_table, expert_of, xn_dram, work, out, y_stored,
                 rows, rows_ready, gathered, down_loaded):
    with ExitStack() as ctx:
        sbuf, psum, sem = allocator(nc, ctx)
        U = ROW_SLOTS
        R = GS
        NF = len(FCH)
        xg = work[:, 0:R, :]
        y = work[:, R:2 * R, :]
        X = 2
        xg_hi = sbuf("xg_hi", [P, X, KC, P], F32R)
        xg_lo = sbuf("xg_lo", [P, X, KC, P], F32R)
        HR = 2
        units = work[:, 3 * R:4 * R, :].rearrange("p a d -> p (a d)")
        silu, hid = [units[:, n * HR * F:(n + 1) * HR * F].rearrange("p (u f) -> p u f", u=HR)
                     for n in range(2)]
        hid_t = work[:, 2 * R:2 * R + HR, 0:NF * P].rearrange("p u (k t) -> p u k t", k=NF)
        w_hi = sbuf("rw_hi", [P, KC, 2 * F], F32R)
        w_lo = sbuf("rw_lo", [P, KC, 2 * F], F32R)
        ps_t = psum("ps_xt", [P, KC, P])
        ps_g = [psum(f"ps_rg{n}", [P, TBW]) for n in range(2)]
        ps_u = [psum(f"ps_ru{n}", [P, TBW]) for n in range(2)]
        ps_h = psum("ps_ht", [P, NF, P])
        ps_y = [psum(f"ps_ry{n}", [P, D]) for n in range(2)]
        x_turned = sem("x_turned")
        x_hi_ready = sem("x_hi_ready")
        x_lo_ready = sem("x_lo_ready")
        w_hi_ready = sem("rw_hi_ready")
        w_lo_ready = sem("rw_lo_ready")
        w_used = sem("rw_used")
        silu_ready = sem("rsilu_ready")
        hid_ready = sem("rhid_ready")
        h_turned = sem("h_turned")
        h_ready = sem("h_ready")
        y_done = sem("ry_done")
        y_ready = sem("y_ready")
        scattered = sem("scattered")
        passed = sem("r_passed")

        def expert(eng, j):
            return eng.value_load(expert_of[0:1, bass.ds(j, 1)], min_val=0, max_val=E - 1)

        def chunk(e, k):
            return gu_sb[:, bass.ds(e * KC + k, 1), :].rearrange("p a f -> p (a f)")

        with nc.Block() as block:
            @block.gpsimd
            def _(pool):
                def gather(i, c):
                    j = U * i + c
                    if isinstance(j, int) and j < GS:
                        return
                    wait(pool, x_turned, j - R + 1)
                    wait(pool, rows_ready, j + 1)
                    pool.sem_inc(passed, 1)
                    nc.gpsimd.indirect_dma_start(
                        xg[:, c % R, :], None, xn_dram,
                        bass.IndirectOffsetOnAxis(rows[:, c:c + 1], 0)).then_inc(gathered[c % R], 16)

                def scatter(i, c):
                    j = U * i + c
                    if isinstance(j, int) and j == 0:
                        for n in range(YS):
                            pool.wait_ge(y_stored[n], 16 * (NT // YS))
                    wait(pool, scattered, 16 * j)
                    wait(pool, y_ready, j + 1)
                    pool.sem_inc(passed, 1)
                    nc.gpsimd.indirect_dma_start(
                        out, bass.IndirectOffsetOnAxis(rows[:, c:c + 1], 0), y[:, c % R, :], None,
                        compute_op=ALU.add).then_inc(scattered, 16)
                pipeline(pool, NST, U, [(0, gather), (3, scatter)])
                pool.wait_ge(scattered, 16 * NST)

            @block.scalar
            def _(act):
                def turn_x(i, c):
                    j = U * i + c
                    wait(act, x_turned, j + 1)
                    wait(act, w_used, KC * (j - X + 1))
                    nc.scalar.activation(xg_hi[:, c % X], ps_t[:, :, :], ACT.Copy
                                         ).then_inc(x_hi_ready, 1)

                def weights_hi(i, c, ks):
                    j = U * i + c
                    e = expert(act, j)
                    for k in ks:
                        wait(act, w_used, KC * j + k - KC + 1)
                        nc.scalar.activation(w_hi[:, k, :], chunk(e, k), ACT.Copy
                                             ).then_inc(w_hi_ready, 1)

                def first_chunks(i, c):
                    weights_hi(i, c, range(KC - 1))

                def last_chunk(i, c):
                    weights_hi(i, c, [KC - 1])

                def gate_unit(i, c):
                    j = U * i + c
                    wait(act, w_used, KC * (j + 1))
                    wait(act, hid_ready, j - HR + 1)
                    nc.scalar.activation(silu[:, c % HR, :], ps_g[c % 2][:, 0:F], ACT.Silu
                                         ).then_inc(silu_ready, 1)
                pipeline(act, NST, U, [(0, turn_x), (0, first_chunks), (1, gate_unit), (0, last_chunk)],
                         back=R)

            @block.vector
            def _(dve):
                def row_numbers(i, c):
                    j = U * i + c
                    if isinstance(j, int) and j < GS:
                        return
                    wait(dve, scattered, 16 * (j - U + 1))
                    nc.vector.tensor_copy(rows[:, c:c + 1],
                                          slot_table[:, bass.ds(j, 1), 0].bitcast(I32)
                                          ).then_inc(rows_ready, 1)

                def hidden(i, c):
                    j = U * i + c
                    wait(dve, silu_ready, j + 1)
                    wait(dve, h_turned, j - HR + 1)
                    nc.vector.tensor_tensor(hid[:, c % HR, :], ps_u[c % 2][:, 0:F], silu[:, c % HR, :],
                                            ALU.mult).then_inc(hid_ready, 1)

                def turn_h(i, c):
                    j = U * i + c
                    wait(dve, h_turned, j + 1)
                    wait(dve, y_done, j - HR + 1)
                    nc.vector.tensor_copy(hid_t[:, c % HR, 0:2, :], ps_h[:, 0:2, :]).then_inc(h_ready, 1)
                    w = FCH[-1][1]
                    nc.vector.tensor_copy(hid_t[0:w, c % HR, 2, :], ps_h[0:w, 2, :]).then_inc(h_ready, 1)

                def weigh(i, c):
                    j = U * i + c
                    wait(dve, y_done, j + 1)
                    wait(dve, scattered, 16 * (j - R + 1))
                    nc.vector.tensor_scalar(y[:, c % R, :], ps_y[c % 2][:, :],
                                            slot_table[:, bass.ds(j, 1), 1], None,
                                            ALU.mult).then_inc(y_ready, 1)

                def x_lo(i, c):
                    j = U * i + c
                    wait(dve, x_hi_ready, j + 1)
                    nc.vector.tensor_tensor(xg_lo[:, c % X], ps_t[:, :, :], xg_hi[:, c % X].bitcast(F32),
                                            ALU.subtract).then_inc(x_lo_ready, 1)

                def weights_lo(i, c, ks):
                    j = U * i + c
                    e = expert(dve, j)
                    for k in ks:
                        wait(dve, w_hi_ready, KC * j + k + 1)
                        nc.vector.tensor_tensor(w_lo[:, k, :], chunk(e, k),
                                                w_hi[:, k, :].bitcast(F32),
                                                ALU.subtract).then_inc(w_lo_ready, 1)

                def first_chunks(i, c):
                    weights_lo(i, c, range(KC - 1))

                def last_chunk(i, c):
                    weights_lo(i, c, [KC - 1])

                pipeline(dve, NST, U, [(0, row_numbers), (4, turn_h), (2, x_lo), (2, first_chunks),
                                       (3, hidden), (2, last_chunk), (4, weigh)], back=U)

            @block.tensor
            def _(pe):
                def turn_x(i, c):
                    j = U * i + c
                    wait(pe, gathered[c % R], 16 * (U // R * i + c // R + 1))
                    wait(pe, x_lo_ready, j)
                    for k in range(KC):
                        last = nc.tensor.transpose(ps_t[:, k, :], xg[:, c % R, k * P:(k + 1) * P],
                                                   ident[:, :])
                    last.then_inc(x_turned, 1)

                def gate_up(i, c):
                    j = U * i + c
                    wait(pe, x_lo_ready, j + 1)
                    wait(pe, hid_ready, j - 1)
                    for k in range(KC):
                        wait(pe, w_lo_ready, KC * j + k + 1)
                        for n, ps in enumerate((ps_g, ps_u)):
                            for a, b in ((xg_hi, w_hi), (xg_hi, w_lo), (xg_lo, w_hi)):
                                last = nc.tensor.matmul(
                                    ps[c % 2][:, 0:F], a[:, c % X, k, :], b[:, k, n * F:(n + 1) * F],
                                    start=(k == 0 and a is xg_hi and b is w_hi),
                                    stop=(k == KC - 1 and a is xg_lo))
                        last.then_inc(w_used, 1)

                def turn_h(i, c):
                    j = U * i + c
                    wait(pe, hid_ready, j + 1)
                    wait(pe, h_ready, 2 * j)
                    for k, (f0, w) in enumerate(FCH):
                        last = nc.tensor.transpose(ps_h[0:w, k, :], hid[:, c % HR, f0:f0 + w], ident[:, :])
                    last.then_inc(h_turned, 1)

                def down(i, c):
                    j = U * i + c
                    e = expert(pe, j)
                    if isinstance(j, int) and j == 0:
                        pe.wait_ge(down_loaded, 32 * E)
                    wait(pe, h_ready, 2 * (j + 1))
                    wait(pe, y_ready, j - 1)
                    for k, (f0, w) in enumerate(FCH):
                        last = nc.tensor.matmul(
                            ps_y[c % 2][:, :], hid_t[0:w, c % HR, k, :],
                            d_sb[0:w, bass.ds(e * NF + k, 1), :].rearrange("p a d -> p (a d)"),
                            start=(k == 0), stop=(k == NF - 1))
                    last.then_inc(y_done, 1)
                pipeline(pe, NST, U, [(2, turn_h), (0, turn_x), (1, gate_up), (2, down)], back=R)


def kernel(L0_attn_x, L0_attn_Wq, L0_attn_Wk, L0_attn_Wv, L0_attn_Wo, L0_ffn_router_weight,
           L0_ffn_e_score_correction_bias, L0_ffn_gate_w, L0_ffn_up_w, L0_ffn_down_w,
           L0_ffn_shared_gate_w, L0_ffn_shared_up_w, L0_ffn_shared_down_w):
    import numpy as np
    import concourse.bacc as bacc
    from concourse.bass_utils import run_bass_kernel_spmd

    def by_partition(w):
        return w.reshape(KC, P, -1).transpose(1, 0, 2)

    def columns(w):
        return w.reshape(KC, P, D // P, P).transpose(2, 1, 0, 3)

    def blocks_in(w):
        return w.reshape(-1, F, KC, P).transpose(0, 3, 2, 1)

    def pieces_in(w):
        return w.reshape(E, F, KC, P).transpose(0, 2, 3, 1).reshape(E * KC, P, F)

    a = {k: np.asarray(v) for k, v in dict(
        x=L0_attn_x, wq=L0_attn_Wq, wk=L0_attn_Wk, wv=L0_attn_Wv, wo=L0_attn_Wo,
        r=L0_ffn_router_weight, b=L0_ffn_e_score_correction_bias, g=L0_ffn_gate_w, u=L0_ffn_up_w,
        d=L0_ffn_down_w, sg=L0_ffn_shared_gate_w, su=L0_ffn_shared_up_w,
        sd=L0_ffn_shared_down_w).items()}
    arrays = {
        "x": a["x"].reshape(T, D),
        "wqk": np.concatenate([columns(a["wq"].T), columns(a["wk"].T)]),
        "wv": by_partition(a["wv"].T),
        "wo": by_partition(a["wo"].T),
        "router": by_partition(a["r"].T),
        "bias": a["b"],
        "gate": pieces_in(a["g"]),
        "up": pieces_in(a["u"]),
        "down": a["d"].transpose(0, 2, 1),
        "sgate": blocks_in(a["sg"]),
        "sup": blocks_in(a["su"]),
        "sdown": a["sd"].T.reshape(NSH, F, D),
    }
    arrays = {k: np.ascontiguousarray(v) for k, v in arrays.items()}
    nc = bacc.Bacc("TRN2", target_bir_lowering=False, num_devices=1)
    ins = [nc.dram_tensor(f"in_{k}", v.shape, mybir.dt.from_np(v.dtype), kind="ExternalInput").ap()
           for k, v in arrays.items()]
    out = nc.dram_tensor("out", [T + P, D], F32, kind="ExternalOutput").ap()
    moe_attention_kernel(nc, *ins, out)
    r = run_bass_kernel_spmd(nc, [{f"in_{k}": v for k, v in arrays.items()}], core_ids=[0])
    return r.results[0]["out"][:T].reshape(B, S, D)
```
